# Optimizing a Trainium2 kernel written in Bass

```python
import numpy as np
import jax
import jax.numpy as jnp

def _softmax(x, axis=-1):
    return jax.nn.softmax(x, axis=axis)

def _gelu(x):
    return jax.nn.gelu(x, approximate=True)

def _silu(x):
    return jax.nn.silu(x)

def _sigmoid(x):
    return jax.nn.sigmoid(x)

def _layernorm(x, axis=-1, eps=1e-05):
    m = jnp.mean(x, axis=axis, keepdims=True)
    v = jnp.var(x, axis=axis, keepdims=True)
    return (x - m) / jnp.sqrt(v + eps)

def _scatter_add(tgt, idx, src, axis=0):
    return tgt.at[idx].add(src)

def _segment_sum(src, seg, n):
    return jax.ops.segment_sum(src, seg, n)
kernel_name = 'mk_cond_resid_d4_seqx_r8_dac330'

def setup_inputs(seed: int=0):
    np.random.seed(seed)
    _w = jnp.asarray

    def _rec_inputs():
        import jax
        import jax.numpy as jnp
        _rk = jax.random.key(seed)
        x = 7.22e-05 + 1 * jax.random.normal(jax.random.fold_in(_rk, 1), (2, 512, 128), jnp.float32)
        _lenS = 512 - jax.random.randint(jax.random.fold_in(_rk, 7), (2,), 0, max(1, 512 // 4) + 1, jnp.int32)
        _lenS2 = 512 - jax.random.randint(jax.random.fold_in(_rk, 8), (2,), 0, max(1, 512 // 4) + 1, jnp.int32)
        cond_64 = -0.104238 + 1.01173 * jax.random.normal(jax.random.fold_in(_rk, 11), (2, 64), jnp.float32)
        fside_16xSxS_0 = -5.72187e-05 + 0.999849 * jax.random.normal(jax.random.fold_in(_rk, 12), (16, 512, 512), jnp.float32)
        _validS = jnp.arange(512)[None, :] < _lenS[:, None]
        _validS2 = jnp.arange(512)[None, :] < _lenS2[:, None]
        _causal = jnp.tril(jnp.ones((512, 512), dtype=bool))
        mask_BxS_bk0 = jnp.logical_not(jnp.broadcast_to(_validS[:, :], (2, 512)))
        mask_BxS_bf1 = jnp.ones((2, 512), dtype=bool)
        return (x, cond_64, fside_16xSxS_0, mask_BxS_bk0, mask_BxS_bf1)
    x, cond_64, fside_16xSxS_0, mask_BxS_bk0, mask_BxS_bf1 = _rec_inputs()

    def _L0_cond_setup():
        import jax, jax.numpy as jnp
        import numpy as np
        B, S, H = (4, 256, 128)
        E = 8
        M = 64
        K = 2
        N_SHARED = 2
        SM = M * N_SHARED
        G = 64
        GE_TEMP = 1.0
        ALPHA = 0.001
        SEQ_AUX = True
        NORM_TOPK = True
        COS_TEMP = 0.78
        CONS_ALPHA = 0.01
        LEAKY_SLOPE = 0.01
        EPS_COS = 1e-08

        def _leaky(x):
            return jnp.where(x >= 0, x, LEAKY_SLOPE * x)

        def _moe_forward(hidden_states, g, wt, wg, w_gate, w_up, w_down, sw_gate, sw_up, sw_down):
            b, s, h = hidden_states.shape
            x = hidden_states.reshape(-1, h)
            T = x.shape[0]
            logits_h = x @ wt.T
            logits_g = g @ wg.T
            logits_g = jnp.repeat(logits_g, s, axis=0)
            logits = (logits_h + logits_g / GE_TEMP) / (1.0 + 1.0 / GE_TEMP)
            scores = jax.nn.softmax(logits, axis=-1)
            topk_w, topk_idx = jax.lax.top_k(scores, K)
            if K > 1 and NORM_TOPK:
                topk_w = topk_w / (topk_w.sum(-1, keepdims=True) + 1e-20)
            onehot = jax.nn.one_hot(topk_idx.reshape(b, s * K), E, dtype=jnp.float32)
            ce = onehot.sum(1) / (s * K / E)
            aux_loss = (ce * scores.reshape(b, s, E).mean(1)).sum(1).mean() * ALPHA
            gp = _leaky(jnp.einsum('th,ehm->etm', x, w_gate))
            up = jnp.einsum('th,ehm->etm', x, w_up)
            y_all = jnp.einsum('etm,emh->eth', gp * up, w_down)
            y_sel = y_all[topk_idx, jnp.arange(T)[:, None], :]
            y = (y_sel * topk_w[..., None]).sum(1).reshape(b, s, h)
            p = _leaky(hidden_states @ sw_gate) * (hidden_states @ sw_up) @ sw_down
            y = y + p
            num = jnp.sum(y * p, -1)
            den = jnp.maximum(jnp.linalg.norm(y, axis=-1), EPS_COS) * jnp.maximum(jnp.linalg.norm(p, axis=-1), EPS_COS)
            closs = CONS_ALPHA * jnp.mean(num / den / (1.0 + COS_TEMP))
            return (y, aux_loss + closs)
        key = jax.random.key(seed)
        ks = jax.random.split(key, 12)
        sh = 1.0 / np.sqrt(H)
        sm = 1.0 / np.sqrt(M)
        ssm = 1.0 / np.sqrt(SM)
        sg = 1.0 / np.sqrt(G)
        return {'hidden_states': jax.random.normal(ks[0], (B, S, H), jnp.float32), 'g': jax.random.normal(ks[1], (B, G), jnp.float32), 'wt': jax.random.uniform(ks[2], (E, H), jnp.float32, -sh, sh), 'wg': jax.random.uniform(ks[3], (E, G), jnp.float32, -sg, sg), 'w_gate': jax.random.uniform(ks[4], (E, H, M), jnp.float32, -sh, sh), 'w_up': jax.random.uniform(ks[5], (E, H, M), jnp.float32, -sh, sh), 'w_down': jax.random.uniform(ks[6], (E, M, H), jnp.float32, -sm, sm), 'sw_gate': jax.random.uniform(ks[7], (H, SM), jnp.float32, -sh, sh), 'sw_up': jax.random.uniform(ks[8], (H, SM), jnp.float32, -sh, sh), 'sw_down': jax.random.uniform(ks[9], (SM, H), jnp.float32, -ssm, ssm)}
    _L0_cond_all = _L0_cond_setup()
    _L0_cond_in = {k: v for k, v in _L0_cond_all.items() if k in ('wt', 'wg', 'w_gate', 'w_up', 'w_down', 'sw_gate', 'sw_up', 'sw_down')}
    del _L0_cond_all

    def _L1_cond_setup():
        import jax, jax.numpy as jnp
        import numpy as np
        B, N, DIM, H, DH = (2, 256, 128, 16, 64)
        INNER = H * DH
        EPS = 1e-05

        def layernorm(x, g):
            mean = jnp.mean(x, axis=-1, keepdims=True)
            var = jnp.var(x, axis=-1, keepdims=True)
            return (x - mean) * jax.lax.rsqrt(var + EPS) * g
        key = jax.random.key(seed)
        ks = jax.random.split(key, 10)
        x = jax.random.normal(ks[0], (B, N, DIM), dtype=jnp.float32)
        attn_bias = jax.random.normal(ks[1], (H, N, N), dtype=jnp.float32)
        mask = jax.random.randint(ks[2], (B, N), 0, 2).astype(bool)
        g_in = jnp.ones((DIM,), dtype=jnp.float32)
        null_attn_bias = jax.random.normal(ks[3], (H,), dtype=jnp.float32)
        null_kv = jax.random.normal(ks[4], (2, DH), dtype=jnp.float32)
        Wq = jax.random.normal(ks[5], (DIM, INNER), dtype=jnp.float32) * 0.02
        Wkv = jax.random.normal(ks[6], (DIM, 2 * DH), dtype=jnp.float32) * 0.02
        Wo = jax.random.normal(ks[7], (INNER, DIM), dtype=jnp.float32) * 0.02
        g_out = jnp.ones((DIM,), dtype=jnp.float32)
        return {'x': x, 'attn_bias': attn_bias, 'mask': mask, 'g_in': g_in, 'null_attn_bias': null_attn_bias, 'null_kv': null_kv, 'Wq': Wq, 'Wkv': Wkv, 'Wo': Wo, 'g_out': g_out}
    _L1_cond_all = _L1_cond_setup()
    _L1_cond_in = {k: v for k, v in _L1_cond_all.items() if k in ('g_in', 'null_attn_bias', 'Wq', 'Wkv', 'Wo', 'g_out')}
    del _L1_cond_all

    def _L2_cond_setup():
        import jax, jax.numpy as jnp
        import numpy as np
        DIM = 128
        HEADS = 16
        DIM_HEAD = 64
        SCALE = 8.0

        def ln(x, g, eps=1e-05):
            mean = x.mean(axis=-1, keepdims=True)
            var = ((x - mean) ** 2).mean(axis=-1, keepdims=True)
            return (x - mean) * jax.lax.rsqrt(var + eps) * g

        def l2norm(t):
            n = jnp.maximum(jnp.linalg.norm(t, axis=-1, keepdims=True), 1e-12)
            return t / n

        def rel_pos_bias(n, w0, b0, g0, w1, b1, g1, w2, b2, dtype):
            pos = jnp.arange(-n + 1, n, dtype=dtype)[:, None]
            h = jax.nn.silu(ln(pos @ w0 + b0, g0))
            h = jax.nn.silu(ln(h @ w1 + b1, g1))
            h = h @ w2 + b2
            i = jnp.arange(n)
            idx = i[:, None] - i[None, :] + n - 1
            bias = h[idx]
            return jnp.transpose(bias, (2, 0, 1))
        key = jax.random.key(seed)
        ks = jax.random.split(key, 16)
        b, n = (2, 256)
        inner = HEADS * DIM_HEAD
        s = 0.02
        return {'x': jax.random.normal(ks[0], (b, n, DIM), jnp.float32), 'mask': jnp.ones((b, n), dtype=bool), 'g_norm': jnp.ones((DIM,), jnp.float32), 'Wq': jax.random.normal(ks[1], (DIM, inner), jnp.float32) * s, 'Wkv': jax.random.normal(ks[2], (DIM, 2 * DIM_HEAD), jnp.float32) * s, 'q_scale': jnp.ones((DIM_HEAD,), jnp.float32), 'k_scale': jnp.ones((DIM_HEAD,), jnp.float32), 'null_kv': jax.random.normal(ks[3], (2, DIM_HEAD), jnp.float32), 'null_attn_bias': jax.random.normal(ks[4], (HEADS,), jnp.float32), 'w0': jax.random.normal(ks[5], (1, DIM), jnp.float32) * s, 'b0': jnp.zeros((DIM,), jnp.float32), 'g0': jnp.ones((DIM,), jnp.float32), 'w1': jax.random.normal(ks[6], (DIM, DIM), jnp.float32) * s, 'b1': jnp.zeros((DIM,), jnp.float32), 'g1': jnp.ones((DIM,), jnp.float32), 'w2': jax.random.normal(ks[7], (DIM, HEADS), jnp.float32) * s, 'b2': jnp.zeros((HEADS,), jnp.float32), 'Wout': jax.random.normal(ks[8], (inner, DIM), jnp.float32) * s, 'g_out': jnp.ones((DIM,), jnp.float32)}
    _L2_cond_all = _L2_cond_setup()
    _L2_cond_in = {k: v for k, v in _L2_cond_all.items() if k in ('g_norm', 'Wq', 'Wkv', 'q_scale', 'k_scale', 'null_attn_bias', 'w0', 'b0', 'g0', 'w1', 'b1', 'g1', 'w2', 'b2', 'Wout', 'g_out')}
    del _L2_cond_all

    def _L3_cond_setup():
        import jax, jax.numpy as jnp
        import numpy as np
        DIM = 128
        HEADS = 16
        DIM_HEAD = 64
        SCALE = 8.0

        def ln(x, g, eps=1e-05):
            mean = x.mean(axis=-1, keepdims=True)
            var = ((x - mean) ** 2).mean(axis=-1, keepdims=True)
            return (x - mean) * jax.lax.rsqrt(var + eps) * g

        def l2norm(t):
            n = jnp.maximum(jnp.linalg.norm(t, axis=-1, keepdims=True), 1e-12)
            return t / n

        def rel_pos_bias(n, w0, b0, g0, w1, b1, g1, w2, b2, dtype):
            pos = jnp.arange(-n + 1, n, dtype=dtype)[:, None]
            h = jax.nn.silu(ln(pos @ w0 + b0, g0))
            h = jax.nn.silu(ln(h @ w1 + b1, g1))
            h = h @ w2 + b2
            i = jnp.arange(n)
            idx = i[:, None] - i[None, :] + n - 1
            bias = h[idx]
            return jnp.transpose(bias, (2, 0, 1))
        key = jax.random.key(seed)
        ks = jax.random.split(key, 16)
        b, n = (2, 256)
        inner = HEADS * DIM_HEAD
        s = 0.02
        return {'x': jax.random.normal(ks[0], (b, n, DIM), jnp.float32), 'mask': jnp.ones((b, n), dtype=bool), 'g_norm': jnp.ones((DIM,), jnp.float32), 'Wq': jax.random.normal(ks[1], (DIM, inner), jnp.float32) * s, 'Wkv': jax.random.normal(ks[2], (DIM, 2 * DIM_HEAD), jnp.float32) * s, 'q_scale': jnp.ones((DIM_HEAD,), jnp.float32), 'k_scale': jnp.ones((DIM_HEAD,), jnp.float32), 'null_kv': jax.random.normal(ks[3], (2, DIM_HEAD), jnp.float32), 'null_attn_bias': jax.random.normal(ks[4], (HEADS,), jnp.float32), 'w0': jax.random.normal(ks[5], (1, DIM), jnp.float32) * s, 'b0': jnp.zeros((DIM,), jnp.float32), 'g0': jnp.ones((DIM,), jnp.float32), 'w1': jax.random.normal(ks[6], (DIM, DIM), jnp.float32) * s, 'b1': jnp.zeros((DIM,), jnp.float32), 'g1': jnp.ones((DIM,), jnp.float32), 'w2': jax.random.normal(ks[7], (DIM, HEADS), jnp.float32) * s, 'b2': jnp.zeros((HEADS,), jnp.float32), 'Wout': jax.random.normal(ks[8], (inner, DIM), jnp.float32) * s, 'g_out': jnp.ones((DIM,), jnp.float32)}
    _L3_cond_all = _L3_cond_setup()
    _L3_cond_in = {k: v for k, v in _L3_cond_all.items() if k in ('g_norm', 'Wq', 'Wkv', 'q_scale', 'k_scale', 'null_attn_bias', 'w0', 'b0', 'g0', 'w1', 'b1', 'g1', 'w2', 'b2', 'Wout', 'g_out')}
    del _L3_cond_all
    return {'x': x, 'cond_64': cond_64, 'fside_16xSxS_0': fside_16xSxS_0, 'mask_BxS_bk0': mask_BxS_bk0, 'mask_BxS_bf1': mask_BxS_bf1, 'L0_cond_wt': _L0_cond_in['wt'], 'L0_cond_wg': _L0_cond_in['wg'], 'L0_cond_w_gate': _L0_cond_in['w_gate'], 'L0_cond_w_up': _L0_cond_in['w_up'], 'L0_cond_w_down': _L0_cond_in['w_down'], 'L0_cond_sw_gate': _L0_cond_in['sw_gate'], 'L0_cond_sw_up': _L0_cond_in['sw_up'], 'L0_cond_sw_down': _L0_cond_in['sw_down'], 'L1_cond_g_in': _L1_cond_in['g_in'], 'L1_cond_null_attn_bias': _L1_cond_in['null_attn_bias'], 'L1_cond_Wq': _L1_cond_in['Wq'], 'L1_cond_Wkv': _L1_cond_in['Wkv'], 'L1_cond_Wo': _L1_cond_in['Wo'], 'L1_cond_g_out': _L1_cond_in['g_out'], 'L2_cond_g_norm': _L2_cond_in['g_norm'], 'L2_cond_Wq': _L2_cond_in['Wq'], 'L2_cond_Wkv': _L2_cond_in['Wkv'], 'L2_cond_q_scale': _L2_cond_in['q_scale'], 'L2_cond_k_scale': _L2_cond_in['k_scale'], 'L2_cond_null_attn_bias': _L2_cond_in['null_attn_bias'], 'L2_cond_w0': _L2_cond_in['w0'], 'L2_cond_b0': _L2_cond_in['b0'], 'L2_cond_g0': _L2_cond_in['g0'], 'L2_cond_w1': _L2_cond_in['w1'], 'L2_cond_b1': _L2_cond_in['b1'], 'L2_cond_g1': _L2_cond_in['g1'], 'L2_cond_w2': _L2_cond_in['w2'], 'L2_cond_b2': _L2_cond_in['b2'], 'L2_cond_Wout': _L2_cond_in['Wout'], 'L2_cond_g_out': _L2_cond_in['g_out'], 'L3_cond_g_norm': _L3_cond_in['g_norm'], 'L3_cond_Wq': _L3_cond_in['Wq'], 'L3_cond_Wkv': _L3_cond_in['Wkv'], 'L3_cond_q_scale': _L3_cond_in['q_scale'], 'L3_cond_k_scale': _L3_cond_in['k_scale'], 'L3_cond_null_attn_bias': _L3_cond_in['null_attn_bias'], 'L3_cond_w0': _L3_cond_in['w0'], 'L3_cond_b0': _L3_cond_in['b0'], 'L3_cond_g0': _L3_cond_in['g0'], 'L3_cond_w1': _L3_cond_in['w1'], 'L3_cond_b1': _L3_cond_in['b1'], 'L3_cond_g1': _L3_cond_in['g1'], 'L3_cond_w2': _L3_cond_in['w2'], 'L3_cond_b2': _L3_cond_in['b2'], 'L3_cond_Wout': _L3_cond_in['Wout'], 'L3_cond_g_out': _L3_cond_in['g_out']}

def reference(x, cond_64, fside_16xSxS_0, mask_BxS_bk0, mask_BxS_bf1, L0_cond_wt, L0_cond_wg, L0_cond_w_gate, L0_cond_w_up, L0_cond_w_down, L0_cond_sw_gate, L0_cond_sw_up, L0_cond_sw_down, L1_cond_g_in, L1_cond_null_attn_bias, L1_cond_Wq, L1_cond_Wkv, L1_cond_Wo, L1_cond_g_out, L2_cond_g_norm, L2_cond_Wq, L2_cond_Wkv, L2_cond_q_scale, L2_cond_k_scale, L2_cond_null_attn_bias, L2_cond_w0, L2_cond_b0, L2_cond_g0, L2_cond_w1, L2_cond_b1, L2_cond_g1, L2_cond_w2, L2_cond_b2, L2_cond_Wout, L2_cond_g_out, L3_cond_g_norm, L3_cond_Wq, L3_cond_Wkv, L3_cond_q_scale, L3_cond_k_scale, L3_cond_null_attn_bias, L3_cond_w0, L3_cond_b0, L3_cond_g0, L3_cond_w1, L3_cond_b1, L3_cond_g1, L3_cond_w2, L3_cond_b2, L3_cond_Wout, L3_cond_g_out):
    import jax
    import jax.numpy as jnp

    def _L0_cond_ref(hidden_states, g, wt, wg, w_gate, w_up, w_down, sw_gate, sw_up, sw_down):
        import jax, jax.numpy as jnp
        import numpy as np
        B, S, H = (4, 256, 128)
        E = 8
        M = 64
        K = 2
        N_SHARED = 2
        SM = M * N_SHARED
        G = 64
        GE_TEMP = 1.0
        ALPHA = 0.001
        SEQ_AUX = True
        NORM_TOPK = True
        COS_TEMP = 0.78
        CONS_ALPHA = 0.01
        LEAKY_SLOPE = 0.01
        EPS_COS = 1e-08

        def _leaky(x):
            return jnp.where(x >= 0, x, LEAKY_SLOPE * x)

        def _moe_forward(hidden_states, g, wt, wg, w_gate, w_up, w_down, sw_gate, sw_up, sw_down):
            b, s, h = hidden_states.shape
            x = hidden_states.reshape(-1, h)
            T = x.shape[0]
            logits_h = x @ wt.T
            logits_g = g @ wg.T
            logits_g = jnp.repeat(logits_g, s, axis=0)
            logits = (logits_h + logits_g / GE_TEMP) / (1.0 + 1.0 / GE_TEMP)
            scores = jax.nn.softmax(logits, axis=-1)
            topk_w, topk_idx = jax.lax.top_k(scores, K)
            if K > 1 and NORM_TOPK:
                topk_w = topk_w / (topk_w.sum(-1, keepdims=True) + 1e-20)
            onehot = jax.nn.one_hot(topk_idx.reshape(b, s * K), E, dtype=jnp.float32)
            ce = onehot.sum(1) / (s * K / E)
            aux_loss = (ce * scores.reshape(b, s, E).mean(1)).sum(1).mean() * ALPHA
            gp = _leaky(jnp.einsum('th,ehm->etm', x, w_gate))
            up = jnp.einsum('th,ehm->etm', x, w_up)
            y_all = jnp.einsum('etm,emh->eth', gp * up, w_down)
            y_sel = y_all[topk_idx, jnp.arange(T)[:, None], :]
            y = (y_sel * topk_w[..., None]).sum(1).reshape(b, s, h)
            p = _leaky(hidden_states @ sw_gate) * (hidden_states @ sw_up) @ sw_down
            y = y + p
            num = jnp.sum(y * p, -1)
            den = jnp.maximum(jnp.linalg.norm(y, axis=-1), EPS_COS) * jnp.maximum(jnp.linalg.norm(p, axis=-1), EPS_COS)
            closs = CONS_ALPHA * jnp.mean(num / den / (1.0 + COS_TEMP))
            return (y, aux_loss + closs)
        y, _ = _moe_forward(hidden_states, g, wt, wg, w_gate, w_up, w_down, sw_gate, sw_up, sw_down)
        return y

    def _L1_cond_ref(x, attn_bias, mask, g_in, null_attn_bias, null_kv, Wq, Wkv, Wo, g_out):
        import jax, jax.numpy as jnp
        import numpy as np
        B, N, DIM, H, DH = (2, 256, 128, 16, 64)
        INNER = H * DH
        EPS = 1e-05

        def layernorm(x, g):
            mean = jnp.mean(x, axis=-1, keepdims=True)
            var = jnp.var(x, axis=-1, keepdims=True)
            return (x - mean) * jax.lax.rsqrt(var + EPS) * g
        b, n, _ = x.shape
        scale = DH ** (-0.5)
        xn = layernorm(x, g_in)
        q = (xn @ Wq).reshape(b, n, H, DH).transpose(0, 2, 1, 3) * scale
        kv = xn @ Wkv
        k, v = (kv[..., :DH], kv[..., DH:])
        nk = jnp.broadcast_to(null_kv[0], (b, 1, DH))
        nv = jnp.broadcast_to(null_kv[1], (b, 1, DH))
        k = jnp.concatenate([nk, k], axis=1)
        v = jnp.concatenate([nv, v], axis=1)
        sim = jnp.einsum('bhid,bjd->bhij', q, k)
        null_col = jnp.broadcast_to(null_attn_bias[:, None, None], (H, n, 1))
        bias = jnp.concatenate([null_col, attn_bias], axis=-1)
        sim = sim + bias
        neg = -jnp.finfo(sim.dtype).max
        j = n + 1
        causal_mask = jnp.triu(jnp.ones((n, j), dtype=bool), k=j - n + 1)
        sim = jnp.where(causal_mask, neg, sim)
        mask_p = jnp.pad(mask, ((0, 0), (1, 0)), constant_values=True)
        sim = jnp.where(mask_p[:, None, None, :], sim, neg)
        attn = jax.nn.softmax(sim, axis=-1)
        out = jnp.einsum('bhij,bjd->bhid', attn, v)
        out = out.transpose(0, 2, 1, 3).reshape(b, n, INNER)
        out = out @ Wo
        return layernorm(out, g_out)

    def _L2_cond_ref(x, mask, g_norm, Wq, Wkv, q_scale, k_scale, null_kv, null_attn_bias, w0, b0, g0, w1, b1, g1, w2, b2, Wout, g_out):
        import jax, jax.numpy as jnp
        import numpy as np
        DIM = 128
        HEADS = 16
        DIM_HEAD = 64
        SCALE = 8.0

        def ln(x, g, eps=1e-05):
            mean = x.mean(axis=-1, keepdims=True)
            var = ((x - mean) ** 2).mean(axis=-1, keepdims=True)
            return (x - mean) * jax.lax.rsqrt(var + eps) * g

        def l2norm(t):
            n = jnp.maximum(jnp.linalg.norm(t, axis=-1, keepdims=True), 1e-12)
            return t / n

        def rel_pos_bias(n, w0, b0, g0, w1, b1, g1, w2, b2, dtype):
            pos = jnp.arange(-n + 1, n, dtype=dtype)[:, None]
            h = jax.nn.silu(ln(pos @ w0 + b0, g0))
            h = jax.nn.silu(ln(h @ w1 + b1, g1))
            h = h @ w2 + b2
            i = jnp.arange(n)
            idx = i[:, None] - i[None, :] + n - 1
            bias = h[idx]
            return jnp.transpose(bias, (2, 0, 1))
        b, n, _ = x.shape
        xn = ln(x, g_norm)
        q = (xn @ Wq).reshape(b, n, HEADS, DIM_HEAD).transpose(0, 2, 1, 3)
        kv = xn @ Wkv
        k, v = (kv[..., :DIM_HEAD], kv[..., DIM_HEAD:])
        nk = jnp.broadcast_to(null_kv[0], (b, 1, DIM_HEAD))
        nv = jnp.broadcast_to(null_kv[1], (b, 1, DIM_HEAD))
        k = jnp.concatenate([nk, k], axis=1)
        v = jnp.concatenate([nv, v], axis=1)
        q = l2norm(q) * q_scale
        k = l2norm(k) * k_scale
        sim = jnp.einsum('bhid,bjd->bhij', q, k) * SCALE
        bias = rel_pos_bias(n, w0, b0, g0, w1, b1, g1, w2, b2, q.dtype)
        null_bias = jnp.broadcast_to(null_attn_bias[:, None, None], (HEADS, n, 1))
        attn_bias = jnp.concatenate([null_bias, bias], axis=-1)
        sim = sim + attn_bias
        neg = -jnp.finfo(sim.dtype).max
        causal = jnp.triu(jnp.ones((n, n + 1), dtype=bool), k=2)
        sim = jnp.where(causal, neg, sim)
        m = jnp.pad(mask, ((0, 0), (1, 0)), constant_values=True)[:, None, None, :]
        sim = jnp.where(m, sim, neg)
        attn = jax.nn.softmax(sim, axis=-1)
        out = jnp.einsum('bhij,bjd->bhid', attn, v)
        out = out.transpose(0, 2, 1, 3).reshape(b, n, HEADS * DIM_HEAD)
        return ln(out @ Wout, g_out)

    def _L3_cond_ref(x, mask, g_norm, Wq, Wkv, q_scale, k_scale, null_kv, null_attn_bias, w0, b0, g0, w1, b1, g1, w2, b2, Wout, g_out):
        import jax, jax.numpy as jnp
        import numpy as np
        DIM = 128
        HEADS = 16
        DIM_HEAD = 64
        SCALE = 8.0

        def ln(x, g, eps=1e-05):
            mean = x.mean(axis=-1, keepdims=True)
            var = ((x - mean) ** 2).mean(axis=-1, keepdims=True)
            return (x - mean) * jax.lax.rsqrt(var + eps) * g

        def l2norm(t):
            n = jnp.maximum(jnp.linalg.norm(t, axis=-1, keepdims=True), 1e-12)
            return t / n

        def rel_pos_bias(n, w0, b0, g0, w1, b1, g1, w2, b2, dtype):
            pos = jnp.arange(-n + 1, n, dtype=dtype)[:, None]
            h = jax.nn.silu(ln(pos @ w0 + b0, g0))
            h = jax.nn.silu(ln(h @ w1 + b1, g1))
            h = h @ w2 + b2
            i = jnp.arange(n)
            idx = i[:, None] - i[None, :] + n - 1
            bias = h[idx]
            return jnp.transpose(bias, (2, 0, 1))
        b, n, _ = x.shape
        xn = ln(x, g_norm)
        q = (xn @ Wq).reshape(b, n, HEADS, DIM_HEAD).transpose(0, 2, 1, 3)
        kv = xn @ Wkv
        k, v = (kv[..., :DIM_HEAD], kv[..., DIM_HEAD:])
        nk = jnp.broadcast_to(null_kv[0], (b, 1, DIM_HEAD))
        nv = jnp.broadcast_to(null_kv[1], (b, 1, DIM_HEAD))
        k = jnp.concatenate([nk, k], axis=1)
        v = jnp.concatenate([nv, v], axis=1)
        q = l2norm(q) * q_scale
        k = l2norm(k) * k_scale
        sim = jnp.einsum('bhid,bjd->bhij', q, k) * SCALE
        bias = rel_pos_bias(n, w0, b0, g0, w1, b1, g1, w2, b2, q.dtype)
        null_bias = jnp.broadcast_to(null_attn_bias[:, None, None], (HEADS, n, 1))
        attn_bias = jnp.concatenate([null_bias, bias], axis=-1)
        sim = sim + attn_bias
        neg = -jnp.finfo(sim.dtype).max
        causal = jnp.triu(jnp.ones((n, n + 1), dtype=bool), k=2)
        sim = jnp.where(causal, neg, sim)
        m = jnp.pad(mask, ((0, 0), (1, 0)), constant_values=True)[:, None, None, :]
        sim = jnp.where(m, sim, neg)
        attn = jax.nn.softmax(sim, axis=-1)
        out = jnp.einsum('bhij,bjd->bhid', attn, v)
        out = out.transpose(0, 2, 1, 3).reshape(b, n, HEADS * DIM_HEAD)
        return ln(out @ Wout, g_out)
    x = x + _L0_cond_ref(x, cond_64, L0_cond_wt, L0_cond_wg, L0_cond_w_gate, L0_cond_w_up, L0_cond_w_down, L0_cond_sw_gate, L0_cond_sw_up, L0_cond_sw_down)
    x = x + _L1_cond_ref(x, fside_16xSxS_0, mask_BxS_bk0, L1_cond_g_in, L1_cond_null_attn_bias, cond_64, L1_cond_Wq, L1_cond_Wkv, L1_cond_Wo, L1_cond_g_out)
    x = x + _L2_cond_ref(x, mask_BxS_bf1, L2_cond_g_norm, L2_cond_Wq, L2_cond_Wkv, L2_cond_q_scale, L2_cond_k_scale, cond_64, L2_cond_null_attn_bias, L2_cond_w0, L2_cond_b0, L2_cond_g0, L2_cond_w1, L2_cond_b1, L2_cond_g1, L2_cond_w2, L2_cond_b2, L2_cond_Wout, L2_cond_g_out)
    x = x + _L3_cond_ref(x, mask_BxS_bf1, L3_cond_g_norm, L3_cond_Wq, L3_cond_Wkv, L3_cond_q_scale, L3_cond_k_scale, cond_64, L3_cond_null_attn_bias, L3_cond_w0, L3_cond_b0, L3_cond_g0, L3_cond_w1, L3_cond_b1, L3_cond_g1, L3_cond_w2, L3_cond_b2, L3_cond_Wout, L3_cond_g_out)
    return x

_drawn_inputs = setup_inputs


def setup_inputs(seed=0):
    import zlib

    import numpy as np

    out = dict(_drawn_inputs(seed))
    spreads = {'L1_cond_g_in': (1.0, 0.2),
     'L1_cond_g_out': (1.0, 0.2),
     'L2_cond_g_norm': (1.0, 0.2),
     'L2_cond_q_scale': (1.0, 0.6),
     'L2_cond_k_scale': (1.0, 0.6),
     'L2_cond_b0': (0.0, 2.0),
     'L2_cond_g0': (1.0, 0.6),
     'L2_cond_b1': (0.0, 0.51),
     'L2_cond_g1': (1.0, 0.6),
     'L2_cond_b2': (0.0, 0.8),
     'L2_cond_g_out': (1.0, 0.2),
     'L3_cond_g_norm': (1.0, 0.2),
     'L3_cond_q_scale': (1.0, 0.6),
     'L3_cond_k_scale': (1.0, 0.6),
     'L3_cond_b0': (0.0, 0.8),
     'L3_cond_g0': (1.0, 0.6),
     'L3_cond_b1': (0.0, 0.479),
     'L3_cond_g1': (1.0, 0.6),
     'L3_cond_b2': (0.0, 0.607),
     'L3_cond_g_out': (1.0, 0.2)}
    factors = {'L2_cond_w0': 4.787,
     'L2_cond_w1': 4.344,
     'L2_cond_w2': 5.144,
     'L3_cond_w0': 8.0,
     'L3_cond_w1': 7.07,
     'L3_cond_w2': 5.726}
    for name, (base, spread) in spreads.items():
        noise = np.random.default_rng([zlib.crc32(name.encode()), seed]).standard_normal(out[name].shape)
        drawn = base * np.exp(spread * noise) if base else spread * noise
        out[name] = jnp.asarray(drawn.astype(out[name].dtype))
    for name, factor in factors.items():
        out[name] = (out[name] * factor).astype(out[name].dtype)
    return out
```

```python
from contextlib import ExitStack

import concourse.bass as bass
from concourse import mybir

F32 = mybir.dt.float32
F32R = mybir.dt.float32r
BF16 = mybir.dt.bfloat16
U8 = mybir.dt.uint8
ALU = mybir.AluOpType
ACT = mybir.ActivationFunctionType
AX_X = mybir.AxisListType.X

P = 128
BATCH = 2
SEQ = 512
DIM = 128
ROWS = SEQ // P
STEPS = ROWS * BATCH
LAYERS = 3
HEADS = 16
DH = 64
INNER = HEADS * DH
VW = DH + 1
GROUP = 4
GROUPS = HEADS // GROUP
HALF = HEADS // 2
UNITS = STEPS * HEADS
KV = 2 * DH
PROJ = KV + HEADS
EXPERTS = 8
MID = 64
PAIRS = EXPERTS // 2
CHUNKS = PAIRS + 1
GDIM = 64
BIG = 1e30
EPS = 1e-5
NORM_FLOOR = 1e-24
Q_SCALE = 8.0
BIAS_ROW = SEQ + P
RING = 4
T_LAG = 2
AV_LAG = 4
ATTN_LOADS = 16 * (2 + 1 + 2 + 2 + 1 + 2 * (LAYERS + 1) + LAYERS + 4)


class Step:

    def __init__(self, layer, c):
        self.layer, self.c = layer, c

    def count(self, per_step, k):
        own = self.c * per_step + k
        return own if self.layer is None else self.layer * (STEPS * per_step) + own


def on_vector(k):
    return k % 4 == 3


def copied_by(vector, k):
    return sum(on_vector(i) == vector for i in range(k + 1))


def width(step):
    return P * (step // BATCH + 1)


def pick(table, layer):
    n = table.shape[2]
    flat = table[:].rearrange("p l n -> p (l n)")
    return flat[:, layer * n:(layer + 1) * n] if isinstance(layer, int) else flat[:, bass.ds(layer * n, n)]


LINKS_STEP = 2 + 2 + 2 + 2 + 1 + 2 * GROUPS + 4


def build(nc, d, out):
    with ExitStack() as ctx:
        def sb(name, shape, dt=F32):
            return ctx.enter_context(nc.sbuf_tensor(name, shape, dt))

        def sem(name):
            return ctx.enter_context(nc.semaphore(name))

        def rows(vector):
            return vector.unsqueeze(0).to_broadcast([P, vector.shape[0]])

        def column(vector):
            return vector.unsqueeze(1)

        ident = sb("ident", [P, P])
        ident_r = sb("ident_r", [P, P], F32R)
        w_q = sb("w_q", [P, LAYERS + 1, INNER])
        w_kvn = sb("w_kvn", [P, LAYERS + 1, PROJ])
        w_o = sb("w_o", [P, LAYERS, STEPS * DIM])
        g_in = sb("g_in", [P, LAYERS + 1, 1])
        g_out = sb("g_out", [P, LAYERS, DIM])
        null_bias = sb("null_bias", [P, LAYERS + 1, HEADS])
        k_factor = sb("k_factor", [P, LAYERS + 1, DH])
        norm_power = sb("norm_power", [P, LAYERS + 1, HEADS + 1])
        rsqrt_power = sb("rsqrt_power", [P, STEPS])
        qk_scales = sb("qk_scales", [P, 2, 2, DH])
        null_k = sb("null_k", [P, DH])
        null_kl = sb("null_kl", [P, LAYERS, DH])
        null_r = sb("null_r", [P, LAYERS])
        null_v = sb("null_v", [P, 1])
        null_v_cols = sb("null_v_cols", [P, STEPS * HEADS])
        null_out = sb("null_out", [HEADS, LAYERS, DIM])
        mask_u8 = sb("mask_u8", [P, 2, BATCH * SEQ], U8)
        mask_all = sb("mask_all", [P, LAYERS, BATCH * SEQ], BF16)
        mask_cur = sb("mask_cur", [P, BATCH * SEQ], BF16)
        first_row = sb("first_row", [P, P], BF16)

        x_res = sb("x_res", [P, STEPS, DIM])
        bias = sb("bias", [P, 2, HEADS, SEQ])
        keys = sb("keys", [P, BATCH, 2, SEQ], F32R)
        values = sb("values", [P, BATCH, ROWS, VW])
        q_stack = sb("q_stack", [P, BATCH, HEADS, P], F32R)
        stats = sb("stats", [P, 6])
        mv = sb("mv", [P, 2])
        var_eps = sb("var_eps", [P, 1])
        rstd = sb("rstd", [P, 1])
        xn = sb("xn", [P, DIM])
        xn_t = sb("xn_t", [P, P])
        kvn = sb("kvn", [P, PROJ])
        q_raw = sb("q_raw", [P, HEADS, DH])
        q_sq = sb("q_sq", [P, HALF, DH])
        k_sq = sb("k_sq", [P, DH])
        sumsq = sb("sumsq", [P, HEADS + 1])
        r_norm = sb("r_norm", [P, HEADS + 1])
        q_n = sb("q_n", [P, HEADS, DH])
        q_split = sb("q_split", [P, HEADS, 2, DH], F32R)
        k_n = sb("k_n", [P, DH])
        k_split = sb("k_split", [P, 2, 2, DH], F32R)
        null_t = sb("null_t", [P, HEADS])
        neg_null = sb("neg_null", [P, BATCH, HEADS])
        neg_logits = sb("neg_logits", [P, RING, SEQ])
        probs = sb("probs", [P, RING, SEQ])
        probs_t = sb("probs_t", [P, RING, SEQ])
        neg_max = sb("neg_max", [P, BATCH, HEADS])
        null_arg = sb("null_arg", [P, BATCH, HEADS])
        null_p = sb("null_p", [P, BATCH, HEADS])
        denom = sb("denom", [P, HEADS])
        r_denom = sb("r_denom", [P, HEADS])
        null_w = sb("null_w", [P, HEADS])
        o_n = sb("o_n", [P, HEADS, DH])
        o_t = sb("o_t", [P, STEPS, P])
        null_wt = sb("null_wt", [HEADS, P])
        y_sb = sb("y_sb", [P, DIM])
        y_stats = sb("y_stats", [P, 6])
        y_mv = sb("y_mv", [P, 2])
        y_var = sb("y_var", [P, 1])
        y_rstd = sb("y_rstd", [P, 1])
        y_c = sb("y_c", [P, DIM])
        spare = sb("spare", [1, 3, 16])

        rank8 = sb("rank8", [P, EXPERTS])
        w_t = sb("w_t", [P, EXPERTS])
        w_g = sb("w_g", [GDIM, EXPERTS])
        g_col = sb("g_col", [GDIM, BATCH])
        g_rep = sb("g_rep", [GDIM, BATCH, P])
        route = sb("route", [P, 4, STEPS, EXPERTS])
        best = sb("best", [P, 4, STEPS])
        pos = sb("pos", [P, ROWS])
        m_cols = sb("m_cols", [P, 2, 2])
        m_w2 = sb("m_w2", [P, 2, HEADS])
        m_b2 = sb("m_b2", [HEADS, 2])
        m_stats = sb("m_stats", [P, STEPS, 6])
        m_mv = sb("m_mv", [P, STEPS, 2])
        m_var = sb("m_var", [P, STEPS])
        m_rstd = sb("m_rstd", [P, STEPS])
        m_bias = sb("m_bias", [HEADS, 2, BIAS_ROW])
        scratch = bias[:, 1].rearrange("p h c -> p (h c)")
        tokens_t = scratch[:, 0:1024]
        leak = scratch[:, 1024:2048].rearrange("p (i c) -> p i c", i=2)
        gated = scratch[:, 2048:2560]
        m_h = scratch[:, 2560:3584].rearrange("p (s c) -> p s c", s=STEPS)
        m_act = scratch[:, 3584:4608].rearrange("p (s c) -> p s c", s=STEPS)
        w_gate, w_up, w_down = (scratch[:, 4608 + 640 * i:5248 + 640 * i].rearrange("p (k c) -> p k c", k=CHUNKS)
                                for i in range(3))
        m_rows = scratch[:, 6528:7296].rearrange("p (l i c) -> p l i c", l=2, i=3)
        m_w1 = scratch[:, 7296:7552].rearrange("p (l c) -> p l c", l=2)
        pair_sel = scratch[0:EXPERTS, 7552:8064]
        hidden = [a[:].rearrange("p r c -> p (r c)")[:, 0:STEPS * P] for a in (neg_logits, probs, probs_t)]
        hidden += [a[:].rearrange("p r c -> p (r c)")[:, STEPS * P:2 * STEPS * P] for a in (neg_logits, probs)]
        coef_t = o_t[0:EXPERTS].rearrange("e s c -> e (s c)")
        rel_bias = nc.dram_tensor("rel_bias", [2, HEADS, P, SEQ], F32, kind="Internal").ap()

        bank = [ctx.enter_context(nc.psum_tensor(f"bank{i}", [P, 512], F32)) for i in range(8)]
        scores_ps, probs_t_bank, av_bank, misc = bank[0:2], bank[2:4], bank[4:6], bank[6:8]

        x_in, consts_in, route_in, expert_in, mlp_in = (sem(n) for n in (
            "x_in", "consts_in", "route_in", "expert_in", "mlp_in"))
        attn_in, mask_in, rel_bias_out, out_done = (sem(n) for n in (
            "attn_in", "mask_in", "rel_bias_out", "out_done"))
        bias_in = [sem("bias_in0"), sem("bias_in1")]
        pool_consts, first_row_made, tables_made, mask_made = (sem(n) for n in (
            "pool_consts", "first_row_made", "tables_made", "mask_made"))
        x_t_ps, x_t_sb, g_rep_made, router_ps, router_arg, router_exp = (sem(n) for n in (
            "x_t_ps", "x_t_sb", "g_rep_made", "router_ps", "router_arg", "router_exp"))
        coef_made, coef_t_ps, coef_t_sb, up_ps, leak_sb = (sem(n) for n in (
            "coef_made", "coef_t_ps", "coef_t_sb", "up_ps", "leak_sb"))
        hidden_made, spread_ps, hidden_ready, moe_ps = (sem(n) for n in (
            "hidden_made", "spread_ps", "hidden_ready", "moe_ps"))
        null_sq_made, null_r_made, null_cols_made, null_out_ps = (sem(n) for n in (
            "null_sq_made", "null_r_made", "null_cols_made", "null_out_ps"))
        m_var_ready, m_rstd_ready, m_norm_ready, m_t_ps, m_t_sb = (sem(n) for n in (
            "m_var_ready", "m_rstd_ready", "m_norm_ready", "m_t_ps", "m_t_sb"))
        m_h_ps, m_h_sb, m_out_ps, m_out_sb = (sem(n) for n in ("m_h_ps", "m_h_sb", "m_out_ps", "m_out_sb"))
        var_ready, rstd_ready, xn_ready, xn_t_ps, xn_t_sb = (sem(n) for n in (
            "var_ready", "rstd_ready", "xn_ready", "xn_t_ps", "xn_t_sb"))
        kvn_ps, kvn_sb, q_ps, q_sq_sb, sumsq_ready = (sem(n) for n in (
            "kvn_ps", "kvn_sb", "q_ps", "q_sq_sb", "sumsq_ready"))
        norm_ready, q_scaled, q_high, q_low, k_split_ready = (sem(n) for n in (
            "norm_ready", "q_scaled", "q_high", "q_low", "k_split_ready"))
        k_t_ps, keys_ready, q_t_ps, q_ready, null_ready = (sem(n) for n in (
            "k_t_ps", "keys_ready", "q_t_ps", "q_ready", "null_ready"))
        mask_ready, bias_ready, scores_ready, logits_ready, probs_ready = (sem(n) for n in (
            "mask_ready", "bias_ready", "scores_ready", "logits_ready", "probs_ready"))
        probs_t_ready, copied_scalar, copied_vector, av_ready = (sem(n) for n in (
            "probs_t_ready", "copied_scalar", "copied_vector", "av_ready"))
        null_arg_ready, null_p_ready, group_ready, o_t_ps, o_t_sb = (sem(n) for n in (
            "null_arg_ready", "null_p_ready", "group_ready", "o_t_ps", "o_t_sb"))
        null_wt_sb, y_ps, y_sb_ready, y_var_ready, y_rstd_ready = (sem(n) for n in (
            "null_wt_sb", "y_ps", "y_sb_ready", "y_var_ready", "y_rstd_ready"))
        x_ready, vector_link = sem("x_ready"), sem("vector_link")

        def wait_copied(eng, layer, k):
            v = on_vector(k)
            eng.wait_ge(copied_vector if v else copied_scalar,
                        layer * copied_by(v, UNITS - 1) + copied_by(v, k))

        def wait_apart(eng):
            calls = apart_calls.setdefault(eng.engine, [0])
            calls[0] += 1
            column = calls[0] % spare.shape[2]
            if eng is nc.vector:
                eng.memset(spare[0:1, 0, column:column + 1], 0.0)
            elif eng is nc.gpsimd:
                eng.tensor_tensor(spare[0:1, 1, column:column + 1], rsqrt_power[0:1, 0:1], rsqrt_power[0:1, 0:1], ALU.add)
            else:
                eng.copy(spare[0:1, 2, column:column + 1], ident[0:1, 0:1])

        apart_calls = {}
        block = ctx.enter_context(nc.Block())

        @block.sync
        def _(sp):
            for b in range(BATCH):
                sp.dma_start(x_res[:].rearrange("p (r b) c -> p r b c", b=BATCH)[:, :, b, :],
                             d["x"][b].rearrange("(r p) c -> p r c", p=P)).then_inc(x_in, 16)
            for to, name in ((ident, "ident"), (pos, "pos"), (pair_sel, "pair_sel")):
                sp.dma_start(to[:], d[name]).then_inc(consts_in, 16)
            sp.dma_start(rank8[:], rows(d["rank8"])).then_inc(consts_in, 16)
            for to, name in ((w_t, "wt_t"), (w_g, "wg_t"), (g_col, "cond_t")):
                sp.dma_start(to[:], d[name]).then_inc(route_in, 16)
            for to, routed, shared in ((w_gate, "w_gate", "sw_gate"), (w_up, "w_up", "sw_up")):
                sp.dma_start(to[:, 0:PAIRS, :].rearrange("h k (e m) -> h (k e) m", e=2),
                             d[routed].rearrange("e h m -> h e m")).then_inc(expert_in, 16)
                sp.dma_start(to[:, PAIRS, :], d[shared]).then_inc(expert_in, 16)
            sp.dma_start(w_down[:, 0:PAIRS, :],
                         d["w_down"].rearrange("(k e) m h -> (e m) k h", e=2)).then_inc(expert_in, 16)
            sp.dma_start(w_down[:, PAIRS, :], d["sw_down"]).then_inc(expert_in, 16)
            for b in range(2):
                sp.dma_start(null_v[b * DH:(b + 1) * DH, :], column(d["cond"][1])).then_inc(attn_in, 16)
            sp.dma_start(null_k[:], rows(d["cond"][0])).then_inc(attn_in, 16)
            sp.dma_start(w_q[:, 0:LAYERS, :], d["w_q"].rearrange("l c n -> c l n")).then_inc(attn_in, 16)
            sp.dma_start(w_q[:, LAYERS, :], d["w_q"][0]).then_inc(attn_in, 16)
            sp.dma_start(w_kvn[:, 0:LAYERS, 0:KV], d["w_kv"].rearrange("l c n -> c l n")).then_inc(attn_in, 16)
            sp.dma_start(w_kvn[:, LAYERS, 0:KV], d["w_kv"][0]).then_inc(attn_in, 16)
            sp.dma_start(w_o[:].rearrange("p l (k n) -> p (l k) n", n=DIM),
                         d["w_o"].rearrange("l (k p) n -> p (l k) n", p=P)).then_inc(attn_in, 16)
            for l in range(LAYERS + 1):
                sp.dma_start(g_in[:, l, :], column(d["g_in"][l % LAYERS])).then_inc(attn_in, 16)
                sp.dma_start(null_bias[:, l, :], rows(d["null_bias"][l % LAYERS])).then_inc(attn_in, 16)
            for l in range(LAYERS):
                sp.dma_start(g_out[:, l, :], rows(d["g_out"][l])).then_inc(attn_in, 16)
            for l in range(2):
                sp.dma_start(qk_scales[:, l, 0, :], rows(d["q_scale"][l])).then_inc(attn_in, 16)
                sp.dma_start(qk_scales[:, l, 1, :], rows(d["k_scale"][l])).then_inc(attn_in, 16)
            for i, name in enumerate(("mask0", "mask1")):
                sp.dma_start(mask_u8[:, i, :], rows(d[name])).then_inc(mask_in, 16)
            for t in range(ROWS):
                if t == 1:
                    sp.wait_ge(x_ready, STEPS)
                    sp.wait_ge(m_out_sb, 2)
                    for l in range(2):
                        skewed = bass.AP(m_bias, l * BIAS_ROW + P - 1, [[2 * BIAS_ROW, HEADS], [-1, P], [1, SEQ]])
                        sp.dma_start(rel_bias[l], skewed).then_inc(rel_bias_out, 16)
                if t >= 2:
                    sp.wait_ge(logits_ready, HEADS * BATCH * (t - 1))
                w = P * (t + 1)
                sp.dma_start(bias[:, t % 2, :, 0:w],
                             d["attn_bias"][:, P * t:P * (t + 1), 0:w].rearrange("h p c -> p h c")
                             ).then_inc(bias_in[t % 2], 16)
            sp.wait_ge(rel_bias_out, 32)
            for layer in range(1, LAYERS):
                for t in range(ROWS):
                    sp.wait_ge(logits_ready, UNITS * layer + HEADS * BATCH * (t - 1))
                    w = P * (t + 1)
                    sp.dma_start(bias[:, t % 2, :, 0:w],
                                 rel_bias[layer - 1, :, :, SEQ - w:SEQ].rearrange("h p c -> p h c")
                                 ).then_inc(bias_in[t % 2], 16)
            for s in range(STEPS):
                sp.wait_ge(x_ready, STEPS * LAYERS + s + 1)
                sp.dma_start(out[s % BATCH, (s // BATCH) * P:(s // BATCH + 1) * P, :], x_res[:, s, :]
                             ).then_inc(out_done, 16)
            sp.wait_ge(out_done, 16 * STEPS)

        @block.gpsimd
        def _(pool):
            for to, value in ((rsqrt_power[:], -0.5), (norm_power[:, 1:3, :], -0.5), (norm_power[:, 0, :], 0.0),
                              (norm_power[:, 3, :], 0.0), (k_factor[:, 0, :], DH ** -0.5),
                              (k_factor[:, 3, :], DH ** -0.5), (first_row[:], 0.0), (null_v_cols[:], 0.0),
                              (values[:], 1.0), (m_bias[:], 0.0)):
                pool.memset(to, value).then_inc(pool_consts, 1)
            pool.wait_ge(pool_consts, 10)
            pool.memset(first_row[0:1, :], 1.0).then_inc(first_row_made, 1)
            for l in range(2):
                for i, name in enumerate(("w0", "b0", "b1")):
                    pool.dma_start(m_rows[:, l, i, :], rows(d[name][l])).then_inc(mlp_in, 16)
                for i, name in enumerate(("g0", "g1")):
                    pool.dma_start(m_cols[:, l, i:i + 1], column(d[name][l])).then_inc(mlp_in, 16)
                pool.dma_start(m_w1[:, l, :], d["w1"][l]).then_inc(mlp_in, 16)
                pool.dma_start(m_w2[:, l, :], d["w2"][l]).then_inc(mlp_in, 16)
                pool.dma_start(m_b2[:, l:l + 1], column(d["b2"][l])).then_inc(mlp_in, 16)
            for stage in range(2):
                pool.wait_ge(m_var_ready, stage + 1)
                pool.tensor_tensor(m_rstd[:], m_var[:], rsqrt_power[:], ALU.pow).then_inc(m_rstd_ready, 1)
            pool.wait_ge(null_sq_made, 1)
            for l in range(LAYERS):
                pool.tensor_tensor(null_r[:, l:l + 1], sumsq[:, 0:1], norm_power[:, l, 0:1], ALU.pow
                                   ).then_inc(null_r_made, 1)

            def input_rstd(m):
                pool.wait_ge(var_ready, m.count(1, 1))
                pool.tensor_tensor(rstd[:], var_eps[:], rsqrt_power[:, 0:1], ALU.pow).then_inc(rstd_ready, 1)

            def output_rstd(n):
                pool.wait_ge(y_var_ready, n.count(1, 1))
                pool.tensor_tensor(y_rstd[:], y_var[:], rsqrt_power[:, 0:1], ALU.pow).then_inc(y_rstd_ready, 1)

            def queries(m, layer, half):
                a, b = (0, 1 + HALF) if half == 0 else (1 + HALF, 1 + HEADS)
                h0, h1 = half * HALF, (half + 1) * HALF
                pool.wait_ge(sumsq_ready, m.count(2, half + 1))
                wait_apart(pool)
                pool.tensor_tensor(r_norm[:, a:b], sumsq[:, a:b], pick(norm_power, layer)[:, a:b], ALU.pow
                                   ).then_inc(norm_ready, 1)
                pool.wait_ge(norm_ready, m.count(2, half + 1))
                pool.tensor_tensor(q_n[:, h0:h1, :], q_raw[:, h0:h1, :],
                                   r_norm[:, 1 + h0:1 + h1].unsqueeze(2).to_broadcast([P, HALF, DH]),
                                   ALU.mult).then_inc(q_scaled, 1)
                pool.wait_ge(q_scaled, m.count(2, half + 1))
                if m.layer is not None:
                    pool.wait_ge(q_t_ps, m.count(GROUPS, 0))
                wait_apart(pool)
                pool.tensor_scalar(q_split[:, h0:h1, 0, :], q_n[:, h0:h1, :], 1.0, 0.0, ALU.mult, ALU.add
                                   ).then_inc(q_high, 1)
                pool.wait_ge(q_high, m.count(2, half + 1))
                pool.tensor_tensor(q_split[:, h0:h1, 1, :], q_n[:, h0:h1, :],
                                   q_split[:, h0:h1, 0, :].bitcast(F32), ALU.subtract).then_inc(q_low, 1)

            def causal(layer, t):
                pool.wait_ge(bias_in[t % 2], layer * 32 + 16 * (t // 2 + 1))
                wait_apart(pool)
                diagonal = bias[:, t % 2, :, P * t:P * (t + 1)]
                pool.affine_select(out=diagonal, in_=diagonal, compare_op=ALU.is_ge, fill=masked, base=0,
                                   pattern=[[0, HEADS], [-1, P]], channel_multiplier=1
                                   ).then_inc(bias_ready, 1)

            input_rstd(Step(None, 0))
            input_rstd(Step(None, 1))
            for half in range(2):
                queries(Step(None, 0), 0, half)
            masked = pool.to_reg(-BIG)
            with pool.Fori(0, LAYERS) as layer:
                causal(layer, 0)
                for s in range(STEPS):
                    for half in range(2):
                        queries(Step(layer, s + 1), layer + (s + 1) // STEPS, half)
                    if s >= 1:
                        output_rstd(Step(layer, s - 1))
                    input_rstd(Step(layer, s + 2))
                    if s % 2 == 1 and s < STEPS - 1:
                        causal(layer, s // 2 + 1)
                output_rstd(Step(layer, STEPS - 1))

        @block.scalar
        def _(act):
            for i in range(2):
                act.wait_ge(x_t_ps, i + 1)
                act.copy(tokens_t[:, 512 * i:512 * (i + 1)], bank[i][:]).then_inc(x_t_sb, 1)
            act.wait_ge(router_arg, 1)
            act.activation(route[:, 1], route[:, 0], ACT.Exp, scale=0.5).then_inc(router_exp, 1)
            for j in range(2 * CHUNKS):
                act.wait_ge(up_ps, j + 1)
                if j >= 2:
                    act.wait_ge(hidden_made, j - 1)
                act.mul(leak[:, j % 2, :], bank[2 + j % 2][:], 0.01).then_inc(leak_sb, 1)
            for stage in range(2):
                for i in range(4):
                    l = i // 2
                    act.wait_ge(m_t_ps, 4 * stage + i + 1)
                    if stage == 1:
                        act.wait_ge(m_h_ps, 4)
                    act.activation(m_act[:, 2 * i:2 * i + 2, :].rearrange("p s c -> p (s c)"),
                                   bank[4 + i % 2][:, 0:2 * P], ACT.Silu, scale=m_cols[:, l, stage:stage + 1]
                                   ).then_inc(m_t_sb, 1)

            def input_t(m, layer):
                act.wait_ge(xn_t_ps, m.count(1, 1))
                if m.layer is not None:
                    act.wait_ge(q_ps, m.count(2, 0))
                wait_apart(act)
                act.activation(xn_t[:], misc[0][:, 0:P], ACT.Copy, scale=pick(g_in, layer)).then_inc(xn_t_sb, 1)

            def raw_queries(m, half):
                act.wait_ge(q_ps, m.count(2, half + 1))
                if m.layer is not None:
                    act.wait_ge(q_scaled, m.count(2, 0))
                if m.layer is not None or half == 1:
                    act.wait_ge(sumsq_ready, m.count(2, half))
                act.copy(q_raw[:, half * HALF:(half + 1) * HALF, :].rearrange("p h d -> p (h d)"),
                         misc[half][:])
                act.activation(q_sq[:].rearrange("p h d -> p (h d)"), misc[half][:], ACT.Square
                               ).then_inc(q_sq_sb, 1)

            def queries_t(m, g):
                act.wait_ge(q_t_ps, m.count(GROUPS, g + 1))
                if m.c >= 2:
                    act.wait_ge(scores_ready, m.count(HEADS, -HEADS))
                act.copy(q_stack[:, m.c % BATCH, GROUP * g:GROUP * (g + 1), :].rearrange("p h c -> p (h c)"),
                         misc[g % 2][:]).then_inc(q_ready, 1)

            def output_t(n, i):
                act.wait_ge(o_t_ps, n.count(3, i + 1))
                if n.c >= 1:
                    act.wait_ge(y_ps, n.count(1, 0))
                act.copy(o_t[:, 4 * i:4 * i + 4, :].rearrange("p k c -> p (k c)"), misc[i][:]
                         ).then_inc(o_t_sb, 1)

            def exponentials(layer, k):
                s, h = divmod(k, HEADS)
                act.wait_ge(logits_ready, layer * UNITS + k + 1)
                if k >= RING:
                    act.wait_ge(probs_t_ready, layer * UNITS + k - RING + 1)
                act.activation(probs[:, k % RING, 0:width(s)], neg_logits[:, k % RING, 0:width(s)], ACT.Exp,
                               bias=neg_max[:, s % BATCH, h:h + 1], scale=-1.0).then_inc(probs_ready, 1)

            def null_exponentials(n, g):
                act.wait_ge(null_arg_ready, n.count(GROUPS, g + 1))
                act.activation(null_p[:, n.c % BATCH, GROUP * g:GROUP * (g + 1)],
                               null_arg[:, n.c % BATCH, GROUP * g:GROUP * (g + 1)], ACT.Exp, scale=-1.0
                               ).then_inc(null_p_ready, 1)

            def copy_probs(layer, k):
                act.wait_ge(probs_t_ready, layer * UNITS + k + 1)
                if k >= RING:
                    act.wait_ge(av_ready, layer * UNITS + k - RING + 1)
                act.copy(probs_t[:, k % RING, 0:width(k // HEADS)], probs_t_bank[k % 2][:, 0:width(k // HEADS)]
                         ).then_inc(copied_scalar, 1)

            first = Step(None, 0)
            input_t(first, 0)
            for half in range(2):
                raw_queries(first, half)
            for g in range(GROUPS):
                queries_t(first, g)
            with act.Fori(0, LAYERS) as layer:
                for s in range(STEPS):
                    n, m, before = Step(layer, s), Step(layer, s + 1), Step(layer, s - 1)
                    for h in range(HEADS):
                        k = s * HEADS + h
                        if k >= T_LAG and not on_vector(k - T_LAG):
                            copy_probs(layer, k - T_LAG)
                        exponentials(layer, k)
                        if h % GROUP == 0 and k >= GROUP:
                            null_exponentials(Step(layer, (k - 1) // HEADS), (k - 1) % HEADS // GROUP)
                        if h == 1:
                            input_t(m, layer + (s + 1) // STEPS)
                        if h in (3, 5):
                            raw_queries(m, (h - 3) // 2)
                        if h in (6, 8) and s >= 1:
                            output_t(before, (h - 6) // 2)
                        if h >= HEADS - GROUPS:
                            queries_t(m, h - (HEADS - GROUPS))
                for k in range(UNITS - T_LAG, UNITS):
                    if not on_vector(k):
                        copy_probs(layer, k)
                null_exponentials(Step(layer, STEPS - 1), GROUPS - 1)
                for i in range(2):
                    output_t(Step(layer, STEPS - 1), i)

        @block.vector
        def _(dve):
            links, base = [0], [0]

            def link(ins, apart=False):
                links[0] += 1
                ins.then_inc(vector_link, 1)
                dve.wait_ge(vector_link, base[0] + links[0])
                if apart:
                    wait_apart(dve)

            dve.wait_ge(consts_in, 64)
            dve.wait_ge(mlp_in, 16 * 16)

            def normalize_positions(stage):
                for i in range(STEPS):
                    ins = dve.bn_stats(m_stats[:, i, :], m_h[:, i, :])
                link(ins)
                for i in range(STEPS - 1):
                    dve.bn_aggr(m_mv[:, i, :], m_stats[:, i, :])
                link(dve.bn_aggr(m_mv[:, STEPS - 1, :], m_stats[:, STEPS - 1, :]))
                dve.tensor_scalar(m_var[:], m_mv[:, :, 1], EPS, None, ALU.add).then_inc(m_var_ready, 1)
                dve.wait_ge(m_rstd_ready, stage + 1)
                for i in range(STEPS):
                    dve.tensor_scalar(m_h[:, i, :], m_h[:, i, :], m_mv[:, i, 0:1], m_rstd[:, i:i + 1],
                                      ALU.subtract, ALU.mult).then_inc(m_norm_ready, 1)

            for i in range(STEPS):
                ins = dve.scalar_tensor_tensor(out=m_h[:, i, :], in0=m_rows[:, i // ROWS, 0, :],
                                               scalar=pos[:, i % ROWS:i % ROWS + 1],
                                               in1=m_rows[:, i // ROWS, 1, :], op0=ALU.mult, op1=ALU.add)
            link(ins)
            normalize_positions(0)
            dve.wait_ge(route_in, 48)
            dve.tensor_copy(g_rep[:], g_col[:].unsqueeze(2).to_broadcast([GDIM, BATCH, P])
                            ).then_inc(g_rep_made, 1)
            link(dve.tensor_copy(ident_r[:], ident[:]))
            over = [P, STEPS, EXPERTS]
            dve.wait_ge(router_ps, 1)
            logits = bank[2][:, 0:STEPS * EXPERTS].rearrange("p (s e) -> p s e", s=STEPS)
            link(dve.tensor_reduce(best[:, 0], logits, AX_X, ALU.max))
            dve.tensor_tensor(route[:, 0], logits, best[:, 0].unsqueeze(2).to_broadcast(over), ALU.subtract
                              ).then_inc(router_arg, 1)
            dve.wait_ge(router_exp, 1)
            link(dve.tensor_reduce(best[:, 0], route[:, 1], AX_X, ALU.add))
            link(dve.reciprocal(best[:, 1], best[:, 0]))
            link(dve.tensor_tensor(route[:, 0], route[:, 1], best[:, 1].unsqueeze(2).to_broadcast(over),
                                   ALU.mult))
            ranks = rank8[:].unsqueeze(1).to_broadcast(over)
            for i, rest in enumerate((route[:, 0], route[:, 3])):
                link(dve.tensor_reduce(best[:, 0], rest, AX_X, ALU.max))
                link(dve.tensor_tensor(route[:, 1], rest, best[:, 0].unsqueeze(2).to_broadcast(over),
                                       ALU.is_equal))
                link(dve.tensor_tensor(route[:, 1], route[:, 1], ranks, ALU.mult))
                link(dve.tensor_reduce(best[:, 1], route[:, 1], AX_X, ALU.max))
                link(dve.tensor_tensor(route[:, 2 - i], route[:, 1],
                                       best[:, 1].unsqueeze(2).to_broadcast(over), ALU.is_equal))
                if i == 0:
                    link(dve.scalar_tensor_tensor(out=route[:, 3], in0=route[:, 2], scalar=-2.0,
                                                  in1=route[:, 0], op0=ALU.mult, op1=ALU.add))
            link(dve.tensor_tensor(route[:, 3], route[:, 1], route[:, 2], ALU.add))
            link(dve.tensor_tensor(route[:, 1], route[:, 0], route[:, 3], ALU.mult))
            link(dve.tensor_reduce(best[:, 0], route[:, 1], AX_X, ALU.add))
            link(dve.tensor_scalar(best[:, 1], best[:, 0], 1e-20, None, ALU.add))
            link(dve.reciprocal(best[:, 2], best[:, 1]))
            dve.tensor_tensor(route[:, 2], route[:, 1], best[:, 2].unsqueeze(2).to_broadcast(over), ALU.mult
                              ).then_inc(coef_made, 1)
            for j in range(2 * CHUNKS):
                half, c = divmod(j, CHUNKS)
                dve.wait_ge(leak_sb, j + 1)
                link(dve.tensor_tensor(gated, bank[2 + j % 2][:], leak[:, j % 2, :], ALU.max))
                dve.tensor_tensor(hidden[c][:, 512 * half:512 * (half + 1)], gated, bank[4 + j % 2][:],
                                  ALU.mult).then_inc(hidden_made, 1)
                dve.wait_ge(hidden_made, j + 1)
                if j == 1:
                    for i in range(2):
                        dve.wait_ge(coef_t_ps, i + 1)
                        dve.tensor_copy(coef_t[:, 512 * i:512 * (i + 1)], bank[6 + i][0:EXPERTS, :]
                                        ).then_inc(coef_t_sb, 1)
            for j in range(2 * PAIRS):
                half, c = divmod(j, PAIRS)
                dve.wait_ge(spread_ps, j + 1)
                part = hidden[c][:, 512 * half:512 * (half + 1)]
                dve.tensor_tensor(part, part, bank[j % 2][:], ALU.mult).then_inc(hidden_ready, 1)
            for i in range(4):
                l = i // 2
                dve.wait_ge(m_h_ps, i + 1)
                ins = dve.tensor_tensor(m_h[:, 2 * i:2 * i + 2, :],
                                        bank[6 + i % 2][:, 0:2 * P].rearrange("p (s c) -> p s c", s=2),
                                        m_rows[:, l, 2:3, :].to_broadcast([P, 2, DIM]), ALU.add)
                ins.then_inc(m_h_sb, 1)
            dve.wait_ge(m_h_sb, 4)
            normalize_positions(1)
            dve.wait_ge(mask_in, 32)
            for l in range(LAYERS):
                dve.tensor_scalar(mask_all[:, l, :], mask_u8[:, min(l, 1), :], -1.0, BIG, ALU.add, ALU.mult
                                  ).then_inc(mask_made, 1)
            dve.wait_ge(attn_in, ATTN_LOADS)
            dve.wait_ge(pool_consts, 10)
            for l in range(2):
                link(dve.scalar_tensor_tensor(out=k_factor[:, 1 + l, :], in0=qk_scales[:, l, 0, :],
                                              scalar=Q_SCALE, in1=qk_scales[:, l, 1, :],
                                              op0=ALU.mult, op1=ALU.mult))
            for i in range(2):
                cols = slice(i, (STEPS - 1) * (HEADS + 2) + i + 1, HEADS + 2)
                ins = dve.tensor_copy(null_v_cols[i * DH:(i + 1) * DH, cols],
                                      null_v[i * DH:(i + 1) * DH, :].to_broadcast([DH, STEPS]))
            ins.then_inc(null_cols_made, 1)
            link(dve.tensor_tensor(k_sq[:], null_k[:], null_k[:], ALU.mult))
            link(dve.tensor_reduce(sumsq[:, 0:1], k_sq[:], AX_X, ALU.add))
            link(dve.tensor_scalar(sumsq[:, 0:1], sumsq[:, 0:1], NORM_FLOOR, None, ALU.max))
            dve.engine_nop().then_inc(null_sq_made, 1)
            dve.wait_ge(null_r_made, LAYERS)
            for l in range(LAYERS):
                link(dve.scalar_tensor_tensor(out=null_kl[:, l, :], in0=null_k[:], scalar=null_r[:, l:l + 1],
                                              in1=k_factor[:, l, :], op0=ALU.mult, op1=ALU.mult))
                link(dve.tensor_tensor(q_n[:], w_q[:, l, :].rearrange("p (h d) -> p h d", h=HEADS),
                                       null_kl[:, l:l + 1, :].to_broadcast([P, HEADS, DH]), ALU.mult))
                link(dve.tensor_reduce(w_kvn[:, l, KV:PROJ], q_n[:], AX_X, ALU.add))
            dve.tensor_copy(w_kvn[:, LAYERS, KV:PROJ], w_kvn[:, 0, KV:PROJ]).then_inc(tables_made, 1)
            dve.wait_ge(null_out_ps, 1)
            link(dve.tensor_copy(null_out[:].rearrange("h l n -> h (l n)"), bank[2][0:HEADS, 0:LAYERS * DIM]))
            dve.wait_ge(x_in, 32)
            for s in range(STEPS):
                dve.wait_ge(moe_ps, s + 1)
                dve.tensor_tensor(x_res[:, s, :], x_res[:, s, :], bank[6 + s % 2][:, 0:DIM], ALU.add
                                  ).then_inc(x_ready, 1)
            for l in range(2):
                dve.wait_ge(m_out_ps, l + 1)
                dve.tensor_scalar(m_bias[:, l, 0:SEQ], bank[l][0:HEADS, :], m_b2[:, l:l + 1], None, ALU.add
                                  ).then_inc(m_out_sb, 1)

            def input_stats(m):
                dve.wait_ge(x_ready, m.count(1, 1))
                if m.layer is not None or m.c >= 1:
                    dve.wait_ge(xn_ready, m.count(1, 0))
                link(dve.bn_stats(stats[:], x_res[:, m.c % STEPS, :]), apart=True)
                link(dve.bn_aggr(mv[:], stats[:]))
                dve.tensor_scalar(var_eps[:], mv[:, 1:2], EPS, None, ALU.add).then_inc(var_ready, 1)

            def input_norm(m):
                dve.wait_ge(rstd_ready, m.count(1, 1))
                if m.layer is not None or m.c >= 1:
                    dve.wait_ge(xn_t_ps, m.count(1, 0))
                dve.tensor_scalar(xn[:], x_res[:, m.c % STEPS, :], mv[:, 0:1], rstd[:], ALU.subtract, ALU.mult
                                  ).then_inc(xn_ready, 1)

            def keys_values(m):
                dve.wait_ge(kvn_ps, m.count(1, 1))
                dve.tensor_copy(kvn[:], misc[1][:, 0:PROJ]).then_inc(kvn_sb, 1)
                dve.wait_ge(kvn_sb, m.count(1, 1))
                if m.c == STEPS:
                    dve.wait_ge(av_ready, m.count(HEADS, -HEADS))
                dve.tensor_copy(values[:, m.c % BATCH, m.c % STEPS // BATCH, 0:DH], kvn[:, DH:KV])
                link(dve.tensor_tensor(k_sq[:], kvn[:, 0:DH], kvn[:, 0:DH], ALU.mult))
                link(dve.tensor_reduce(sumsq[:, 0:1], k_sq[:], AX_X, ALU.add))

            def query_squares(m, half):
                a, b = (0, 1 + HALF) if half == 0 else (1 + HALF, 1 + HEADS)
                dve.wait_ge(q_sq_sb, m.count(2, half + 1))
                link(dve.tensor_reduce(sumsq[:, 1 + half * HALF:b], q_sq[:], AX_X, ALU.add))
                dve.tensor_scalar(sumsq[:, a:b], sumsq[:, a:b], NORM_FLOOR, None, ALU.max
                                  ).then_inc(sumsq_ready, 1)

            def split_keys(m, layer):
                dve.wait_ge(norm_ready, m.count(2, 1))
                link(dve.scalar_tensor_tensor(out=k_n[:], in0=kvn[:, 0:DH], scalar=r_norm[:, 0:1],
                                              in1=pick(k_factor, layer), op0=ALU.mult, op1=ALU.mult))
                twice = k_n[:].unsqueeze(1).to_broadcast([P, 2, DH])
                if m.layer is not None:
                    dve.wait_ge(k_t_ps, m.count(1, 0))
                link(dve.tensor_copy(k_split[:, 0], twice))
                dve.tensor_tensor(k_split[:, 1], twice, k_split[:, 0].bitcast(F32), ALU.subtract
                                  ).then_inc(k_split_ready, 1)

            def null_scores(m, layer):
                dve.wait_ge(norm_ready, m.count(2, 2))
                link(dve.tensor_tensor(null_t[:], kvn[:, KV:PROJ], r_norm[:, 1:1 + HEADS], ALU.mult))
                dve.scalar_tensor_tensor(out=neg_null[:, m.c % BATCH, :], in0=null_t[:], scalar=-1.0,
                                         in1=pick(null_bias, layer), op0=ALU.mult, op1=ALU.subtract
                                         ).then_inc(null_ready, 1)

            def keys_t(m):
                t = m.c % STEPS // BATCH
                dve.wait_ge(k_t_ps, m.count(1, 1))
                if m.c == STEPS:
                    dve.wait_ge(scores_ready, m.count(HEADS, -HEADS))
                dve.tensor_copy(keys[:, m.c % BATCH, :, P * t:P * (t + 1)],
                                misc[1][:, 0:2 * P].rearrange("p (i c) -> p i c", i=2)
                                ).then_inc(keys_ready, 1)

            def unit_logits(layer, k):
                s, h = divmod(k, HEADS)
                if h == 0:
                    dve.wait_ge(bias_ready, layer * ROWS + s // BATCH + 1)
                    dve.wait_ge(null_ready, Step(layer, s).count(1, 1))
                dve.wait_ge(scores_ready, layer * UNITS + k + 1)
                if k >= RING:
                    dve.wait_ge(probs_ready, layer * UNITS + k - RING + 1)
                wait_apart(dve)
                dve.tensor_tensor_reduce(neg_logits[:, k % RING, 0:width(s)], scores_ps[k % 2][:, 0:width(s)],
                                         bias[:, s // BATCH % 2, h, 0:width(s)], -1.0,
                                         neg_null[:, s % BATCH, h:h + 1], ALU.add, ALU.min,
                                         neg_max[:, s % BATCH, h:h + 1]).then_inc(logits_ready, 1)

            def copy_probs(layer, k):
                dve.wait_ge(probs_t_ready, layer * UNITS + k + 1)
                if k >= RING:
                    dve.wait_ge(av_ready, layer * UNITS + k - RING + 1)
                dve.tensor_copy(probs_t[:, k % RING, 0:width(k // HEADS)],
                                probs_t_bank[k % 2][:, 0:width(k // HEADS)]).then_inc(copied_vector, 1)

            def null_arguments(n, g):
                b, hs = n.c % BATCH, slice(GROUP * g, GROUP * (g + 1))
                dve.wait_ge(logits_ready, n.count(HEADS, GROUP * (g + 1)))
                dve.tensor_tensor(null_arg[:, b, hs], neg_null[:, b, hs], neg_max[:, b, hs], ALU.subtract
                                  ).then_inc(null_arg_ready, 1)

            def normalize_group(n, g):
                b, hs = n.c % BATCH, slice(GROUP * g, GROUP * (g + 1))
                av = av_bank[g % 2][:, 0:GROUP * VW].rearrange("p (h c) -> p h c", h=GROUP)
                dve.wait_ge(null_p_ready, n.count(GROUPS, g + 1))
                dve.wait_ge(av_ready, n.count(HEADS, GROUP * (g + 1)))
                link(dve.tensor_tensor(denom[:, hs], av[:, :, DH], null_p[:, b, hs], ALU.add))
                link(dve.reciprocal(r_denom[:, hs], denom[:, hs]))
                if n.c >= 1:
                    dve.wait_ge(o_t_ps, n.count(3, 0))
                dve.tensor_tensor(null_w[:, hs], null_p[:, b, hs], r_denom[:, hs], ALU.mult)
                dve.tensor_tensor(o_n[:, hs, :], av[:, :, 0:DH],
                                  r_denom[:, hs].unsqueeze(2).to_broadcast([P, GROUP, DH]), ALU.mult
                                  ).then_inc(group_ready, 1)

            def null_weights_t(n):
                dve.wait_ge(o_t_ps, n.count(3, 3))
                dve.tensor_copy(null_wt[:], misc[0][0:HEADS, 0:P]).then_inc(null_wt_sb, 1)

            def output_stats(n):
                dve.wait_ge(y_ps, n.count(1, 1))
                dve.tensor_copy(y_sb[:], misc[0][:, P:P + DIM]).then_inc(y_sb_ready, 1)
                dve.wait_ge(y_sb_ready, n.count(1, 1))
                link(dve.bn_stats(y_stats[:], y_sb[:]), apart=True)
                link(dve.bn_aggr(y_mv[:], y_stats[:]))
                dve.tensor_scalar(y_var[:], y_mv[:, 1:2], EPS, None, ALU.add).then_inc(y_var_ready, 1)

            def add_output(n, layer):
                dve.wait_ge(y_rstd_ready, n.count(1, 1))
                link(dve.tensor_scalar(y_c[:], y_sb[:], y_mv[:, 0:1], y_rstd[:], ALU.subtract, ALU.mult))
                link(dve.tensor_tensor(y_c[:], y_c[:], pick(g_out, layer), ALU.mult))
                dve.tensor_tensor(x_res[:, n.c, :], x_res[:, n.c, :], y_c[:], ALU.add).then_inc(x_ready, 1)

            first = Step(None, 0)
            input_stats(first)
            input_norm(first)
            keys_values(first)
            query_squares(first, 0)
            query_squares(first, 1)
            input_stats(Step(None, 1))
            split_keys(first, 0)
            input_norm(Step(None, 1))
            null_scores(first, 0)
            keys_t(first)

            before_loop = links[0]
            with dve.Fori(0, LAYERS) as layer:
                base[0], links[0] = layer * (STEPS * LINKS_STEP) + before_loop, 0
                dve.wait_ge(x_ready, Step(layer, 0).count(1, STEPS))
                dve.wait_ge(mask_made, LAYERS)
                dve.tensor_copy(mask_cur[:], pick(mask_all, layer)).then_inc(mask_ready, 1)
                for s in range(STEPS):
                    m, ml = Step(layer, s + 1), layer + (s + 1) // STEPS
                    before = Step(layer, s - 1)
                    for h in range(HEADS):
                        k = s * HEADS + h
                        unit_logits(layer, k)
                        if k >= T_LAG and on_vector(k - T_LAG):
                            copy_probs(layer, k - T_LAG)
                        if h % GROUP == GROUP - 1:
                            null_arguments(Step(layer, s), h // GROUP)
                        if h % GROUP == 1 and k >= 2 * GROUP:
                            done = k - 2 * GROUP
                            normalize_group(Step(layer, done // HEADS), done % HEADS // GROUP)
                        if h == 2:
                            keys_values(m)
                        if h == 4:
                            query_squares(m, 0)
                        if h == 6:
                            query_squares(m, 1)
                        if h == 8:
                            split_keys(m, ml)
                        if h == 9 and s >= 1:
                            null_weights_t(before)
                        if h == 11:
                            keys_t(m)
                        if h == 12 and s >= 1:
                            output_stats(before)
                        if h == 13:
                            input_stats(Step(layer, s + 2))
                        if h == 14:
                            null_scores(m, ml)
                        if h == 15:
                            if s >= 1:
                                add_output(before, layer)
                            input_norm(Step(layer, s + 2))
                for k in range(UNITS - T_LAG, UNITS):
                    if on_vector(k):
                        copy_probs(layer, k)
                last = Step(layer, STEPS - 1)
                normalize_group(last, GROUPS - 2)
                normalize_group(last, GROUPS - 1)
                null_weights_t(last)
                output_stats(last)
                add_output(last, layer)
                assert links[0] == STEPS * LINKS_STEP, links

        @block.tensor
        def _(pe):
            def mm(to, stationary, moving, start=True, stop=True):
                return pe.matmul(to, stationary, moving, start=start, stop=stop, skip_group_check=True)

            pe.wait_ge(consts_in, 64)
            pe.wait_ge(x_in, 32)
            for s in range(STEPS):
                ins = pe.transpose(bank[s // 4][:, P * (s % 4):P * (s % 4 + 1)], x_res[:, s, :], ident[:])
                if s % 4 == 3:
                    ins.then_inc(x_t_ps, 1)
            pe.wait_ge(x_t_sb, 2)
            pe.wait_ge(route_in, 48)
            pe.wait_ge(g_rep_made, 1)
            for s in range(STEPS):
                to = bank[2][:, EXPERTS * s:EXPERTS * (s + 1)]
                mm(to, tokens_t[:, P * s:P * (s + 1)], w_t[:], stop=False)
                ins = mm(to, g_rep[:, s % BATCH, :], w_g[:], start=False)
            ins.then_inc(router_ps, 1)
            pe.wait_ge(expert_in, 96)

            def gate_up(j):
                half, c = divmod(j, CHUNKS)
                if j == 0:
                    pe.wait_ge(router_arg, 1)
                if j >= 2:
                    pe.wait_ge(hidden_made, j - 1)
                moving = tokens_t[:, 512 * half:512 * (half + 1)]
                mm(bank[2 + j % 2][:], w_gate[:, c, :], moving)
                mm(bank[4 + j % 2][:], w_up[:, c, :], moving).then_inc(up_ps, 1)

            def coefficients_t():
                pe.wait_ge(coef_made, 1)
                for s in range(STEPS):
                    ins = pe.transpose(bank[6 + s // 4][0:EXPERTS, P * (s % 4):P * (s % 4 + 1)],
                                       route[:, 2, s, :], ident[:])
                    if s % 4 == 3:
                        ins.then_inc(coef_t_ps, 1)

            gate_up(0)
            gate_up(1)
            coefficients_t()
            for j in range(2, 2 * CHUNKS):
                gate_up(j)
            pe.wait_ge(coef_t_sb, 2)
            for j in range(2 * PAIRS):
                half, c = divmod(j, PAIRS)
                if j >= 2:
                    pe.wait_ge(hidden_ready, j - 1)
                mm(bank[j % 2][:], pair_sel[:, P * c:P * (c + 1)], coef_t[:, 512 * half:512 * (half + 1)]
                   ).then_inc(spread_ps, 1)

            def positions_t(stage):
                for i in range(4):
                    pe.wait_ge(m_norm_ready, STEPS * stage + 2 * i + 2)
                    if i >= 2:
                        pe.wait_ge(m_t_sb, 4 * stage + i - 1)
                    elif stage == 0:
                        pe.wait_ge(hidden_made, 2 * CHUNKS)
                    for j in range(2):
                        ins = pe.transpose(bank[4 + i % 2][:, P * j:P * (j + 1)], m_h[:, 2 * i + j, :],
                                           ident[:])
                    ins.then_inc(m_t_ps, 1)

            pe.wait_ge(mlp_in, 16 * 16)
            positions_t(0)
            for i in range(4):
                pe.wait_ge(m_t_sb, i + 1)
                if i >= 2:
                    pe.wait_ge(m_h_sb, i - 1)
                else:
                    pe.wait_ge(coef_t_sb, 2)
                for j in range(2):
                    ins = mm(bank[6 + i % 2][:, P * j:P * (j + 1)], m_act[:, 2 * i + j, :], m_w1[:, i // 2, :])
                ins.then_inc(m_h_ps, 1)
            pe.wait_ge(attn_in, ATTN_LOADS)
            pe.wait_ge(null_cols_made, 1)
            for l in range(LAYERS):
                for c in range(STEPS):
                    ins = mm(bank[2][0:HEADS, DIM * l:DIM * (l + 1)], null_v_cols[:, HEADS * c:HEADS * (c + 1)],
                             w_o[:, l, DIM * c:DIM * (c + 1)], start=(c == 0), stop=(c == STEPS - 1))
            ins.then_inc(null_out_ps, 1)
            pe.wait_ge(hidden_ready, 2 * PAIRS)
            pe.wait_ge(m_h_sb, 4)
            for s in range(STEPS):
                if s >= 2:
                    pe.wait_ge(x_ready, s - 1)
                for c in range(CHUNKS):
                    ins = mm(bank[6 + s % 2][:, 0:DIM], hidden[c][:, P * s:P * (s + 1)], w_down[:, c, :],
                             start=(c == 0), stop=(c == CHUNKS - 1))
                ins.then_inc(moe_ps, 1)
            positions_t(1)
            for l in range(2):
                pe.wait_ge(m_t_sb, 4 + 2 * l + 2)
                mm(bank[l][0:HEADS, :], m_w2[:, l, :],
                   m_act[:, ROWS * l:ROWS * (l + 1), :].rearrange("p s c -> p (s c)")).then_inc(m_out_ps, 1)

            def input_t(m):
                pe.wait_ge(xn_ready, m.count(1, 1))
                if m.layer is not None:
                    pe.wait_ge(q_ready, m.count(GROUPS, 0))
                pe.transpose(misc[0][:, 0:P], xn[:], ident[:]).then_inc(xn_t_ps, 1)

            def project_kvn(m, layer):
                pe.wait_ge(xn_t_sb, m.count(1, 1))
                mm(misc[1][:, 0:PROJ], xn_t[:], pick(w_kvn, layer)).then_inc(kvn_ps, 1)

            def project_q(m, layer, half):
                if half == 1:
                    pe.wait_ge(kvn_sb, m.count(1, 1))
                mm(misc[half][:], xn_t[:], pick(w_q, layer)[:, 512 * half:512 * (half + 1)]
                   ).then_inc(q_ps, 1)

            def keys_t(m, before):
                pe.wait_ge(k_split_ready, m.count(1, 1))
                if before is None:
                    pe.wait_ge(q_sq_sb, m.count(2, 2))
                else:
                    pe.wait_ge(o_t_sb, before.count(2, 2))
                for i in range(2):
                    ins = mm(misc[1][:, P * i:P * (i + 1)], k_split[:, i].rearrange("p i d -> p (i d)"),
                             ident_r[:])
                ins.then_inc(k_t_ps, 1)

            def queries_t(m, g, before):
                pe.wait_ge(q_low, m.count(2, g // 2 + 1))
                if g >= 2:
                    pe.wait_ge(q_ready, m.count(GROUPS, g - 1))
                elif g == 1:
                    pe.wait_ge(keys_ready, m.count(1, 1))
                elif before is None:
                    pe.wait_ge(q_sq_sb, m.count(2, 1))
                else:
                    pe.wait_ge(y_sb_ready, before.count(1, 1))
                for i in range(GROUP):
                    ins = mm(misc[g % 2][:, P * i:P * (i + 1)],
                             q_split[:, GROUP * g + i].rearrange("p i d -> p (i d)"), ident_r[:])
                ins.then_inc(q_t_ps, 1)

            def scores(layer, k):
                s, h = divmod(k, HEADS)
                n, b, w = Step(layer, s), s % BATCH, width(s)
                if h == 0:
                    pe.wait_ge(keys_ready, n.count(1, 1))
                if h % GROUP == 0:
                    pe.wait_ge(q_ready, n.count(GROUPS, h // GROUP + 1))
                if k == 0:
                    pe.wait_ge(mask_ready, layer + 1)
                if k >= 2:
                    pe.wait_ge(logits_ready, layer * UNITS + k - 1)
                to = scores_ps[k % 2][:, 0:w]
                mm(to, first_row[:], mask_cur[:, SEQ * b:SEQ * b + w], stop=False)
                mm(to, q_stack[:, b, h, :], keys[:, b, 0, 0:w], start=False, stop=False)
                mm(to, q_stack[:, b, h, :], keys[:, b, 1, 0:w], start=False).then_inc(scores_ready, 1)

            def probs_transposed(layer, k):
                pe.wait_ge(probs_ready, layer * UNITS + k + 1)
                if k >= 2:
                    wait_copied(pe, layer, k - 2)
                for c in range(width(k // HEADS) // P):
                    ins = pe.transpose(probs_t_bank[k % 2][:, P * c:P * (c + 1)],
                                       probs[:, k % RING, P * c:P * (c + 1)], ident[:])
                ins.then_inc(probs_t_ready, 1)

            def times_values(layer, k):
                s, h = divmod(k, HEADS)
                wait_copied(pe, layer, k)
                if h % GROUP == 0 and k >= 2 * GROUP:
                    pe.wait_ge(group_ready, layer * (STEPS * GROUPS) + k // GROUP - 1)
                to = av_bank[h // GROUP % 2][:, VW * (h % GROUP):VW * (h % GROUP + 1)]
                blocks = width(s) // P
                for c in range(blocks):
                    ins = mm(to, probs_t[:, k % RING, P * c:P * (c + 1)], values[:, s % BATCH, c, :],
                             start=(c == 0), stop=(c == blocks - 1))
                ins.then_inc(av_ready, 1)

            def outputs_t(n, i):
                pe.wait_ge(group_ready, n.count(GROUPS, 2 * i + 2))
                if n.c == STEPS - 1:
                    pe.wait_ge(q_ready, n.count(GROUPS, 2 * GROUPS))
                else:
                    pe.wait_ge(q_sq_sb, Step(n.layer, n.c + 2).count(2, i + 1))
                for c in range(4):
                    two = o_n[:, 2 * (4 * i + c):2 * (4 * i + c) + 2, :].rearrange("p h d -> p (h d)")
                    ins = pe.transpose(misc[i][:, P * c:P * (c + 1)], two, ident[:])
                ins.then_inc(o_t_ps, 1)

            def null_weights_t(n):
                pe.wait_ge(o_t_sb, n.count(2, 1))
                pe.transpose(misc[0][0:HEADS, 0:P], null_w[:], ident[:]).then_inc(o_t_ps, 1)

            def project_output(n, layer):
                pe.wait_ge(o_t_sb, n.count(2, 2))
                pe.wait_ge(null_wt_sb, n.count(1, 1))
                to, w = misc[0][:, P:P + DIM], pick(w_o, layer)
                for c in range(STEPS):
                    mm(to, o_t[:, c, :], w[:, DIM * c:DIM * (c + 1)], start=(c == 0), stop=False)
                mm(to, null_wt[:], pick(null_out, layer), start=False).then_inc(y_ps, 1)

            first = Step(None, 0)
            pe.wait_ge(tables_made, 1)
            pe.wait_ge(x_ready, STEPS)
            input_t(first)
            project_kvn(first, 0)
            for half in range(2):
                project_q(first, 0, half)
            keys_t(first, None)
            for g in range(GROUPS):
                queries_t(first, g, None)
            pe.wait_ge(m_out_sb, 2)
            pe.wait_ge(first_row_made, 1)
            with pe.Fori(0, LAYERS) as layer:
                for s in range(STEPS):
                    m, ml = Step(layer, s + 1), layer + (s + 1) // STEPS
                    before = Step(layer, s - 1) if s >= 1 else None
                    for h in range(HEADS):
                        k = s * HEADS + h
                        scores(layer, k)
                        if k >= T_LAG:
                            probs_transposed(layer, k - T_LAG)
                        if k >= AV_LAG:
                            times_values(layer, k - AV_LAG)
                        if h == 0:
                            input_t(m)
                        if h == 1:
                            project_kvn(m, ml)
                        if h == 2:
                            project_q(m, ml, 0)
                        if h == 4:
                            project_q(m, ml, 1)
                        if before is not None:
                            if h == 6:
                                outputs_t(before, 0)
                            if h == 7:
                                outputs_t(before, 1)
                            if h == 8:
                                null_weights_t(before)
                            if h == 10:
                                project_output(before, layer)
                        if h == 10:
                            keys_t(m, before)
                        if h >= HEADS - GROUPS:
                            queries_t(m, h - (HEADS - GROUPS), before)
                for k in range(UNITS - T_LAG, UNITS):
                    probs_transposed(layer, k)
                for k in range(UNITS - AV_LAG, UNITS):
                    times_values(layer, k)
                last = Step(layer, STEPS - 1)
                outputs_t(last, 0)
                outputs_t(last, 1)
                null_weights_t(last)
                project_output(last, layer)


def kernel(**inputs):
    import numpy as np
    import concourse.bacc as bacc
    from concourse.bass_utils import run_bass_kernel_spmd

    a = {name: np.asarray(v) for name, v in inputs.items()}
    L0 = {n: a["L0_cond_" + n] for n in (
        "wt", "wg", "w_gate", "w_up", "w_down", "sw_gate", "sw_up", "sw_down")}

    def stacked(*names):
        return np.stack([a[n] for n in names])

    def later(name):
        return stacked(f"L2_cond_{name}", f"L3_cond_{name}")

    given = {
        "x": a["x"], "cond": a["cond_64"], "cond_t": a["cond_64"].T, "attn_bias": a["fside_16xSxS_0"],
        "mask0": a["mask_BxS_bk0"].reshape(-1), "mask1": a["mask_BxS_bf1"].reshape(-1),
        "wt_t": L0["wt"].T, "wg_t": L0["wg"].T,
        "w_gate": L0["w_gate"], "w_up": L0["w_up"], "w_down": L0["w_down"],
        "sw_gate": L0["sw_gate"], "sw_up": L0["sw_up"], "sw_down": L0["sw_down"],
        "g_in": stacked("L1_cond_g_in", "L2_cond_g_norm", "L3_cond_g_norm"),
        "g_out": stacked("L1_cond_g_out", "L2_cond_g_out", "L3_cond_g_out"),
        "null_bias": stacked("L1_cond_null_attn_bias", "L2_cond_null_attn_bias", "L3_cond_null_attn_bias"),
        "w_q": stacked("L1_cond_Wq", "L2_cond_Wq", "L3_cond_Wq"),
        "w_kv": stacked("L1_cond_Wkv", "L2_cond_Wkv", "L3_cond_Wkv"),
        "w_o": stacked("L1_cond_Wo", "L2_cond_Wout", "L3_cond_Wout"),
        "q_scale": later("q_scale"), "k_scale": later("k_scale"),
        "w0": later("w0").reshape(2, DIM), "b0": later("b0"), "g0": later("g0"), "w1": later("w1"),
        "b1": later("b1"), "g1": later("g1"), "w2": later("w2"), "b2": later("b2"),
        "ident": np.eye(P, dtype=np.float32),
        "pos": (SEQ - 1 - np.arange(SEQ)).reshape(ROWS, P).T.astype(np.float32),
        "pair_sel": np.repeat(np.eye(EXPERTS, dtype=np.float32), MID, axis=1),
        "rank8": np.arange(EXPERTS, 0, -1).astype(np.float32),
    }
    nc = bacc.Bacc("TRN2", target_bir_lowering=False, num_devices=1)
    arrays, handles = {}, {}
    for name, array in given.items():
        arrays["in_" + name] = np.ascontiguousarray(array)
        handles[name] = nc.dram_tensor("in_" + name, array.shape, mybir.dt.from_np(array.dtype),
                                       kind="ExternalInput").ap()
    out = nc.dram_tensor("out_x", (BATCH, SEQ, DIM), F32, kind="ExternalOutput").ap()
    build(nc, handles, out)
    return run_bass_kernel_spmd(nc, [arrays], core_ids=[0]).results[0]["out_x"]
```

```python
from contextlib import ExitStack

import concourse.bass as bass
from concourse import mybir

F32 = mybir.dt.float32
F32R = mybir.dt.float32r
BF16 = mybir.dt.bfloat16
U8 = mybir.dt.uint8
ALU = mybir.AluOpType
ACT = mybir.ActivationFunctionType
AX_X = mybir.AxisListType.X

P = 128
BATCH = 2
SEQ = 512
DIM = 128
ROWS = SEQ // P
STEPS = ROWS * BATCH
LAYERS = 3
HEADS = 16
DH = 64
INNER = HEADS * DH
VW = DH + 1
GROUP = 4
GROUPS = HEADS // GROUP
HALF = HEADS // 2
UNITS = STEPS * HEADS
KV = 2 * DH
PROJ = KV + HEADS
EXPERTS = 8
MID = 64
PAIRS = EXPERTS // 2
CHUNKS = PAIRS + 1
GDIM = 64
BIG = 1e30
EPS = 1e-5
NORM_FLOOR = 1e-24
Q_SCALE = 8.0
BIAS_ROW = SEQ + P
BEFORE_LOOP = 2
RING = 4
T_LAG = 2
AV_LAG = 4
POOL_CONSTS = 8
ATTN_LOADS = 16 * 11
MLP_LOADS = 16 * 7



class Step:

    def __init__(self, layer, c):
        self.layer, self.c = layer, c

    def count(self, per_step, k):
        own = self.c * per_step + k
        return own if self.layer is None else self.layer * (STEPS * per_step) + own

    def of_layer(self):
        return (0 if self.layer is None else self.layer) + self.c // STEPS

    def exists(self):
        return not isinstance(self.layer, int) or self.layer * STEPS + self.c < LAYERS * STEPS


def on_vector(k):
    return k % 4 == 3


def copied_by(vector, k):
    return sum(on_vector(i) == vector for i in range(k + 1))


def width(step):
    return P * (step % STEPS // BATCH + 1)


def pick(table, layer):
    n = table.shape[2]
    flat = table[:].rearrange("p l n -> p (l n)")
    return flat[:, layer * n:(layer + 1) * n] if isinstance(layer, int) else flat[:, bass.ds(layer * n, n)]


LINKS_LAYER = STEPS * (2 + 2 + 2 + 2 + 1 + 2 * GROUPS + 4)


def build(nc, d, out):
    with ExitStack() as ctx:
        def sb(name, shape, dt=F32):
            return ctx.enter_context(nc.sbuf_tensor(name, shape, dt))

        def sem(name):
            return ctx.enter_context(nc.semaphore(name))

        def rows(vector):
            return vector.unsqueeze(0).to_broadcast([P, vector.shape[0]])

        def column(vector):
            return vector.unsqueeze(1)

        ident = sb("ident", [P, P])
        ident_r = sb("ident_r", [P, P], F32R)
        w_q = sb("w_q", [P, LAYERS, INNER])
        w_kvn = sb("w_kvn", [P, LAYERS, PROJ])
        w_o = sb("w_o", [P, LAYERS, STEPS * DIM])
        g_in = sb("g_in", [P, LAYERS, 1])
        g_out = sb("g_out", [P, LAYERS, DIM])
        null_bias = sb("null_bias", [P, LAYERS, HEADS])
        k_factor = sb("k_factor", [P, LAYERS, DH])
        norm_power = sb("norm_power", [P, LAYERS, HEADS + 1])
        rsqrt_power = sb("rsqrt_power", [P, STEPS])
        qk_scales = sb("qk_scales", [P, 2, 2, DH])
        null_k = sb("null_k", [P, DH])
        null_kl = sb("null_kl", [P, LAYERS, DH])
        null_r = sb("null_r", [P, LAYERS])
        null_v = sb("null_v", [P, 1])
        null_v_cols = sb("null_v_cols", [P, STEPS * HEADS])
        null_out = sb("null_out", [HEADS, LAYERS, DIM])
        mask_u8 = sb("mask_u8", [P, 2, BATCH * SEQ], U8)
        mask_all = sb("mask_all", [P, LAYERS, BATCH * SEQ], BF16)
        first_row = sb("first_row", [P, P], BF16)

        x_res = sb("x_res", [P, STEPS, DIM])
        bias = sb("bias", [P, 2, HEADS, SEQ])
        keys = sb("keys", [P, BATCH, 2, SEQ], F32R)
        values = sb("values", [P, BATCH, ROWS, VW])
        q_stack = sb("q_stack", [P, BATCH, HEADS, P], F32R)
        stats = sb("stats", [P, 6])
        mv = sb("mv", [P, 2])
        var_eps = sb("var_eps", [P, 1])
        rstd = sb("rstd", [P, 1])
        xn = sb("xn", [P, DIM])
        xn_t = sb("xn_t", [P, P])
        kvn = sb("kvn", [P, PROJ])
        q_raw = sb("q_raw", [P, HEADS, DH])
        q_sq = sb("q_sq", [P, HALF, DH])
        k_sq = sb("k_sq", [P, DH])
        sumsq = sb("sumsq", [P, HEADS + 1])
        r_norm = sb("r_norm", [P, HEADS + 1])
        q_n = sb("q_n", [P, HEADS, DH])
        q_split = sb("q_split", [P, HEADS, 2, DH], F32R)
        k_n = sb("k_n", [P, DH])
        k_split = sb("k_split", [P, 2, 2, DH], F32R)
        null_t = sb("null_t", [P, HEADS])
        neg_null = sb("neg_null", [P, BATCH, HEADS])
        neg_logits = sb("neg_logits", [P, RING, SEQ])
        probs = sb("probs", [P, RING, SEQ])
        probs_t = sb("probs_t", [P, RING, SEQ])
        neg_max = sb("neg_max", [P, BATCH, HEADS])
        null_arg = sb("null_arg", [P, BATCH, HEADS])
        null_p = sb("null_p", [P, BATCH, HEADS])
        denom = sb("denom", [P, HEADS])
        r_denom = sb("r_denom", [P, HEADS])
        null_w = sb("null_w", [P, HEADS])
        o_n = sb("o_n", [P, HEADS, DH])
        o_t = sb("o_t", [P, STEPS, P])
        null_wt = sb("null_wt", [HEADS, P])
        y_sb = sb("y_sb", [P, DIM])
        y_stats = sb("y_stats", [P, 6])
        y_mv = sb("y_mv", [P, 2])
        y_var = sb("y_var", [P, 1])
        y_rstd = sb("y_rstd", [P, 1])
        y_c = sb("y_c", [P, DIM])
        spare = sb("spare", [1, 3, 16])

        rank8 = sb("rank8", [P, EXPERTS])
        w_t = sb("w_t", [P, EXPERTS])
        w_g = sb("w_g", [GDIM, EXPERTS])
        g_col = sb("g_col", [GDIM, BATCH])
        g_rep = sb("g_rep", [GDIM, BATCH, P])
        route = sb("route", [P, 4, STEPS, EXPERTS])
        best = sb("best", [P, 4, STEPS])
        pos = sb("pos", [P, ROWS])
        m_cols = sb("m_cols", [P, 4])
        m_w2 = sb("m_w2", [P, 2, HEADS])
        m_b2 = sb("m_b2", [HEADS, 2])
        m_stats = sb("m_stats", [P, STEPS, 6])
        m_mv = sb("m_mv", [P, STEPS, 2])
        m_var = sb("m_var", [P, STEPS])
        m_rstd = sb("m_rstd", [P, STEPS])
        m_bias = sb("m_bias", [HEADS, 2, BIAS_ROW])
        scratch = bias[:, 1].rearrange("p h c -> p (h c)")
        tokens_t = scratch[:, 0:1024]
        leak = scratch[:, 1024:2048].rearrange("p (i c) -> p i c", i=2)
        gated = scratch[:, 2048:2560]
        m_h = scratch[:, 2560:3584].rearrange("p (s c) -> p s c", s=STEPS)
        m_act = scratch[:, 3584:4608].rearrange("p (s c) -> p s c", s=STEPS)
        w_gate, w_up, w_down = (scratch[:, 4608 + 640 * i:5248 + 640 * i].rearrange("p (k c) -> p k c", k=CHUNKS)
                                for i in range(3))
        m_rows = scratch[:, 6528:7296].rearrange("p (i l c) -> p i l c", l=2, i=3)
        m_w1 = scratch[:, 7296:7552].rearrange("p (l c) -> p l c", l=2)
        pair_sel = scratch[0:EXPERTS, 7552:8064]
        hidden = [a[:].rearrange("p r c -> p (r c)")[:, 0:STEPS * P] for a in (neg_logits, probs, probs_t)]
        hidden += [a[:].rearrange("p r c -> p (r c)")[:, STEPS * P:2 * STEPS * P] for a in (neg_logits, probs)]
        null_prod = (q_n, q_raw, o_n)
        coef_t = o_t[0:EXPERTS].rearrange("e s c -> e (s c)")
        rel_bias = nc.dram_tensor("rel_bias", [2, HEADS, P, SEQ], F32, kind="Internal").ap()

        bank = [ctx.enter_context(nc.psum_tensor(f"bank{i}", [P, 512], F32)) for i in range(8)]
        scores_ps, probs_t_bank, av_bank, misc = bank[0:2], bank[2:4], bank[4:6], bank[6:8]

        ident_in, x_in, consts_in, route_in, expert_in, mlp_in = (sem(n) for n in (
            "ident_in", "x_in", "consts_in", "route_in", "expert_in", "mlp_in"))
        attn_in, mask_in, rel_bias_out, out_done = (sem(n) for n in (
            "attn_in", "mask_in", "rel_bias_out", "out_done"))
        bias_in = [sem("bias_in0"), sem("bias_in1")]
        pool_consts, first_row_made, tables_made, mask_made = (sem(n) for n in (
            "pool_consts", "first_row_made", "tables_made", "mask_made"))
        x_t_ps, x_t_sb, g_rep_made, router_ps, router_arg, router_exp = (sem(n) for n in (
            "x_t_ps", "x_t_sb", "g_rep_made", "router_ps", "router_arg", "router_exp"))
        coef_made, coef_t_ps, coef_t_sb, up_ps, leak_sb = (sem(n) for n in (
            "coef_made", "coef_t_ps", "coef_t_sb", "up_ps", "leak_sb"))
        hidden_made, spread_ps, hidden_ready, moe_ps = (sem(n) for n in (
            "hidden_made", "spread_ps", "hidden_ready", "moe_ps"))
        null_sq_made, null_r_made, null_kl_made, null_prod_made = (sem(n) for n in (
            "null_sq_made", "null_r_made", "null_kl_made", "null_prod_made"))
        null_cols_made, null_out_ps, null_out_sb = (sem(n) for n in (
            "null_cols_made", "null_out_ps", "null_out_sb"))
        m_var_ready, m_rstd_ready, m_norm_ready, m_t_ps, m_t_sb = (sem(n) for n in (
            "m_var_ready", "m_rstd_ready", "m_norm_ready", "m_t_ps", "m_t_sb"))
        m_h_ps, m_h_sb, m_out_ps, m_out_sb = (sem(n) for n in ("m_h_ps", "m_h_sb", "m_out_ps", "m_out_sb"))
        var_ready, rstd_ready, xn_ready, xn_t_ps, xn_t_sb = (sem(n) for n in (
            "var_ready", "rstd_ready", "xn_ready", "xn_t_ps", "xn_t_sb"))
        kvn_ps, kvn_sb, q_ps, q_sq_sb, sumsq_ready = (sem(n) for n in (
            "kvn_ps", "kvn_sb", "q_ps", "q_sq_sb", "sumsq_ready"))
        norm_ready, q_scaled, q_high, q_low, k_split_ready = (sem(n) for n in (
            "norm_ready", "q_scaled", "q_high", "q_low", "k_split_ready"))
        k_t_ps, keys_ready, q_t_ps, q_ready, null_ready = (sem(n) for n in (
            "k_t_ps", "keys_ready", "q_t_ps", "q_ready", "null_ready"))
        bias_ready, scores_ready, logits_ready, probs_ready = (sem(n) for n in (
            "bias_ready", "scores_ready", "logits_ready", "probs_ready"))
        probs_t_ready, copied_scalar, copied_vector, av_ready = (sem(n) for n in (
            "probs_t_ready", "copied_scalar", "copied_vector", "av_ready"))
        null_arg_ready, null_p_ready, group_ready, o_t_ps, o_t_sb = (sem(n) for n in (
            "null_arg_ready", "null_p_ready", "group_ready", "o_t_ps", "o_t_sb"))
        null_wt_sb, y_ps, y_sb_ready, y_var_ready, y_rstd_ready = (sem(n) for n in (
            "null_wt_sb", "y_ps", "y_sb_ready", "y_var_ready", "y_rstd_ready"))
        x_ready, vector_link = sem("x_ready"), sem("vector_link")

        def wait_copied(eng, layer, k):
            v = on_vector(k)
            eng.wait_ge(copied_vector if v else copied_scalar,
                        layer * copied_by(v, UNITS - 1) + copied_by(v, k))

        def wait_apart(eng):
            calls = apart_calls.setdefault(eng.engine, [0])
            calls[0] += 1
            column = calls[0] % spare.shape[2]
            if eng is nc.vector:
                eng.memset(spare[0:1, 0, column:column + 1], 0.0)
            elif eng is nc.gpsimd:
                eng.tensor_tensor(spare[0:1, 1, column:column + 1], rsqrt_power[0:1, 0:1], rsqrt_power[0:1, 0:1], ALU.add)
            else:
                eng.copy(spare[0:1, 2, column:column + 1], ident[0:1, 0:1])

        apart_calls = {}
        block = ctx.enter_context(nc.Block())

        @block.sync
        def _(sp):
            sp.dma_start(ident[:], d["ident"]).then_inc(ident_in, 16)
            for b in range(BATCH):
                sp.dma_start(x_res[:].rearrange("p (r b) c -> p r b c", b=BATCH)[:, :, b, :],
                             d["x"][b].rearrange("(r p) c -> p r c", p=P)).then_inc(x_in, 16)
            for to, name in ((w_t, "wt_t"), (w_g, "wg_t"), (g_col, "cond_t")):
                sp.dma_start(to[:], d[name]).then_inc(route_in, 16)
            for to, name in ((pos, "pos"), (pair_sel, "pair_sel")):
                sp.dma_start(to[:], d[name]).then_inc(consts_in, 16)
            sp.dma_start(rank8[:], rows(d["rank8"])).then_inc(consts_in, 16)
            for to, routed, shared in ((w_gate, "w_gate", "sw_gate"), (w_up, "w_up", "sw_up")):
                sp.dma_start(to[:, 0:PAIRS, :].rearrange("h k (e m) -> h (k e) m", e=2),
                             d[routed].rearrange("e h m -> h e m")).then_inc(expert_in, 16)
                sp.dma_start(to[:, PAIRS, :], d[shared]).then_inc(expert_in, 16)
            sp.dma_start(w_down[:, 0:PAIRS, :],
                         d["w_down"].rearrange("(k e) m h -> (e m) k h", e=2)).then_inc(expert_in, 16)
            sp.dma_start(w_down[:, PAIRS, :], d["sw_down"]).then_inc(expert_in, 16)
            for b in range(2):
                sp.dma_start(null_v[b * DH:(b + 1) * DH, :], column(d["cond"][1])).then_inc(attn_in, 16)
            sp.dma_start(null_k[:], rows(d["cond"][0])).then_inc(attn_in, 16)
            sp.dma_start(w_q[:], d["w_q"].rearrange("l c n -> c l n")).then_inc(attn_in, 16)
            sp.dma_start(w_kvn[:, :, 0:KV], d["w_kv"].rearrange("l c n -> c l n")).then_inc(attn_in, 16)
            sp.dma_start(w_o[:].rearrange("p l (k n) -> p (l k) n", n=DIM),
                         d["w_o"].rearrange("l (k p) n -> p (l k) n", p=P)).then_inc(attn_in, 16)
            sp.dma_start(g_in[:, :, 0], d["g_in_t"]).then_inc(attn_in, 16)
            for to, name in ((null_bias, "null_bias"), (g_out, "g_out")):
                sp.dma_start(to[:].rearrange("p l n -> p (l n)"), rows(d[name])).then_inc(attn_in, 16)
            sp.dma_start(qk_scales[:, :, 0, :].rearrange("p l d -> p l d"),
                         rows(d["q_scale"]).rearrange("p (l d) -> p l d", l=2)).then_inc(attn_in, 16)
            sp.dma_start(qk_scales[:, :, 1, :], rows(d["k_scale"]).rearrange("p (l d) -> p l d", l=2)
                         ).then_inc(attn_in, 16)
            sp.dma_start(mask_u8[:].rearrange("p i c -> p (i c)"), rows(d["masks"])).then_inc(mask_in, 16)
            for t in range(ROWS):
                if t == 1:
                    sp.wait_ge(x_ready, STEPS)
                    sp.wait_ge(m_out_sb, 2)
                    for l in range(2):
                        skewed = bass.AP(m_bias, l * BIAS_ROW + P - 1, [[2 * BIAS_ROW, HEADS], [-1, P], [1, SEQ]])
                        sp.dma_start(rel_bias[l], skewed).then_inc(rel_bias_out, 16)
                if t >= 2:
                    sp.wait_ge(logits_ready, HEADS * BATCH * (t - 1))
                w = P * (t + 1)
                sp.dma_start(bias[:, t % 2, :, 0:w],
                             d["attn_bias"][:, P * t:P * (t + 1), 0:w].rearrange("h p c -> p h c")
                             ).then_inc(bias_in[t % 2], 16)
            sp.wait_ge(rel_bias_out, 32)
            for layer in range(1, LAYERS):
                for t in range(ROWS):
                    sp.wait_ge(logits_ready, UNITS * layer + HEADS * BATCH * (t - 1))
                    w = P * (t + 1)
                    sp.dma_start(bias[:, t % 2, :, 0:w],
                                 rel_bias[layer - 1, :, :, SEQ - w:SEQ].rearrange("h p c -> p h c")
                                 ).then_inc(bias_in[t % 2], 16)
            for s in range(STEPS):
                sp.wait_ge(x_ready, STEPS * LAYERS + s + 1)
                sp.dma_start(out[s % BATCH, (s // BATCH) * P:(s // BATCH + 1) * P, :], x_res[:, s, :]
                             ).then_inc(out_done, 16)
            sp.wait_ge(out_done, 16 * STEPS)

        @block.gpsimd
        def _(pool):
            for to, value in ((rsqrt_power[:], -0.5), (norm_power[:, 1:3, :], -0.5), (norm_power[:, 0, :], 0.0),
                              (k_factor[:, 0, :], DH ** -0.5), (first_row[:], 0.0), (null_v_cols[:], 0.0),
                              (values[:], 1.0), (m_bias[:], 0.0)):
                pool.memset(to, value).then_inc(pool_consts, 1)
            pool.wait_ge(pool_consts, POOL_CONSTS)
            pool.memset(first_row[0:1, :], 1.0).then_inc(first_row_made, 1)

            def normalize_positions(stage):
                pool.wait_ge(m_var_ready, stage + 1)
                pool.tensor_tensor(m_rstd[:], m_var[:], rsqrt_power[:], ALU.pow).then_inc(m_rstd_ready, 1)
                pool.wait_ge(m_rstd_ready, stage + 1)
                for i in range(STEPS):
                    pool.tensor_scalar(m_h[:, i, :], m_h[:, i, :], m_mv[:, i, 0:1], m_rstd[:, i:i + 1],
                                       ALU.subtract, ALU.mult).then_inc(m_norm_ready, 1)

            normalize_positions(0)
            pool.wait_ge(mask_in, 16)
            for l in range(LAYERS):
                pool.tensor_scalar(mask_all[:, l, :], mask_u8[:, min(l, 1), :], -1.0, BIG, ALU.add, ALU.mult
                                   ).then_inc(mask_made, 1)
            normalize_positions(1)
            pool.wait_ge(null_sq_made, 1)
            for l in range(LAYERS):
                pool.tensor_tensor(null_r[:, l:l + 1], sumsq[:, 0:1], norm_power[:, l, 0:1], ALU.pow
                                   ).then_inc(null_r_made, 1)
            pool.wait_ge(null_kl_made, 1)
            for l in range(LAYERS):
                pool.tensor_tensor(null_prod[l][:], w_q[:, l, :].rearrange("p (h d) -> p h d", h=HEADS),
                                   null_kl[:, l:l + 1, :].to_broadcast([P, HEADS, DH]), ALU.mult
                                   ).then_inc(null_prod_made, 1)

            def input_rstd(m):
                pool.wait_ge(var_ready, m.count(1, 1))
                pool.tensor_tensor(rstd[:], var_eps[:], rsqrt_power[:, 0:1], ALU.pow).then_inc(rstd_ready, 1)

            def output_rstd(n):
                pool.wait_ge(y_var_ready, n.count(1, 1))
                pool.tensor_tensor(y_rstd[:], y_var[:], rsqrt_power[:, 0:1], ALU.pow).then_inc(y_rstd_ready, 1)

            def queries(m, half):
                a, b = (0, 1 + HALF) if half == 0 else (1 + HALF, 1 + HEADS)
                h0, h1 = half * HALF, (half + 1) * HALF
                pool.wait_ge(sumsq_ready, m.count(2, half + 1))
                wait_apart(pool)
                pool.tensor_tensor(r_norm[:, a:b], sumsq[:, a:b], pick(norm_power, m.of_layer())[:, a:b], ALU.pow
                                   ).then_inc(norm_ready, 1)
                pool.wait_ge(norm_ready, m.count(2, half + 1))
                pool.tensor_tensor(q_n[:, h0:h1, :], q_raw[:, h0:h1, :],
                                   r_norm[:, 1 + h0:1 + h1].unsqueeze(2).to_broadcast([P, HALF, DH]),
                                   ALU.mult).then_inc(q_scaled, 1)
                pool.wait_ge(q_scaled, m.count(2, half + 1))
                if m.layer is not None:
                    pool.wait_ge(q_t_ps, m.count(GROUPS, 0))
                wait_apart(pool)
                pool.tensor_scalar(q_split[:, h0:h1, 0, :], q_n[:, h0:h1, :], 1.0, 0.0, ALU.mult, ALU.add
                                   ).then_inc(q_high, 1)
                pool.wait_ge(q_high, m.count(2, half + 1))
                pool.tensor_tensor(q_split[:, h0:h1, 1, :], q_n[:, h0:h1, :],
                                   q_split[:, h0:h1, 0, :].bitcast(F32), ALU.subtract).then_inc(q_low, 1)

            def causal(layer, block):
                t = block % ROWS
                pool.wait_ge(bias_in[t % 2], layer * 32 + 16 * (block // 2 + 1))
                wait_apart(pool)
                diagonal = bias[:, t % 2, :, P * t:P * (t + 1)]
                pool.affine_select(out=diagonal, in_=diagonal, compare_op=ALU.is_ge, fill=masked, base=0,
                                   pattern=[[0, HEADS], [-1, P]], channel_multiplier=1
                                   ).then_inc(bias_ready, 1)

            def step(layer, s):
                m, after = Step(layer, s + 1), Step(layer, s + 2)
                if m.exists():
                    for half in range(2):
                        queries(m, half)
                if s >= 1:
                    output_rstd(Step(layer, s - 1))
                if after.exists():
                    input_rstd(after)
                if s % 2 == 1 and m.exists():
                    causal(layer, s // 2 + 1)

            input_rstd(Step(None, 0))
            input_rstd(Step(None, 1))
            for half in range(2):
                queries(Step(None, 0), half)
            masked = pool.to_reg(-BIG)
            causal(0, 0)
            for s in range(BEFORE_LOOP):
                step(0, s)
            with pool.Fori(0, LAYERS - 1) as layer:
                for s in range(BEFORE_LOOP, BEFORE_LOOP + STEPS):
                    step(layer, s)
            for s in range(BEFORE_LOOP, STEPS):
                step(LAYERS - 1, s)
            output_rstd(Step(LAYERS - 1, STEPS - 1))

        @block.scalar
        def _(act):
            for i, name in enumerate(("w0", "b0", "b1")):
                act.dma_start(m_rows[:, i].rearrange("p l c -> p (l c)"), rows(d[name])).then_inc(mlp_in, 16)
            act.dma_start(m_cols[:], d["m_cols"]).then_inc(mlp_in, 16)
            for to, name in ((m_w1, "w1"), (m_w2, "w2")):
                act.dma_start(to[:], d[name].rearrange("l c n -> c l n")).then_inc(mlp_in, 16)
            act.dma_start(m_b2[:], d["b2_t"]).then_inc(mlp_in, 16)
            for i in range(2):
                act.wait_ge(x_t_ps, i + 1)
                act.copy(tokens_t[:, 512 * i:512 * (i + 1)], bank[i][:]).then_inc(x_t_sb, 1)
            act.wait_ge(router_arg, 1)
            act.activation(route[:, 1], route[:, 0], ACT.Exp, scale=0.5).then_inc(router_exp, 1)

            def leaky_slope(j):
                act.wait_ge(up_ps, j + 1)
                if j >= 2:
                    act.wait_ge(hidden_made, j - 1)
                act.mul(leak[:, j % 2, :], bank[2 + j % 2][:], 0.01).then_inc(leak_sb, 1)

            def position_silu(stage):
                for l in range(2):
                    act.wait_ge(m_t_ps, 2 * stage + l + 1)
                    if stage == 1:
                        act.wait_ge(m_h_ps, 2)
                    act.activation(m_act[:, ROWS * l:ROWS * (l + 1), :].rearrange("p s c -> p (s c)"),
                                   bank[6 * stage + l][:], ACT.Silu,
                                   scale=m_cols[:, 2 * stage + l:2 * stage + l + 1]).then_inc(m_t_sb, 1)

            for j in range(2):
                leaky_slope(j)
            act.wait_ge(mlp_in, MLP_LOADS)
            position_silu(0)
            for i in range(2):
                act.wait_ge(coef_t_ps, i + 1)
                act.copy(coef_t[:, 512 * i:512 * (i + 1)], bank[i][0:EXPERTS, :]).then_inc(coef_t_sb, 1)
            for j in range(2, CHUNKS):
                leaky_slope(j)
            position_silu(1)
            act.wait_ge(attn_in, ATTN_LOADS)

            def input_t(m):
                act.wait_ge(xn_t_ps, m.count(1, 1))
                if m.layer is not None:
                    act.wait_ge(q_ps, m.count(2, 0))
                wait_apart(act)
                act.activation(xn_t[:], misc[0][:, 0:P], ACT.Copy, scale=pick(g_in, m.of_layer())).then_inc(xn_t_sb, 1)

            def raw_queries(m, half):
                act.wait_ge(q_ps, m.count(2, half + 1))
                if m.layer is not None:
                    act.wait_ge(q_scaled, m.count(2, 0))
                if m.layer is not None or half == 1:
                    act.wait_ge(sumsq_ready, m.count(2, half))
                act.copy(q_raw[:, half * HALF:(half + 1) * HALF, :].rearrange("p h d -> p (h d)"),
                         misc[half][:])
                act.activation(q_sq[:].rearrange("p h d -> p (h d)"), misc[half][:], ACT.Square
                               ).then_inc(q_sq_sb, 1)

            def queries_t(m, g):
                act.wait_ge(q_t_ps, m.count(GROUPS, g + 1))
                if m.c >= 2:
                    act.wait_ge(scores_ready, m.count(HEADS, -HEADS))
                act.copy(q_stack[:, m.c % BATCH, GROUP * g:GROUP * (g + 1), :].rearrange("p h c -> p (h c)"),
                         misc[g % 2][:]).then_inc(q_ready, 1)

            def output_t(n, i):
                act.wait_ge(o_t_ps, n.count(3, i + 1))
                if n.c >= 1:
                    act.wait_ge(y_ps, n.count(1, 0))
                act.copy(o_t[:, 4 * i:4 * i + 4, :].rearrange("p k c -> p (k c)"), misc[i][:]
                         ).then_inc(o_t_sb, 1)

            def exponentials(layer, k):
                s, h = divmod(k, HEADS)
                act.wait_ge(logits_ready, layer * UNITS + k + 1)
                if k >= RING:
                    act.wait_ge(probs_t_ready, layer * UNITS + k - RING + 1)
                act.activation(probs[:, k % RING, 0:width(s)], neg_logits[:, k % RING, 0:width(s)], ACT.Exp,
                               bias=neg_max[:, s % BATCH, h:h + 1], scale=-1.0).then_inc(probs_ready, 1)

            def null_exponentials(n, g):
                act.wait_ge(null_arg_ready, n.count(GROUPS, g + 1))
                act.activation(null_p[:, n.c % BATCH, GROUP * g:GROUP * (g + 1)],
                               null_arg[:, n.c % BATCH, GROUP * g:GROUP * (g + 1)], ACT.Exp, scale=-1.0
                               ).then_inc(null_p_ready, 1)

            def copy_probs(layer, k):
                act.wait_ge(probs_t_ready, layer * UNITS + k + 1)
                if k >= RING:
                    act.wait_ge(av_ready, layer * UNITS + k - RING + 1)
                act.copy(probs_t[:, k % RING, 0:width(k // HEADS)], probs_t_bank[k % 2][:, 0:width(k // HEADS)]
                         ).then_inc(copied_scalar, 1)

            first = Step(None, 0)
            leaky_slope(CHUNKS)
            input_t(first)
            leaky_slope(CHUNKS + 1)
            raw_queries(first, 0)
            leaky_slope(CHUNKS + 2)
            raw_queries(first, 1)
            leaky_slope(CHUNKS + 3)
            leaky_slope(CHUNKS + 4)
            for g in range(GROUPS):
                queries_t(first, g)

            def step(layer, s):
                m, before = Step(layer, s + 1), Step(layer, s - 1)
                for h in range(HEADS):
                    k = s * HEADS + h
                    if k >= T_LAG and not on_vector(k - T_LAG):
                        copy_probs(layer, k - T_LAG)
                    exponentials(layer, k)
                    if h % GROUP == 0 and k >= GROUP:
                        null_exponentials(Step(layer, (k - 1) // HEADS), (k - 1) % HEADS // GROUP)
                    if h in (6, 8) and s >= 1:
                        output_t(before, (h - 6) // 2)
                    if not m.exists():
                        continue
                    if h == 1:
                        input_t(m)
                    if h in (3, 5):
                        raw_queries(m, (h - 3) // 2)
                    if h >= HEADS - GROUPS:
                        queries_t(m, h - (HEADS - GROUPS))

            for s in range(BEFORE_LOOP):
                step(0, s)
            with act.Fori(0, LAYERS - 1) as layer:
                for s in range(BEFORE_LOOP, BEFORE_LOOP + STEPS):
                    step(layer, s)
            for s in range(BEFORE_LOOP, STEPS):
                step(LAYERS - 1, s)
            for k in range(UNITS - T_LAG, UNITS):
                if not on_vector(k):
                    copy_probs(LAYERS - 1, k)
            null_exponentials(Step(LAYERS - 1, STEPS - 1), GROUPS - 1)
            for i in range(2):
                output_t(Step(LAYERS - 1, STEPS - 1), i)

        @block.vector
        def _(dve):
            links, base = [0], [0]

            def link(ins, apart=False):
                links[0] += 1
                ins.then_inc(vector_link, 1)
                dve.wait_ge(vector_link, base[0] + links[0])
                if apart:
                    wait_apart(dve)

            def position_stats():
                for i in range(STEPS):
                    ins = dve.bn_stats(m_stats[:, i, :], m_h[:, i, :])
                link(ins)
                for i in range(STEPS):
                    ins = dve.bn_aggr(m_mv[:, i, :], m_stats[:, i, :])
                link(ins)
                dve.tensor_scalar(m_var[:], m_mv[:, :, 1], EPS, None, ALU.add).then_inc(m_var_ready, 1)

            dve.wait_ge(route_in, 48)
            dve.tensor_copy(g_rep[:], g_col[:].unsqueeze(2).to_broadcast([GDIM, BATCH, P])
                            ).then_inc(g_rep_made, 1)
            dve.wait_ge(ident_in, 16)
            link(dve.tensor_copy(ident_r[:], ident[:]))
            dve.wait_ge(consts_in, 48)
            dve.wait_ge(mlp_in, MLP_LOADS)
            for i in range(STEPS):
                ins = dve.scalar_tensor_tensor(out=m_h[:, i, :], in0=m_rows[:, 0, i // ROWS, :],
                                               scalar=pos[:, i % ROWS:i % ROWS + 1],
                                               in1=m_rows[:, 1, i // ROWS, :], op0=ALU.mult, op1=ALU.add)
            link(ins)
            position_stats()
            over = [P, STEPS, EXPERTS]
            dve.wait_ge(router_ps, 1)
            logits = bank[7][:, 0:STEPS * EXPERTS].rearrange("p (s e) -> p s e", s=STEPS)
            link(dve.tensor_reduce(best[:, 0], logits, AX_X, ALU.max))
            dve.tensor_tensor(route[:, 0], logits, best[:, 0].unsqueeze(2).to_broadcast(over), ALU.subtract
                              ).then_inc(router_arg, 1)
            dve.wait_ge(router_exp, 1)
            link(dve.tensor_reduce(best[:, 0], route[:, 1], AX_X, ALU.add))
            link(dve.reciprocal(best[:, 1], best[:, 0]))
            link(dve.tensor_tensor(route[:, 0], route[:, 1], best[:, 1].unsqueeze(2).to_broadcast(over),
                                   ALU.mult))
            ranks = rank8[:].unsqueeze(1).to_broadcast(over)
            for i, rest in enumerate((route[:, 0], route[:, 3])):
                link(dve.tensor_reduce(best[:, 0], rest, AX_X, ALU.max))
                link(dve.tensor_tensor(route[:, 1], rest, best[:, 0].unsqueeze(2).to_broadcast(over),
                                       ALU.is_equal))
                link(dve.tensor_tensor(route[:, 1], route[:, 1], ranks, ALU.mult))
                link(dve.tensor_reduce(best[:, 1], route[:, 1], AX_X, ALU.max))
                link(dve.tensor_tensor(route[:, 2 - i], route[:, 1],
                                       best[:, 1].unsqueeze(2).to_broadcast(over), ALU.is_equal))
                if i == 0:
                    link(dve.scalar_tensor_tensor(out=route[:, 3], in0=route[:, 2], scalar=-2.0,
                                                  in1=route[:, 0], op0=ALU.mult, op1=ALU.add))
            link(dve.tensor_tensor(route[:, 3], route[:, 1], route[:, 2], ALU.add))
            link(dve.tensor_tensor(route[:, 1], route[:, 0], route[:, 3], ALU.mult))
            link(dve.tensor_reduce(best[:, 0], route[:, 1], AX_X, ALU.add))
            link(dve.tensor_scalar(best[:, 1], best[:, 0], 1e-20, None, ALU.add))
            link(dve.reciprocal(best[:, 2], best[:, 1]))
            dve.tensor_tensor(route[:, 2], route[:, 1], best[:, 2].unsqueeze(2).to_broadcast(over), ALU.mult
                              ).then_inc(coef_made, 1)

            def gate_times_up(j):
                half, c = divmod(j, CHUNKS)
                dve.wait_ge(leak_sb, j + 1)
                if j >= 1:
                    dve.wait_ge(hidden_made, j)
                link(dve.tensor_tensor(gated, bank[2 + j % 2][:], leak[:, j % 2, :], ALU.max))
                dve.tensor_tensor(hidden[c][:, 512 * half:512 * (half + 1)], gated, bank[4 + j % 2][:],
                                  ALU.mult).then_inc(hidden_made, 1)

            def times_weights(j):
                half, c = divmod(j, PAIRS)
                dve.wait_ge(spread_ps, j + 1)
                dve.wait_ge(hidden_made, half * CHUNKS + c + 1)
                part = hidden[c][:, 512 * half:512 * (half + 1)]
                dve.tensor_tensor(part, part, bank[j % 2][:], ALU.mult).then_inc(hidden_ready, 1)

            def add_experts(s):
                dve.wait_ge(moe_ps, s + 1)
                dve.tensor_tensor(x_res[:, s, :], x_res[:, s, :], bank[s % 2][:, 0:DIM], ALU.add
                                  ).then_inc(x_ready, 1)

            gate_times_up(0)
            gate_times_up(1)
            for l in range(2):
                dve.wait_ge(m_h_ps, l + 1)
                dve.tensor_tensor(m_h[:, ROWS * l:ROWS * (l + 1), :],
                                  bank[6 + l][:].rearrange("p (s c) -> p s c", s=ROWS),
                                  m_rows[:, 2, l:l + 1, :].to_broadcast([P, ROWS, DIM]), ALU.add
                                  ).then_inc(m_h_sb, 1)
            dve.wait_ge(m_h_sb, 2)
            position_stats()
            for j in range(2, CHUNKS):
                gate_times_up(j)
            dve.wait_ge(attn_in, ATTN_LOADS)
            dve.wait_ge(pool_consts, POOL_CONSTS)
            for l in range(2):
                link(dve.scalar_tensor_tensor(out=k_factor[:, 1 + l, :], in0=qk_scales[:, l, 0, :],
                                              scalar=Q_SCALE, in1=qk_scales[:, l, 1, :],
                                              op0=ALU.mult, op1=ALU.mult))
            link(dve.tensor_tensor(k_sq[:], null_k[:], null_k[:], ALU.mult))
            link(dve.tensor_reduce(sumsq[:, 0:1], k_sq[:], AX_X, ALU.add))
            dve.tensor_scalar(sumsq[:, 0:1], sumsq[:, 0:1], NORM_FLOOR, None, ALU.max
                              ).then_inc(null_sq_made, 1)
            for i in range(2):
                cols = slice(i, (STEPS - 1) * (HEADS + 2) + i + 1, HEADS + 2)
                ins = dve.tensor_copy(null_v_cols[i * DH:(i + 1) * DH, cols],
                                      null_v[i * DH:(i + 1) * DH, :].to_broadcast([DH, STEPS]))
            ins.then_inc(null_cols_made, 1)
            for j in range(PAIRS):
                times_weights(j)
            dve.wait_ge(null_r_made, LAYERS)
            for l in range(LAYERS):
                ins = dve.scalar_tensor_tensor(out=null_kl[:, l, :], in0=null_k[:], scalar=null_r[:, l:l + 1],
                                               in1=k_factor[:, l, :], op0=ALU.mult, op1=ALU.mult)
            ins.then_inc(null_kl_made, 1)
            for l in range(2):
                dve.wait_ge(m_out_ps, l + 1)
                dve.tensor_scalar(m_bias[:, l, 0:SEQ], bank[6 + l][0:HEADS, :], m_b2[:, l:l + 1], None,
                                  ALU.add).then_inc(m_out_sb, 1)
            dve.wait_ge(x_in, 32)
            for s in range(STEPS // 2):
                add_experts(s)

            def input_stats(m):
                dve.wait_ge(x_ready, m.count(1, 1))
                if m.layer is not None or m.c >= 1:
                    dve.wait_ge(xn_ready, m.count(1, 0))
                link(dve.bn_stats(stats[:], x_res[:, m.c % STEPS, :]), apart=True)
                link(dve.bn_aggr(mv[:], stats[:]))
                dve.tensor_scalar(var_eps[:], mv[:, 1:2], EPS, None, ALU.add).then_inc(var_ready, 1)

            def input_norm(m):
                dve.wait_ge(rstd_ready, m.count(1, 1))
                if m.layer is not None or m.c >= 1:
                    dve.wait_ge(xn_t_ps, m.count(1, 0))
                dve.tensor_scalar(xn[:], x_res[:, m.c % STEPS, :], mv[:, 0:1], rstd[:], ALU.subtract, ALU.mult
                                  ).then_inc(xn_ready, 1)

            def keys_values(m):
                dve.wait_ge(kvn_ps, m.count(1, 1))
                dve.tensor_copy(kvn[:], misc[1][:, 0:PROJ]).then_inc(kvn_sb, 1)
                dve.wait_ge(kvn_sb, m.count(1, 1))
                link(dve.tensor_tensor(k_sq[:], kvn[:, 0:DH], kvn[:, 0:DH], ALU.mult))
                link(dve.tensor_reduce(sumsq[:, 0:1], k_sq[:], AX_X, ALU.add))

            def query_squares(m, half):
                a, b = (0, 1 + HALF) if half == 0 else (1 + HALF, 1 + HEADS)
                dve.wait_ge(q_sq_sb, m.count(2, half + 1))
                link(dve.tensor_reduce(sumsq[:, 1 + half * HALF:b], q_sq[:], AX_X, ALU.add))
                dve.tensor_scalar(sumsq[:, a:b], sumsq[:, a:b], NORM_FLOOR, None, ALU.max
                                  ).then_inc(sumsq_ready, 1)

            def split_keys(m):
                if m.c >= STEPS:
                    dve.wait_ge(av_ready, m.count(HEADS, -HEADS))
                dve.tensor_copy(values[:, m.c % BATCH, m.c % STEPS // BATCH, 0:DH], kvn[:, DH:KV])
                dve.wait_ge(norm_ready, m.count(2, 1))
                link(dve.scalar_tensor_tensor(out=k_n[:], in0=kvn[:, 0:DH], scalar=r_norm[:, 0:1],
                                              in1=pick(k_factor, m.of_layer()), op0=ALU.mult, op1=ALU.mult))
                twice = k_n[:].unsqueeze(1).to_broadcast([P, 2, DH])
                if m.layer is not None:
                    dve.wait_ge(k_t_ps, m.count(1, 0))
                link(dve.tensor_copy(k_split[:, 0], twice))
                dve.tensor_tensor(k_split[:, 1], twice, k_split[:, 0].bitcast(F32), ALU.subtract
                                  ).then_inc(k_split_ready, 1)

            def null_scores(m):
                dve.wait_ge(norm_ready, m.count(2, 2))
                link(dve.tensor_tensor(null_t[:], kvn[:, KV:PROJ], r_norm[:, 1:1 + HEADS], ALU.mult))
                dve.scalar_tensor_tensor(out=neg_null[:, m.c % BATCH, :], in0=null_t[:], scalar=-1.0,
                                         in1=pick(null_bias, m.of_layer()), op0=ALU.mult, op1=ALU.subtract
                                         ).then_inc(null_ready, 1)

            def keys_t(m):
                t = m.c % STEPS // BATCH
                dve.wait_ge(k_t_ps, m.count(1, 1))
                if m.c >= STEPS:
                    dve.wait_ge(scores_ready, m.count(HEADS, -HEADS))
                dve.tensor_copy(keys[:, m.c % BATCH, :, P * t:P * (t + 1)],
                                misc[1][:, 0:2 * P].rearrange("p (i c) -> p i c", i=2)
                                ).then_inc(keys_ready, 1)

            def unit_logits(layer, k):
                s, h = divmod(k, HEADS)
                if h == 0:
                    dve.wait_ge(bias_ready, layer * ROWS + s // BATCH + 1)
                    dve.wait_ge(null_ready, Step(layer, s).count(1, 1))
                dve.wait_ge(scores_ready, layer * UNITS + k + 1)
                if k >= RING:
                    dve.wait_ge(probs_ready, layer * UNITS + k - RING + 1)
                wait_apart(dve)
                dve.tensor_tensor_reduce(neg_logits[:, k % RING, 0:width(s)], scores_ps[k % 2][:, 0:width(s)],
                                         bias[:, s // BATCH % 2, h, 0:width(s)], -1.0,
                                         neg_null[:, s % BATCH, h:h + 1], ALU.add, ALU.min,
                                         neg_max[:, s % BATCH, h:h + 1]).then_inc(logits_ready, 1)

            def copy_probs(layer, k):
                dve.wait_ge(probs_t_ready, layer * UNITS + k + 1)
                if k >= RING:
                    dve.wait_ge(av_ready, layer * UNITS + k - RING + 1)
                dve.tensor_copy(probs_t[:, k % RING, 0:width(k // HEADS)],
                                probs_t_bank[k % 2][:, 0:width(k // HEADS)]).then_inc(copied_vector, 1)

            def null_arguments(n, g):
                b, hs = n.c % BATCH, slice(GROUP * g, GROUP * (g + 1))
                dve.wait_ge(logits_ready, n.count(HEADS, GROUP * (g + 1)))
                dve.tensor_tensor(null_arg[:, b, hs], neg_null[:, b, hs], neg_max[:, b, hs], ALU.subtract
                                  ).then_inc(null_arg_ready, 1)

            def normalize_group(n, g):
                b, hs = n.c % BATCH, slice(GROUP * g, GROUP * (g + 1))
                av = av_bank[g % 2][:, 0:GROUP * VW].rearrange("p (h c) -> p h c", h=GROUP)
                dve.wait_ge(null_p_ready, n.count(GROUPS, g + 1))
                dve.wait_ge(av_ready, n.count(HEADS, GROUP * (g + 1)))
                link(dve.tensor_tensor(denom[:, hs], av[:, :, DH], null_p[:, b, hs], ALU.add))
                link(dve.reciprocal(r_denom[:, hs], denom[:, hs]))
                if n.c >= 1:
                    dve.wait_ge(o_t_ps, n.count(3, 0))
                dve.tensor_tensor(null_w[:, hs], null_p[:, b, hs], r_denom[:, hs], ALU.mult)
                dve.tensor_tensor(o_n[:, hs, :], av[:, :, 0:DH],
                                  r_denom[:, hs].unsqueeze(2).to_broadcast([P, GROUP, DH]), ALU.mult
                                  ).then_inc(group_ready, 1)

            def null_weights_t(n):
                dve.wait_ge(o_t_ps, n.count(3, 3))
                dve.tensor_copy(null_wt[:], misc[0][0:HEADS, 0:P]).then_inc(null_wt_sb, 1)

            def output_stats(n):
                dve.wait_ge(y_ps, n.count(1, 1))
                dve.tensor_copy(y_sb[:], misc[0][:, P:P + DIM]).then_inc(y_sb_ready, 1)
                dve.wait_ge(y_sb_ready, n.count(1, 1))
                link(dve.bn_stats(y_stats[:], y_sb[:]), apart=True)
                link(dve.bn_aggr(y_mv[:], y_stats[:]))
                dve.tensor_scalar(y_var[:], y_mv[:, 1:2], EPS, None, ALU.add).then_inc(y_var_ready, 1)

            def add_output(n):
                dve.wait_ge(y_rstd_ready, n.count(1, 1))
                link(dve.tensor_scalar(y_c[:], y_sb[:], y_mv[:, 0:1], y_rstd[:], ALU.subtract, ALU.mult))
                link(dve.tensor_tensor(y_c[:], y_c[:], pick(g_out, n.of_layer()), ALU.mult))
                tile = x_res[:, n.c % STEPS, :]
                dve.tensor_tensor(tile, tile, y_c[:], ALU.add).then_inc(x_ready, 1)

            first = Step(None, 0)
            input_stats(first)
            for l in range(LAYERS):
                dve.wait_ge(null_prod_made, l + 1)
                ins = dve.tensor_reduce(w_kvn[:, l, KV:PROJ], null_prod[l][:], AX_X, ALU.add)
            ins.then_inc(tables_made, 1)
            input_norm(first)
            gate_times_up(CHUNKS)
            input_stats(Step(None, 1))
            gate_times_up(CHUNKS + 1)
            keys_values(first)
            query_squares(first, 0)
            gate_times_up(CHUNKS + 2)
            query_squares(first, 1)
            gate_times_up(CHUNKS + 3)
            split_keys(first)
            gate_times_up(CHUNKS + 4)
            times_weights(PAIRS)
            input_norm(Step(None, 1))
            times_weights(PAIRS + 1)
            null_scores(first)
            keys_t(first)
            for j in range(PAIRS + 2, 2 * PAIRS):
                times_weights(j)
            for s in range(STEPS // 2, STEPS):
                add_experts(s)
            def step(layer, s):
                m, after, before = Step(layer, s + 1), Step(layer, s + 2), Step(layer, s - 1)
                for h in range(HEADS):
                    k = s * HEADS + h
                    unit_logits(layer, k)
                    if k >= T_LAG and on_vector(k - T_LAG):
                        copy_probs(layer, k - T_LAG)
                    if h % GROUP == GROUP - 1:
                        null_arguments(Step(layer, s), h // GROUP)
                    if h % GROUP == 1 and k >= 2 * GROUP:
                        done = k - 2 * GROUP
                        normalize_group(Step(layer, done // HEADS), done % HEADS // GROUP)
                    if s == 0 and h == 9:
                        dve.wait_ge(null_out_ps, 1)
                        dve.tensor_copy(null_out[:].rearrange("h l n -> h (l n)"),
                                        misc[0][0:HEADS, 0:LAYERS * DIM]).then_inc(null_out_sb, 1)
                    if s >= 1:
                        if h == 9:
                            null_weights_t(before)
                        if h == 12:
                            output_stats(before)
                        if h == 15:
                            add_output(before)
                    if m.exists():
                        if h == 2:
                            keys_values(m)
                        if h in (4, 6):
                            query_squares(m, (h - 4) // 2)
                        if h == 8:
                            split_keys(m)
                        if h == 11:
                            keys_t(m)
                        if h == 14:
                            null_scores(m)
                    if after.exists():
                        if h == 13:
                            input_stats(after)
                        if h == 15:
                            input_norm(after)

            for s in range(BEFORE_LOOP):
                step(0, s)
            before_loop = links[0]
            with dve.Fori(0, LAYERS - 1) as layer:
                base[0], links[0] = layer * LINKS_LAYER + before_loop, 0
                for s in range(BEFORE_LOOP, BEFORE_LOOP + STEPS):
                    step(layer, s)
                assert links[0] == LINKS_LAYER, links
            base[0], links[0] = (LAYERS - 1) * LINKS_LAYER + before_loop, 0
            for s in range(BEFORE_LOOP, STEPS):
                step(LAYERS - 1, s)
            for k in range(UNITS - T_LAG, UNITS):
                if on_vector(k):
                    copy_probs(LAYERS - 1, k)
            last = Step(LAYERS - 1, STEPS - 1)
            normalize_group(last, GROUPS - 2)
            normalize_group(last, GROUPS - 1)
            null_weights_t(last)
            output_stats(last)
            add_output(last)

        @block.tensor
        def _(pe):
            def mm(to, stationary, moving, start=True, stop=True):
                return pe.matmul(to, stationary, moving, start=start, stop=stop, skip_group_check=True)

            pe.wait_ge(ident_in, 16)
            pe.wait_ge(x_in, 32)
            for s in range(STEPS):
                ins = pe.transpose(bank[s // 4][:, P * (s % 4):P * (s % 4 + 1)], x_res[:, s, :], ident[:])
                if s % 4 == 3:
                    ins.then_inc(x_t_ps, 1)
            pe.wait_ge(x_t_sb, 2)
            pe.wait_ge(route_in, 48)
            pe.wait_ge(g_rep_made, 1)
            for s in range(STEPS):
                to = bank[7][:, EXPERTS * s:EXPERTS * (s + 1)]
                mm(to, tokens_t[:, P * s:P * (s + 1)], w_t[:], stop=False)
                ins = mm(to, g_rep[:, s % BATCH, :], w_g[:], start=False)
            ins.then_inc(router_ps, 1)

            def gate_up(j):
                half, c = divmod(j, CHUNKS)
                if j >= 2:
                    pe.wait_ge(hidden_made, j - 1)
                moving = tokens_t[:, 512 * half:512 * (half + 1)]
                mm(bank[2 + j % 2][:], w_gate[:, c, :], moving)
                mm(bank[4 + j % 2][:], w_up[:, c, :], moving).then_inc(up_ps, 1)

            def coefficients_t():
                pe.wait_ge(coef_made, 1)
                pe.wait_ge(m_t_sb, 2)
                for s in range(STEPS):
                    ins = pe.transpose(bank[s // 4][0:EXPERTS, P * (s % 4):P * (s % 4 + 1)],
                                       route[:, 2, s, :], ident[:])
                    if s % 4 == 3:
                        ins.then_inc(coef_t_ps, 1)

            def spread(j):
                half, c = divmod(j, PAIRS)
                if half == 0 and c >= 2:
                    pe.wait_ge(hidden_ready, j - 1)
                elif half == 0:
                    pe.wait_ge(consts_in, 48)
                    pe.wait_ge(coef_t_sb, 2)
                elif c < 2:
                    pe.wait_ge(x_ready, c + 3)
                else:
                    pe.wait_ge(hidden_ready, j - 1)
                mm(bank[j % 2][:], pair_sel[:, P * c:P * (c + 1)], coef_t[:, 512 * half:512 * (half + 1)]
                   ).then_inc(spread_ps, 1)

            def down(s):
                half, i = divmod(s, STEPS // 2)
                if i == 0:
                    pe.wait_ge(hidden_ready, (half + 1) * PAIRS)
                    pe.wait_ge(hidden_made, (half + 1) * CHUNKS)
                elif i >= 2:
                    pe.wait_ge(x_ready, s - 1)
                for c in range(CHUNKS):
                    ins = mm(bank[s % 2][:, 0:DIM], hidden[c][:, P * s:P * (s + 1)], w_down[:, c, :],
                             start=(c == 0), stop=(c == CHUNKS - 1))
                ins.then_inc(moe_ps, 1)

            def positions_t(stage):
                for l in range(2):
                    pe.wait_ge(m_norm_ready, STEPS * stage + ROWS * (l + 1))
                    for i in range(ROWS):
                        ins = pe.transpose(bank[6 * stage + l][:, P * i:P * (i + 1)], m_h[:, ROWS * l + i, :],
                                           ident[:])
                    ins.then_inc(m_t_ps, 1)

            pe.wait_ge(expert_in, 96)
            gate_up(0)
            gate_up(1)
            pe.wait_ge(mlp_in, MLP_LOADS)
            positions_t(0)
            for l in range(2):
                pe.wait_ge(m_t_sb, l + 1)
                if l == 1:
                    pe.wait_ge(router_arg, 1)
                for i in range(ROWS):
                    ins = mm(bank[6 + l][:, P * i:P * (i + 1)], m_act[:, ROWS * l + i, :], m_w1[:, l, :])
                ins.then_inc(m_h_ps, 1)
            coefficients_t()
            for j in range(2, CHUNKS):
                gate_up(j)
            spread(0)
            spread(1)
            pe.wait_ge(m_h_sb, 2)
            positions_t(1)
            spread(2)
            spread(3)
            for l in range(2):
                pe.wait_ge(m_t_sb, 2 + l + 1)
                mm(bank[6 + l][0:HEADS, :], m_w2[:, l, :],
                   m_act[:, ROWS * l:ROWS * (l + 1), :].rearrange("p s c -> p (s c)")).then_inc(m_out_ps, 1)
            for s in range(STEPS // 2):
                down(s)

            def input_t(m):
                pe.wait_ge(xn_ready, m.count(1, 1))
                if m.layer is not None:
                    pe.wait_ge(q_ready, m.count(GROUPS, 0))
                pe.transpose(misc[0][:, 0:P], xn[:], ident[:]).then_inc(xn_t_ps, 1)

            def project_kvn(m):
                pe.wait_ge(xn_t_sb, m.count(1, 1))
                mm(misc[1][:, 0:PROJ], xn_t[:], pick(w_kvn, m.of_layer())).then_inc(kvn_ps, 1)

            def project_q(m, half):
                if half == 1:
                    pe.wait_ge(kvn_sb, m.count(1, 1))
                mm(misc[half][:], xn_t[:], pick(w_q, m.of_layer())[:, 512 * half:512 * (half + 1)]
                   ).then_inc(q_ps, 1)

            def keys_t(m, before):
                pe.wait_ge(k_split_ready, m.count(1, 1))
                if before is None:
                    pe.wait_ge(q_sq_sb, m.count(2, 2))
                else:
                    pe.wait_ge(o_t_sb, before.count(2, 2))
                for i in range(2):
                    ins = mm(misc[1][:, P * i:P * (i + 1)], k_split[:, i].rearrange("p i d -> p (i d)"),
                             ident_r[:])
                ins.then_inc(k_t_ps, 1)

            def queries_t(m, g, before):
                pe.wait_ge(q_low, m.count(2, g // 2 + 1))
                if g >= 2:
                    pe.wait_ge(q_ready, m.count(GROUPS, g - 1))
                elif g == 1:
                    pe.wait_ge(keys_ready, m.count(1, 1))
                elif before is None:
                    pe.wait_ge(q_sq_sb, m.count(2, 1))
                    if m.c == 1:
                        pe.wait_ge(null_out_sb, 1)
                else:
                    pe.wait_ge(y_sb_ready, before.count(1, 1))
                for i in range(GROUP):
                    ins = mm(misc[g % 2][:, P * i:P * (i + 1)],
                             q_split[:, GROUP * g + i].rearrange("p i d -> p (i d)"), ident_r[:])
                ins.then_inc(q_t_ps, 1)

            def scores(layer, k):
                s, h = divmod(k, HEADS)
                n, b, w = Step(layer, s), s % BATCH, width(s)
                if h == 0:
                    pe.wait_ge(keys_ready, n.count(1, 1))
                if h % GROUP == 0:
                    pe.wait_ge(q_ready, n.count(GROUPS, h // GROUP + 1))
                if k >= 2:
                    pe.wait_ge(logits_ready, layer * UNITS + k - 1)
                to = scores_ps[k % 2][:, 0:w]
                mm(to, first_row[:], pick(mask_all, n.of_layer())[:, SEQ * b:SEQ * b + w], stop=False)
                mm(to, q_stack[:, b, h, :], keys[:, b, 0, 0:w], start=False, stop=False)
                mm(to, q_stack[:, b, h, :], keys[:, b, 1, 0:w], start=False).then_inc(scores_ready, 1)

            def probs_transposed(layer, k):
                pe.wait_ge(probs_ready, layer * UNITS + k + 1)
                if k >= 2:
                    wait_copied(pe, layer, k - 2)
                for c in range(width(k // HEADS) // P):
                    ins = pe.transpose(probs_t_bank[k % 2][:, P * c:P * (c + 1)],
                                       probs[:, k % RING, P * c:P * (c + 1)], ident[:])
                ins.then_inc(probs_t_ready, 1)

            def times_values(layer, k):
                s, h = divmod(k, HEADS)
                wait_copied(pe, layer, k)
                if h % GROUP == 0 and k >= 2 * GROUP:
                    pe.wait_ge(group_ready, layer * (STEPS * GROUPS) + k // GROUP - 1)
                to = av_bank[h // GROUP % 2][:, VW * (h % GROUP):VW * (h % GROUP + 1)]
                blocks = width(s) // P
                for c in range(blocks):
                    ins = mm(to, probs_t[:, k % RING, P * c:P * (c + 1)], values[:, s % BATCH, c, :],
                             start=(c == 0), stop=(c == blocks - 1))
                ins.then_inc(av_ready, 1)

            def outputs_t(n, i):
                pe.wait_ge(group_ready, n.count(GROUPS, 2 * i + 2))
                if Step(n.layer, n.c + 2).exists():
                    pe.wait_ge(q_sq_sb, Step(n.layer, n.c + 2).count(2, i + 1))
                elif Step(n.layer, n.c + 1).exists():
                    pe.wait_ge(q_ready, n.count(GROUPS, 2 * GROUPS))
                else:
                    pe.wait_ge(y_sb_ready, n.count(1, 0))
                for c in range(4):
                    two = o_n[:, 2 * (4 * i + c):2 * (4 * i + c) + 2, :].rearrange("p h d -> p (h d)")
                    ins = pe.transpose(misc[i][:, P * c:P * (c + 1)], two, ident[:])
                ins.then_inc(o_t_ps, 1)

            def null_weights_t(n):
                pe.wait_ge(o_t_sb, n.count(2, 1))
                pe.transpose(misc[0][0:HEADS, 0:P], null_w[:], ident[:]).then_inc(o_t_ps, 1)

            def project_output(n):
                pe.wait_ge(o_t_sb, n.count(2, 2))
                pe.wait_ge(null_wt_sb, n.count(1, 1))
                to, w = misc[0][:, P:P + DIM], pick(w_o, n.of_layer())
                for c in range(STEPS):
                    mm(to, o_t[:, c, :], w[:, DIM * c:DIM * (c + 1)], start=(c == 0), stop=False)
                mm(to, null_wt[:], pick(null_out, n.of_layer()), start=False).then_inc(y_ps, 1)

            first = Step(None, 0)
            gate_up(CHUNKS)
            pe.wait_ge(m_out_sb, 2)
            input_t(first)
            gate_up(CHUNKS + 1)
            pe.wait_ge(tables_made, 1)
            project_kvn(first)
            project_q(first, 0)
            gate_up(CHUNKS + 2)
            project_q(first, 1)
            gate_up(CHUNKS + 3)
            gate_up(CHUNKS + 4)
            spread(PAIRS)
            spread(PAIRS + 1)
            keys_t(first, None)
            spread(PAIRS + 2)
            spread(PAIRS + 3)
            for i in range(GROUPS):
                down(STEPS // 2 + i)
                queries_t(first, i, None)
            pe.wait_ge(x_ready, STEPS)
            pe.wait_ge(first_row_made, 1)
            pe.wait_ge(mask_made, LAYERS)

            def null_outputs():
                pe.wait_ge(null_cols_made, 1)
                pe.wait_ge(q_sq_sb, 3)
                for l in range(LAYERS):
                    for c in range(STEPS):
                        ins = mm(misc[0][0:HEADS, DIM * l:DIM * (l + 1)],
                                 null_v_cols[:, HEADS * c:HEADS * (c + 1)],
                                 w_o[:, l, DIM * c:DIM * (c + 1)], start=(c == 0), stop=(c == STEPS - 1))
                ins.then_inc(null_out_ps, 1)

            def step(layer, s):
                m = Step(layer, s + 1)
                before = Step(layer, s - 1) if s >= 1 else None
                for h in range(HEADS):
                    k = s * HEADS + h
                    scores(layer, k)
                    if k >= T_LAG:
                        probs_transposed(layer, k - T_LAG)
                    if k >= AV_LAG:
                        times_values(layer, k - AV_LAG)
                    if before is None:
                        if h == 6:
                            null_outputs()
                    else:
                        if h == 6:
                            outputs_t(before, 0)
                        if h == 7:
                            outputs_t(before, 1)
                        if h == 8:
                            null_weights_t(before)
                        if h == 10:
                            project_output(before)
                    if not m.exists():
                        continue
                    if h == 0:
                        input_t(m)
                    if h == 1:
                        project_kvn(m)
                    if h in (2, 4):
                        project_q(m, (h - 2) // 2)
                    if h == 10:
                        keys_t(m, before)
                    if h >= HEADS - GROUPS:
                        queries_t(m, h - (HEADS - GROUPS), before)

            for s in range(BEFORE_LOOP):
                step(0, s)
            with pe.Fori(0, LAYERS - 1) as layer:
                for s in range(BEFORE_LOOP, BEFORE_LOOP + STEPS):
                    step(layer, s)
            for s in range(BEFORE_LOOP, STEPS):
                step(LAYERS - 1, s)
            for k in range(UNITS - T_LAG, UNITS):
                probs_transposed(LAYERS - 1, k)
            for k in range(UNITS - AV_LAG, UNITS):
                times_values(LAYERS - 1, k)
            last = Step(LAYERS - 1, STEPS - 1)
            outputs_t(last, 0)
            outputs_t(last, 1)
            null_weights_t(last)
            project_output(last)


def kernel(**inputs):
    import numpy as np
    import concourse.bacc as bacc
    from concourse.bass_utils import run_bass_kernel_spmd

    a = {name: np.asarray(v) for name, v in inputs.items()}
    L0 = {n: a["L0_cond_" + n] for n in (
        "wt", "wg", "w_gate", "w_up", "w_down", "sw_gate", "sw_up", "sw_down")}

    def stacked(*names):
        return np.stack([a[n] for n in names])

    def later(name):
        return stacked(f"L2_cond_{name}", f"L3_cond_{name}")

    given = {
        "x": a["x"], "cond": a["cond_64"], "cond_t": a["cond_64"].T, "attn_bias": a["fside_16xSxS_0"],
        "masks": stacked("mask_BxS_bk0", "mask_BxS_bf1").reshape(-1),
        "wt_t": L0["wt"].T, "wg_t": L0["wg"].T,
        "w_gate": L0["w_gate"], "w_up": L0["w_up"], "w_down": L0["w_down"],
        "sw_gate": L0["sw_gate"], "sw_up": L0["sw_up"], "sw_down": L0["sw_down"],
        "g_in_t": stacked("L1_cond_g_in", "L2_cond_g_norm", "L3_cond_g_norm").T,
        "g_out": stacked("L1_cond_g_out", "L2_cond_g_out", "L3_cond_g_out").reshape(-1),
        "null_bias": stacked("L1_cond_null_attn_bias", "L2_cond_null_attn_bias",
                             "L3_cond_null_attn_bias").reshape(-1),
        "w_q": stacked("L1_cond_Wq", "L2_cond_Wq", "L3_cond_Wq"),
        "w_kv": stacked("L1_cond_Wkv", "L2_cond_Wkv", "L3_cond_Wkv"),
        "w_o": stacked("L1_cond_Wo", "L2_cond_Wout", "L3_cond_Wout"),
        "q_scale": later("q_scale").reshape(-1), "k_scale": later("k_scale").reshape(-1),
        "w0": later("w0").reshape(-1), "b0": later("b0").reshape(-1), "b1": later("b1").reshape(-1),
        "m_cols": np.concatenate([later("g0"), later("g1")]).T, "w1": later("w1"), "w2": later("w2"),
        "b2_t": later("b2").T,
        "ident": np.eye(P, dtype=np.float32),
        "pos": (SEQ - 1 - np.arange(SEQ)).reshape(ROWS, P).T.astype(np.float32),
        "pair_sel": np.repeat(np.eye(EXPERTS, dtype=np.float32), MID, axis=1),
        "rank8": np.arange(EXPERTS, 0, -1).astype(np.float32),
    }
    nc = bacc.Bacc("TRN2", target_bir_lowering=False, num_devices=1)
    arrays, handles = {}, {}
    for name, array in given.items():
        arrays["in_" + name] = np.ascontiguousarray(array)
        handles[name] = nc.dram_tensor("in_" + name, array.shape, mybir.dt.from_np(array.dtype),
                                       kind="ExternalInput").ap()
    out = nc.dram_tensor("out_x", (BATCH, SEQ, DIM), F32, kind="ExternalOutput").ap()
    build(nc, handles, out)
    return run_bass_kernel_spmd(nc, [arrays], core_ids=[0]).results[0]["out_x"]
```

```python
from contextlib import ExitStack

import concourse.bass as bass
from concourse import mybir

F32 = mybir.dt.float32
F32R = mybir.dt.float32r
U8 = mybir.dt.uint8
ALU = mybir.AluOpType
ACT = mybir.ActivationFunctionType
AX_X = mybir.AxisListType.X

P = 128
BATCH = 2
SEQ = 512
DIM = 128
ROWS = SEQ // P
STEPS = ROWS * BATCH
LAYERS = 3
HEADS = 16
DH = 64
INNER = HEADS * DH
VW = DH + 1
GROUP = 4
GROUPS = HEADS // GROUP
HALF = HEADS // 2
UNITS = STEPS * HEADS
KV = 2 * DH
PROJ = KV + HEADS
EXPERTS = 8
MID = 64
PAIRS = EXPERTS // 2
CHUNKS = PAIRS + 1
GDIM = 64
BIG = 1e30
EPS = 1e-5
NORM_FLOOR = 1e-24
Q_SCALE = 8.0
BEFORE_LOOP = 2
RING = 4
T_LAG = 3
AV_LAG = 5
POOL_CONSTS = 7
ATTN_LOADS = 16 * 11
MLP_LOADS = 16 * 7

TENSOR_AT_WIDE = dict(input_t=1, project_kvn=2, project_q=(3, 5), outputs_t=(5, 7), null_weights_t=8,
                      project_output=10, keys_t=10, queries_t=(13, 14, 15, 15))
TENSOR_AT_NARROW = dict(input_t=0, project_kvn=2, project_q=(2, 4), outputs_t=(6, 7), null_weights_t=8,
                        project_output=10, keys_t=8, queries_t=(12, 13, 14, 15))
SCALAR_AT_WIDE = dict(input_t=0, raw_queries=(3, 5), output_t=(4, 7), queries_t=(13, 13, 15, 15))
SCALAR_AT_NARROW = dict(input_t=0, raw_queries=(3, 5), output_t=(6, 7), queries_t=(12, 13, 14, 15))
VECTOR_AT_WIDE = dict(keys_values=2, query_squares=(4, 6), split_keys=10, null_weights_t=9, keys_t=10,
                      output_stats=11, input_stats=12, null_scores=14, add_output=15, input_norm=13)
VECTOR_AT_NARROW = dict(keys_values=3, query_squares=(4, 6), split_keys=7, null_weights_t=8, keys_t=10,
                        output_stats=12, input_stats=13, null_scores=14, add_output=15, input_norm=14)


def at(h, where):
    return [i for i, place in enumerate(where) if place == h]


class Step:

    def __init__(self, layer, c):
        self.layer, self.c = layer, c

    def count(self, per_step, k):
        own = self.c * per_step + k
        return own if self.layer is None else self.layer * (STEPS * per_step) + own

    def of_layer(self):
        return (0 if self.layer is None else self.layer) + self.c // STEPS

    def exists(self):
        return not isinstance(self.layer, int) or self.layer * STEPS + self.c < LAYERS * STEPS


def width(step):
    return P * (step % STEPS // BATCH + 1)


LOTS = [(s * HEADS + h, n) for s in range(STEPS) for n in [2 if 2 * width(s) <= SEQ else 1]
        for h in range(0, HEADS, n)]


def lot(i):
    first, n = LOTS[i % len(LOTS)]
    return first + i // len(LOTS) * UNITS, n, width(first // HEADS)


def last_unit(i):
    first, n, _ = lot(i)
    return first + n - 1


def lots_of(s):
    return [i for i in range((s // STEPS + 1) * len(LOTS)) if lot(i)[0] // HEADS == s]


def heads_of(s):
    return [(i, k, k % HEADS) for i in lots_of(s) for k in range(lot(i)[0], last_unit(i) + 1)]


def due(i, lag):
    return [j for j in range(max(0, i - 2 * lag), i + 1)
            if last_unit(i - 1) - lag < last_unit(j) <= last_unit(i) - lag]


def left(lag):
    return [j for j in range(len(LOTS)) if last_unit(j) > UNITS - 1 - lag]


def on_vector(i):
    return i % 4 == 3


def copied_by(vector, i):
    return sum(on_vector(j) == vector for j in range(i + 1))


def pick(table, layer):
    n = table.shape[2]
    flat = table[:].rearrange("p l n -> p (l n)")
    return flat[:, layer * n:(layer + 1) * n] if isinstance(layer, int) else flat[:, bass.ds(layer * n, n)]


LINKS_LAYER = STEPS * (2 + 2 + 2 + 2 + 1 + 1 + 2 * GROUPS + 4)


def build(nc, d, out):
    with ExitStack() as ctx:
        def sb(name, shape, dt=F32):
            return ctx.enter_context(nc.sbuf_tensor(name, shape, dt))

        def sem(name):
            return ctx.enter_context(nc.semaphore(name))

        def rows(vector):
            return vector.unsqueeze(0).to_broadcast([P, vector.shape[0]])

        def column(vector):
            return vector.unsqueeze(1)

        ident = sb("ident", [P, P])
        ident_r = sb("ident_r", [P, P], F32R)
        w_q = sb("w_q", [P, LAYERS, INNER])
        w_kvn = sb("w_kvn", [P, LAYERS, PROJ])
        w_o = sb("w_o", [P, LAYERS, STEPS * DIM])
        g_in = sb("g_in", [P, LAYERS, 1])
        g_out = sb("g_out", [P, LAYERS, DIM])
        null_bias = sb("null_bias", [P, LAYERS, HEADS])
        k_factor = sb("k_factor", [P, LAYERS, DH])
        norm_power = sb("norm_power", [P, LAYERS, HEADS + 1])
        rsqrt_power = sb("rsqrt_power", [P, STEPS])
        qk_scales = sb("qk_scales", [P, 2, 2, DH])
        null_k = sb("null_k", [P, DH])
        null_kl = sb("null_kl", [P, LAYERS, DH])
        null_r = sb("null_r", [P, LAYERS])
        null_v = sb("null_v", [P, 1])
        null_v_cols = sb("null_v_cols", [P, STEPS * HEADS])
        null_out = sb("null_out", [HEADS, LAYERS, DIM])
        masks = sb("masks", [P, LAYERS, BATCH * SEQ], U8)

        x_res = sb("x_res", [P, STEPS, DIM])
        bias = sb("bias", [P, 2, HEADS, SEQ])
        keys = sb("keys", [P, BATCH, 2, SEQ], F32R)
        values = sb("values", [P, BATCH, ROWS, VW])
        q_stack = sb("q_stack", [P, BATCH, HEADS, P], F32R)
        q_ones = sb("q_ones", [P, BATCH, HEADS, P], F32R)
        stats = sb("stats", [P, 6])
        mv = sb("mv", [P, 2])
        var_eps = sb("var_eps", [P, 1])
        rstd = sb("rstd", [P, 1])
        xn = sb("xn", [P, DIM])
        xn_t = sb("xn_t", [P, P])
        kvn = sb("kvn", [P, PROJ])
        q_raw = sb("q_raw", [P, HEADS, DH])
        k_sq = sb("k_sq", [P, DH])
        sumsq = sb("sumsq", [P, HEADS + 1])
        r_norm = sb("r_norm", [P, HEADS + 1])
        q_n = sb("q_n", [P, HEADS, DH])
        q_split = sb("q_split", [P, HEADS, 2, DH], F32R)
        k_n = sb("k_n", [P, DH])
        k_split = sb("k_split", [P, 2, 2, DH], F32R)
        null_t = sb("null_t", [P, HEADS])
        neg_null = sb("neg_null", [P, BATCH, HEADS])
        neg_logits = sb("neg_logits", [P, RING, SEQ])
        probs = sb("probs", [P, RING, SEQ])
        probs_t = sb("probs_t", [P, RING, SEQ])
        neg_max = sb("neg_max", [P, BATCH, HEADS])
        null_arg = sb("null_arg", [P, BATCH, HEADS])
        null_p = sb("null_p", [P, BATCH, HEADS])
        denom = sb("denom", [P, HEADS])
        r_denom = sb("r_denom", [P, HEADS])
        null_w = sb("null_w", [P, HEADS])
        o_n = sb("o_n", [P, HEADS, DH])
        o_t = sb("o_t", [P, STEPS, P])
        null_wt = sb("null_wt", [HEADS, P])
        y_sb = sb("y_sb", [P, DIM])
        y_stats = sb("y_stats", [P, 6])
        y_mv = sb("y_mv", [P, 2])
        y_var = sb("y_var", [P, 1])
        y_rstd = sb("y_rstd", [P, 1])
        y_c = sb("y_c", [P, DIM])
        spare = sb("spare", [1, 3, 16])

        rank8 = sb("rank8", [P, EXPERTS])
        w_t = sb("w_t", [P, EXPERTS])
        w_g = sb("w_g", [GDIM, EXPERTS])
        g_col = sb("g_col", [GDIM, BATCH])
        g_rep = sb("g_rep", [GDIM, BATCH, P])
        route = sb("route", [P, 4, STEPS, EXPERTS])
        best = sb("best", [P, 4, STEPS])
        pos = sb("pos", [P, ROWS])
        m_cols = sb("m_cols", [P, 4])
        m_w2 = sb("m_w2", [P, 2, HEADS])
        m_b2 = sb("m_b2", [HEADS, 2])
        m_stats = sb("m_stats", [P, STEPS, 6])
        m_mv = sb("m_mv", [P, STEPS, 2])
        m_var = sb("m_var", [P, STEPS])
        m_rstd = sb("m_rstd", [P, STEPS])
        m_bias = sb("m_bias", [HEADS, 2 * SEQ + P])
        scratch = bias[:, 1].rearrange("p h c -> p (h c)")
        tokens_t = scratch[:, 0:1024]
        leak = scratch[:, 1024:2048].rearrange("p (i c) -> p i c", i=2)
        gated = scratch[:, 2048:2560]
        m_h = scratch[:, 2560:3584].rearrange("p (s c) -> p s c", s=STEPS)
        m_act = scratch[:, 3584:4608].rearrange("p (s c) -> p s c", s=STEPS)
        w_gate, w_up, w_down = (
            scratch[:, 4608 + 640 * i:5248 + 640 * i].rearrange("p (k c) -> p k c", k=CHUNKS) for i in range(3))
        m_rows = scratch[:, 6528:7296].rearrange("p (i l c) -> p i l c", l=2, i=3)
        m_w1 = scratch[:, 7296:7552].rearrange("p (l c) -> p l c", l=2)
        pair_sel = scratch[0:2 * EXPERTS, 7552:8064]
        hidden = [a[:].rearrange("p r c -> p (r c)")[:, 0:STEPS * P] for a in (neg_logits, probs, probs_t)]
        hidden += [a[:].rearrange("p r c -> p (r c)")[:, STEPS * P:2 * STEPS * P]
                   for a in (neg_logits, probs)]
        null_prod = (q_n, q_raw, o_n)
        pair_sel_r = q_stack[0:2 * EXPERTS, 0, STEPS:STEPS + PAIRS].rearrange("e h c -> e (h c)")
        coef_split = k_split[:].rearrange("p i j d -> p (i j d)")[:, 0:STEPS * 2 * EXPERTS].rearrange(
            "p (s i e) -> p s i e", s=STEPS, i=2)
        coef_t = q_stack[0:2 * EXPERTS, 0, 0:STEPS].rearrange("e h c -> e (h c)")
        rel_bias = nc.dram_tensor("rel_bias", [2, HEADS, P, SEQ], F32, kind="Internal").ap()

        bank = [ctx.enter_context(nc.psum_tensor(f"bank{i}", [P, 512], F32)) for i in range(8)]
        scores_ps, probs_t_bank, av_bank, misc = bank[0:2], bank[2:4], bank[4:6], bank[6:8]

        ident_in, x_in, consts_in, route_in, expert_in, mlp_in = (sem(n) for n in (
            "ident_in", "x_in", "consts_in", "route_in", "expert_in", "mlp_in"))
        attn_in, mask_in, rel_bias_out, out_done = (sem(n) for n in (
            "attn_in", "mask_in", "rel_bias_out", "out_done"))
        bias_in = [sem("bias_in0"), sem("bias_in1")]
        pool_consts, tables_made, ones_made = (sem(n) for n in ("pool_consts", "tables_made", "ones_made"))
        x_t_ps, x_t_sb, g_rep_made, router_ps, router_arg, router_exp = (sem(n) for n in (
            "x_t_ps", "x_t_sb", "g_rep_made", "router_ps", "router_arg", "router_exp"))
        coef_made, coef_t_ps, coef_t_sb, up_ps, leak_sb = (sem(n) for n in (
            "coef_made", "coef_t_ps", "coef_t_sb", "up_ps", "leak_sb"))
        hidden_made, spread_ps, hidden_ready, moe_ps = (sem(n) for n in (
            "hidden_made", "spread_ps", "hidden_ready", "moe_ps"))
        null_sq_made, null_r_made, null_kl_made, null_prod_made = (sem(n) for n in (
            "null_sq_made", "null_r_made", "null_kl_made", "null_prod_made"))
        null_cols_made, null_out_ps, null_out_sb = (sem(n) for n in (
            "null_cols_made", "null_out_ps", "null_out_sb"))
        m_var_ready, m_rstd_ready, m_norm_ready, m_t_ps, m_t_sb = (sem(n) for n in (
            "m_var_ready", "m_rstd_ready", "m_norm_ready", "m_t_ps", "m_t_sb"))
        m_h_ps, m_h_sb, m_out_ps, m_out_sb = (sem(n) for n in ("m_h_ps", "m_h_sb", "m_out_ps", "m_out_sb"))
        var_ready, rstd_ready, xn_ready, xn_t_ps, xn_t_sb = (sem(n) for n in (
            "var_ready", "rstd_ready", "xn_ready", "xn_t_ps", "xn_t_sb"))
        kvn_ps, kvn_sb, q_ps, q_sq_sb, sumsq_ready = (sem(n) for n in (
            "kvn_ps", "kvn_sb", "q_ps", "q_sq_sb", "sumsq_ready"))
        norm_ready, q_scaled, q_high, q_low, k_split_ready = (sem(n) for n in (
            "norm_ready", "q_scaled", "q_high", "q_low", "k_split_ready"))
        k_t_ps, keys_ready, q_t_ps, q_ready, null_ready = (sem(n) for n in (
            "k_t_ps", "keys_ready", "q_t_ps", "q_ready", "null_ready"))
        bias_ready, scores_ready, logits_ready, probs_ready = (sem(n) for n in (
            "bias_ready", "scores_ready", "logits_ready", "probs_ready"))
        probs_t_ready, copied_scalar, copied_vector, av_ready = (sem(n) for n in (
            "probs_t_ready", "copied_scalar", "copied_vector", "av_ready"))
        null_arg_ready, null_p_ready, group_ready, o_t_ps, o_t_sb = (sem(n) for n in (
            "null_arg_ready", "null_p_ready", "group_ready", "o_t_ps", "o_t_sb"))
        null_wt_sb, y_ps, y_sb_ready, y_var_ready, y_rstd_ready = (sem(n) for n in (
            "null_wt_sb", "y_ps", "y_sb_ready", "y_var_ready", "y_rstd_ready"))
        x_ready, vector_link = sem("x_ready"), sem("vector_link")

        def wait_copied(eng, layer, i):
            v = on_vector(i)
            eng.wait_ge(copied_vector if v else copied_scalar,
                        layer * copied_by(v, len(LOTS) - 1) + copied_by(v, i))

        def wait_units(eng, signal, layer, i):
            eng.wait_ge(signal, layer * UNITS + last_unit(i) + 1)

        spare_writes = {nc.vector: 0, nc.gpsimd: 0, nc.scalar: 0}

        def wait_apart(eng):
            spare_writes[eng] += 1
            column = spare_writes[eng] % spare.shape[2]
            if eng is nc.vector:
                eng.memset(spare[0:1, 0, column:column + 1], 0.0)
            elif eng is nc.gpsimd:
                one = rsqrt_power[0:1, 0:1]
                eng.tensor_tensor(spare[0:1, 1, column:column + 1], one, one, ALU.add)
            else:
                eng.copy(spare[0:1, 2, column:column + 1], ident[0:1, 0:1])

        block = ctx.enter_context(nc.Block())

        @block.sync
        def _(sp):
            sp.dma_start(ident[:], d["ident"]).then_inc(ident_in, 16)
            for b in range(BATCH):
                sp.dma_start(x_res[:].rearrange("p (r b) c -> p r b c", b=BATCH)[:, :, b, :],
                             d["x"][b].rearrange("(r p) c -> p r c", p=P)).then_inc(x_in, 16)
            for to, name in ((w_t, "wt_t"), (w_g, "wg_t"), (g_col, "cond_t")):
                sp.dma_start(to[:], d[name]).then_inc(route_in, 16)
            for to, name in ((pos, "pos"), (pair_sel, "pair_sel")):
                sp.dma_start(to[:], d[name]).then_inc(consts_in, 16)
            sp.dma_start(rank8[:], rows(d["rank8"])).then_inc(consts_in, 16)
            for to, routed, shared in ((w_gate, "w_gate", "sw_gate"), (w_up, "w_up", "sw_up")):
                sp.dma_start(to[:, 0:PAIRS, :].rearrange("h k (e m) -> h (k e) m", e=2),
                             d[routed].rearrange("e h m -> h e m")).then_inc(expert_in, 16)
                sp.dma_start(to[:, PAIRS, :], d[shared]).then_inc(expert_in, 16)
            sp.dma_start(w_down[:, 0:PAIRS, :],
                         d["w_down"].rearrange("(k e) m h -> (e m) k h", e=2)).then_inc(expert_in, 16)
            sp.dma_start(w_down[:, PAIRS, :], d["sw_down"]).then_inc(expert_in, 16)
            for b in range(2):
                sp.dma_start(null_v[b * DH:(b + 1) * DH, :], column(d["cond"][1])).then_inc(attn_in, 16)
            sp.dma_start(null_k[:], rows(d["cond"][0])).then_inc(attn_in, 16)
            sp.dma_start(w_q[:], d["w_q"].rearrange("l c n -> c l n")).then_inc(attn_in, 16)
            sp.dma_start(w_kvn[:, :, 0:KV], d["w_kv"].rearrange("l c n -> c l n")).then_inc(attn_in, 16)
            sp.dma_start(w_o[:].rearrange("p l (k n) -> p (l k) n", n=DIM),
                         d["w_o"].rearrange("l (k p) n -> p (l k) n", p=P)).then_inc(attn_in, 16)
            sp.dma_start(g_in[:, :, 0], d["g_in_t"]).then_inc(attn_in, 16)
            for to, name in ((null_bias, "null_bias"), (g_out, "g_out")):
                sp.dma_start(to[:].rearrange("p l n -> p (l n)"), rows(d[name])).then_inc(attn_in, 16)
            sp.dma_start(qk_scales[:, :, 0, :],
                         rows(d["q_scale"]).rearrange("p (l d) -> p l d", l=2)).then_inc(attn_in, 16)
            sp.dma_start(qk_scales[:, :, 1, :], rows(d["k_scale"]).rearrange("p (l d) -> p l d", l=2)
                         ).then_inc(attn_in, 16)
            for l in range(LAYERS):
                sp.dma_start(masks[:, l, :], rows(d["masks"][min(l, 1)])).then_inc(mask_in, 16)
            for t in range(ROWS):
                if t == 1:
                    sp.wait_ge(m_out_sb, 2)
                    for l in range(2):
                        skewed = bass.AP(m_bias, l * SEQ + P - 1, [[2 * SEQ + P, HEADS], [-1, P], [1, SEQ]])
                        sp.dma_start(rel_bias[l], skewed).then_inc(rel_bias_out, 16)
                    sp.wait_ge(x_ready, STEPS)
                if t >= 2:
                    sp.wait_ge(logits_ready, HEADS * BATCH * (t - 1))
                w = P * (t + 1)
                sp.dma_start(bias[:, t % 2, :, 0:w],
                             d["attn_bias"][:, P * t:P * (t + 1), 0:w].rearrange("h p c -> p h c")
                             ).then_inc(bias_in[t % 2], 16)
            sp.wait_ge(rel_bias_out, 32)
            for layer in range(1, LAYERS):
                for t in range(ROWS):
                    sp.wait_ge(logits_ready, UNITS * layer + HEADS * BATCH * (t - 1))
                    w = P * (t + 1)
                    sp.dma_start(bias[:, t % 2, :, 0:w],
                                 rel_bias[layer - 1, :, :, SEQ - w:SEQ].rearrange("h p c -> p h c")
                                 ).then_inc(bias_in[t % 2], 16)
            for s in range(STEPS):
                sp.wait_ge(x_ready, STEPS * LAYERS + s + 1)
                sp.dma_start(out[s % BATCH, (s // BATCH) * P:(s // BATCH + 1) * P, :], x_res[:, s, :]
                             ).then_inc(out_done, 16)
            sp.wait_ge(out_done, 16 * STEPS)

        @block.gpsimd
        def _(pool):
            for to, value in ((rsqrt_power[:], -0.5), (norm_power[:, 1:3, :], -0.5), (norm_power[:, 0, :], 0.0),
                              (k_factor[:, 0, :], DH ** -0.5), (null_v_cols[:], 0.0),
                              (values[:], 1.0), (m_bias[:], 0.0)):
                pool.memset(to, value).then_inc(pool_consts, 1)
            pool.wait_ge(pool_consts, POOL_CONSTS)

            def input_rstd(m):
                pool.wait_ge(var_ready, m.count(1, 1))
                pool.tensor_tensor(rstd[:], var_eps[:], rsqrt_power[:, 0:1], ALU.pow).then_inc(rstd_ready, 1)

            def normalize_positions(stage):
                pool.wait_ge(m_var_ready, stage + 1)
                pool.tensor_tensor(m_rstd[:], m_var[:], rsqrt_power[:], ALU.pow).then_inc(m_rstd_ready, 1)
                pool.wait_ge(m_rstd_ready, stage + 1)
                for i in range(STEPS):
                    pool.tensor_scalar(m_h[:, i, :], m_h[:, i, :], m_mv[:, i, 0:1], m_rstd[:, i:i + 1],
                                       ALU.subtract, ALU.mult).then_inc(m_norm_ready, 1)

            normalize_positions(0)
            normalize_positions(1)
            pool.wait_ge(null_sq_made, 1)
            for l in range(LAYERS):
                pool.tensor_tensor(null_r[:, l:l + 1], sumsq[:, 0:1], norm_power[:, l, 0:1], ALU.pow
                                   ).then_inc(null_r_made, 1)
            input_rstd(Step(None, 0))
            pool.wait_ge(null_kl_made, 1)
            for l in range(LAYERS):
                pool.tensor_tensor(null_prod[l][:], w_q[:, l, :].rearrange("p (h d) -> p h d", h=HEADS),
                                   null_kl[:, l:l + 1, :].to_broadcast([P, HEADS, DH]), ALU.mult
                                   ).then_inc(null_prod_made, 1)

            def output_rstd(n):
                pool.wait_ge(y_var_ready, n.count(1, 1))
                pool.tensor_tensor(y_rstd[:], y_var[:], rsqrt_power[:, 0:1], ALU.pow).then_inc(y_rstd_ready, 1)

            def queries(m, half):
                a, b = (0, 1 + HALF) if half == 0 else (1 + HALF, 1 + HEADS)
                h0, h1 = half * HALF, (half + 1) * HALF
                pool.wait_ge(sumsq_ready, m.count(2, half + 1))
                wait_apart(pool)
                power = pick(norm_power, m.of_layer())[:, a:b]
                pool.tensor_tensor(r_norm[:, a:b], sumsq[:, a:b], power, ALU.pow).then_inc(norm_ready, 1)
                pool.wait_ge(norm_ready, m.count(2, half + 1))
                pool.tensor_tensor(q_n[:, h0:h1, :], q_raw[:, h0:h1, :],
                                   r_norm[:, 1 + h0:1 + h1].unsqueeze(2).to_broadcast([P, HALF, DH]),
                                   ALU.mult).then_inc(q_scaled, 1)
                pool.wait_ge(q_scaled, m.count(2, half + 1))
                if m.layer is not None:
                    pool.wait_ge(q_t_ps, m.count(GROUPS, 0))
                wait_apart(pool)
                pool.tensor_scalar(q_split[:, h0:h1, 0, :], q_n[:, h0:h1, :], 1.0, 0.0, ALU.mult, ALU.add
                                   ).then_inc(q_high, 1)
                pool.wait_ge(q_high, m.count(2, half + 1))
                pool.tensor_tensor(q_split[:, h0:h1, 1, :], q_n[:, h0:h1, :],
                                   q_split[:, h0:h1, 0, :].bitcast(F32), ALU.subtract).then_inc(q_low, 1)

            def causal(layer, block):
                t = block % ROWS
                pool.wait_ge(bias_in[t % 2], layer * 32 + 16 * (block // 2 + 1))
                wait_apart(pool)
                diagonal = bias[:, t % 2, :, P * t:P * (t + 1)]
                pool.affine_select(out=diagonal, in_=diagonal, compare_op=ALU.is_ge, fill=masked, base=0,
                                   pattern=[[0, HEADS], [-1, P]], channel_multiplier=1
                                   ).then_inc(bias_ready, 1)

            def step(layer, s):
                m, after = Step(layer, s + 1), Step(layer, s + 2)
                if m.exists():
                    for half in range(2):
                        queries(m, half)
                if s >= 1:
                    output_rstd(Step(layer, s - 1))
                if after.exists():
                    input_rstd(after)
                if s % 2 == 1 and m.exists():
                    causal(layer, s // 2 + 1)

            input_rstd(Step(None, 1))
            for half in range(2):
                queries(Step(None, 0), half)
            masked = pool.to_reg(-BIG)
            causal(0, 0)
            for s in range(BEFORE_LOOP):
                step(0, s)
            with pool.Fori(0, LAYERS - 1) as layer:
                for s in range(BEFORE_LOOP, BEFORE_LOOP + STEPS):
                    step(layer, s)
            for s in range(BEFORE_LOOP, STEPS):
                step(LAYERS - 1, s)
            output_rstd(Step(LAYERS - 1, STEPS - 1))

        @block.scalar
        def _(act):
            for i, name in enumerate(("w0", "b0", "b1")):
                act.dma_start(m_rows[:, i].rearrange("p l c -> p (l c)"), rows(d[name])).then_inc(mlp_in, 16)
            act.dma_start(m_cols[:], d["m_cols"]).then_inc(mlp_in, 16)
            for to, name in ((m_w1, "w1"), (m_w2, "w2")):
                act.dma_start(to[:], d[name].rearrange("l c n -> c l n")).then_inc(mlp_in, 16)
            act.dma_start(m_b2[:], d["b2_t"]).then_inc(mlp_in, 16)
            for i in range(2):
                act.wait_ge(x_t_ps, i + 1)
                act.copy(tokens_t[:, 512 * i:512 * (i + 1)], bank[i][:]).then_inc(x_t_sb, 1)
            act.wait_ge(router_arg, 1)
            act.activation(route[:, 1], route[:, 0], ACT.Exp, scale=0.5).then_inc(router_exp, 1)

            def leaky_slope(j):
                act.wait_ge(up_ps, j + 1)
                if j >= 2:
                    act.wait_ge(hidden_made, j - 1)
                act.mul(leak[:, j % 2, :], bank[2 + j % 2][:], 0.01).then_inc(leak_sb, 1)

            def position_silu(stage):
                for l in range(2):
                    act.wait_ge(m_t_ps, 2 * stage + l + 1)
                    if stage == 1:
                        act.wait_ge(m_h_ps, 2)
                    act.activation(m_act[:, ROWS * l:ROWS * (l + 1), :].rearrange("p s c -> p (s c)"),
                                   bank[6 * stage + l][:], ACT.Silu,
                                   scale=m_cols[:, 2 * stage + l:2 * stage + l + 1]).then_inc(m_t_sb, 1)

            for j in range(2):
                leaky_slope(j)
            act.wait_ge(mlp_in, MLP_LOADS)
            position_silu(0)
            act.copy(q_ones[DH:P].rearrange("p b h c -> p (b h c)"),
                     ident[DH:P, DH:DH + 1].to_broadcast([P - DH, BATCH * HEADS * P])).then_inc(ones_made, 1)
            for i in range(2):
                act.wait_ge(coef_t_ps, i + 1)
                act.copy(coef_t[:, 512 * i:512 * (i + 1)], bank[i][0:2 * EXPERTS, :]).then_inc(coef_t_sb, 1)
            for j in range(2, CHUNKS):
                leaky_slope(j)
            position_silu(1)
            act.wait_ge(attn_in, ATTN_LOADS)

            def input_t(m):
                act.wait_ge(xn_t_ps, m.count(1, 1))
                if m.layer is not None:
                    act.wait_ge(q_ps, m.count(2, 0))
                wait_apart(act)
                act.activation(xn_t[:], misc[0][:, 0:P], ACT.Copy, scale=pick(g_in, m.of_layer())
                               ).then_inc(xn_t_sb, 1)

            def raw_queries(m, half):
                act.wait_ge(q_ps, m.count(2, half + 1))
                if m.layer is not None:
                    act.wait_ge(q_low, m.count(2, 0))
                raw, squares = (a[:, half * HALF:(half + 1) * HALF, :].rearrange("p h d -> p (h d)")
                                for a in (q_raw, q_n))
                act.copy(raw, misc[half][:])
                act.activation(squares, misc[half][:], ACT.Square).then_inc(q_sq_sb, 1)

            def queries_t(m, g):
                act.wait_ge(q_t_ps, m.count(GROUPS, g + 1))
                if m.c >= 2:
                    act.wait_ge(scores_ready, m.count(HEADS, -HEADS))
                b, hs = m.c % BATCH, slice(GROUP * g, GROUP * (g + 1))
                act.copy(q_ones[0:DH, b, hs, :].rearrange("p h c -> p (h c)"), misc[g % 2][0:DH, :])
                act.copy(q_stack[:, b, hs, :].rearrange("p h c -> p (h c)"), misc[g % 2][:]
                         ).then_inc(q_ready, 1)

            def output_t(n, i):
                act.wait_ge(o_t_ps, n.count(3, i + 1))
                if n.c >= 1:
                    act.wait_ge(y_ps, n.count(1, 0))
                act.copy(o_t[:, 4 * i:4 * i + 4, :].rearrange("p k c -> p (k c)"), misc[i][:]
                         ).then_inc(o_t_sb, 1)

            def exponentials(layer, i):
                first, n, w = lot(i)
                if i >= RING:
                    wait_units(act, probs_t_ready, layer, i - RING)
                for u in range(n):
                    s, h = divmod(first + u, HEADS)
                    cols = slice(w * u, w * (u + 1))
                    act.wait_ge(logits_ready, layer * UNITS + first + u + 1)
                    act.activation(probs[:, i % RING, cols], neg_logits[:, i % RING, cols], ACT.Exp,
                                   bias=neg_max[:, s % BATCH, h:h + 1], scale=-1.0).then_inc(probs_ready, 1)

            def null_exponentials(n, g):
                act.wait_ge(null_arg_ready, n.count(GROUPS, g + 1))
                act.activation(null_p[:, n.c % BATCH, GROUP * g:GROUP * (g + 1)],
                               null_arg[:, n.c % BATCH, GROUP * g:GROUP * (g + 1)], ACT.Exp, scale=-1.0
                               ).then_inc(null_p_ready, 1)

            def copy_probs(layer, i):
                _, n, w = lot(i)
                wait_units(act, probs_t_ready, layer, i)
                if i >= RING:
                    wait_units(act, av_ready, layer, i - RING)
                act.copy(probs_t[:, i % RING, 0:n * w], probs_t_bank[i % 2][:, 0:n * w]
                         ).then_inc(copied_scalar, 1)

            first = Step(None, 0)
            leaky_slope(CHUNKS)
            input_t(first)
            leaky_slope(CHUNKS + 1)
            raw_queries(first, 0)
            leaky_slope(CHUNKS + 2)
            raw_queries(first, 1)
            leaky_slope(CHUNKS + 3)
            leaky_slope(CHUNKS + 4)
            for g in range(GROUPS):
                queries_t(first, g)

            def step(layer, s):
                places = SCALAR_AT_WIDE if lot(lots_of(s)[0])[1] == 1 else SCALAR_AT_NARROW
                m, before = Step(layer, s + 1), Step(layer, s - 1)
                for i, k, h in heads_of(s):
                    if k == lot(i)[0]:
                        for j in due(i, T_LAG):
                            if not on_vector(j):
                                copy_probs(layer, j)
                        exponentials(layer, i)
                    if h % GROUP == 0 and k >= GROUP:
                        null_exponentials(Step(layer, (k - 1) // HEADS), (k - 1) % HEADS // GROUP)
                    if s >= 1:
                        for half in at(h, places["output_t"]):
                            output_t(before, half)
                    if not m.exists():
                        continue
                    if h == places["input_t"]:
                        input_t(m)
                    for half in at(h, places["raw_queries"]):
                        raw_queries(m, half)
                    for g in at(h, places["queries_t"]):
                        queries_t(m, g)

            for s in range(BEFORE_LOOP):
                step(0, s)
            with act.Fori(0, LAYERS - 1) as layer:
                for s in range(BEFORE_LOOP, BEFORE_LOOP + STEPS):
                    step(layer, s)
            for s in range(BEFORE_LOOP, STEPS):
                step(LAYERS - 1, s)
            for i in left(T_LAG):
                if not on_vector(i):
                    copy_probs(LAYERS - 1, i)
            null_exponentials(Step(LAYERS - 1, STEPS - 1), GROUPS - 1)
            for i in range(2):
                output_t(Step(LAYERS - 1, STEPS - 1), i)

        @block.vector
        def _(dve):
            links, base = [0], [0]

            def link(ins, apart=False):
                links[0] += 1
                ins.then_inc(vector_link, 1)
                dve.wait_ge(vector_link, base[0] + links[0])
                if apart:
                    wait_apart(dve)

            def position_stats():
                for i in range(STEPS):
                    ins = dve.bn_stats(m_stats[:, i, :], m_h[:, i, :])
                link(ins)
                for i in range(STEPS):
                    ins = dve.bn_aggr(m_mv[:, i, :], m_stats[:, i, :])
                link(ins)
                dve.tensor_scalar(m_var[:], m_mv[:, :, 1], EPS, None, ALU.add).then_inc(m_var_ready, 1)

            dve.wait_ge(route_in, 48)
            dve.tensor_copy(g_rep[:], g_col[:].unsqueeze(2).to_broadcast([GDIM, BATCH, P])
                            ).then_inc(g_rep_made, 1)
            dve.wait_ge(ident_in, 16)
            link(dve.tensor_copy(ident_r[:], ident[:]))
            dve.wait_ge(consts_in, 48)
            dve.tensor_copy(pair_sel_r, pair_sel)
            dve.wait_ge(mlp_in, MLP_LOADS)
            for i in range(STEPS):
                ins = dve.scalar_tensor_tensor(out=m_h[:, i, :], in0=m_rows[:, 0, i // ROWS, :],
                                               scalar=pos[:, i % ROWS:i % ROWS + 1],
                                               in1=m_rows[:, 1, i // ROWS, :], op0=ALU.mult, op1=ALU.add)
            link(ins)
            position_stats()
            over = [P, STEPS, EXPERTS]
            dve.wait_ge(router_ps, 1)
            logits = bank[7][:, 0:STEPS * EXPERTS].rearrange("p (s e) -> p s e", s=STEPS)
            link(dve.tensor_reduce(best[:, 0], logits, AX_X, ALU.max))
            dve.tensor_tensor(route[:, 0], logits, best[:, 0].unsqueeze(2).to_broadcast(over), ALU.subtract
                              ).then_inc(router_arg, 1)
            dve.wait_ge(router_exp, 1)
            link(dve.tensor_reduce(best[:, 0], route[:, 1], AX_X, ALU.add))
            link(dve.reciprocal(best[:, 1], best[:, 0]))
            link(dve.tensor_tensor(route[:, 0], route[:, 1], best[:, 1].unsqueeze(2).to_broadcast(over),
                                   ALU.mult))
            ranks = rank8[:].unsqueeze(1).to_broadcast(over)
            for i, rest in enumerate((route[:, 0], route[:, 3])):
                link(dve.tensor_reduce(best[:, 0], rest, AX_X, ALU.max))
                link(dve.tensor_tensor(route[:, 1], rest, best[:, 0].unsqueeze(2).to_broadcast(over),
                                       ALU.is_equal))
                link(dve.tensor_tensor(route[:, 1], route[:, 1], ranks, ALU.mult))
                link(dve.tensor_reduce(best[:, 1], route[:, 1], AX_X, ALU.max))
                link(dve.tensor_tensor(route[:, 2 - i], route[:, 1],
                                       best[:, 1].unsqueeze(2).to_broadcast(over), ALU.is_equal))
                if i == 0:
                    link(dve.scalar_tensor_tensor(out=route[:, 3], in0=route[:, 2], scalar=-2.0,
                                                  in1=route[:, 0], op0=ALU.mult, op1=ALU.add))
            link(dve.tensor_tensor(route[:, 3], route[:, 1], route[:, 2], ALU.add))
            link(dve.tensor_tensor(route[:, 1], route[:, 0], route[:, 3], ALU.mult))
            link(dve.tensor_reduce(best[:, 0], route[:, 1], AX_X, ALU.add))
            link(dve.tensor_scalar(best[:, 1], best[:, 0], 1e-20, None, ALU.add))
            link(dve.reciprocal(best[:, 2], best[:, 1]))
            link(dve.tensor_tensor(route[:, 2], route[:, 1], best[:, 2].unsqueeze(2).to_broadcast(over),
                                   ALU.mult))
            link(dve.tensor_copy(coef_split[:, :, 0, :], route[:, 2]))
            dve.tensor_tensor(coef_split[:, :, 1, :], route[:, 2], coef_split[:, :, 0, :].bitcast(F32),
                              ALU.subtract).then_inc(coef_made, 1)

            def gate_times_up(j):
                half, c = divmod(j, CHUNKS)
                dve.wait_ge(leak_sb, j + 1)
                if j >= 1:
                    dve.wait_ge(hidden_made, j)
                link(dve.tensor_tensor(gated, bank[2 + j % 2][:], leak[:, j % 2, :], ALU.max))
                dve.tensor_tensor(hidden[c][:, 512 * half:512 * (half + 1)], gated, bank[4 + j % 2][:],
                                  ALU.mult).then_inc(hidden_made, 1)

            def times_weights(j):
                half, c = divmod(j, PAIRS)
                dve.wait_ge(spread_ps, j + 1)
                dve.wait_ge(hidden_made, half * CHUNKS + c + 1)
                part = hidden[c][:, 512 * half:512 * (half + 1)]
                dve.tensor_tensor(part, part, bank[j % 2][:], ALU.mult).then_inc(hidden_ready, 1)

            def add_experts(s):
                dve.wait_ge(moe_ps, s + 1)
                dve.tensor_tensor(x_res[:, s, :], x_res[:, s, :], bank[s % 2][:, 0:DIM], ALU.add
                                  ).then_inc(x_ready, 1)

            gate_times_up(0)
            gate_times_up(1)
            for l in range(2):
                dve.wait_ge(m_h_ps, l + 1)
                dve.tensor_tensor(m_h[:, ROWS * l:ROWS * (l + 1), :],
                                  bank[6 + l][:].rearrange("p (s c) -> p s c", s=ROWS),
                                  m_rows[:, 2, l:l + 1, :].to_broadcast([P, ROWS, DIM]), ALU.add
                                  ).then_inc(m_h_sb, 1)
            dve.wait_ge(m_h_sb, 2)
            position_stats()
            for j in range(2, CHUNKS):
                gate_times_up(j)
            times_weights(0)
            times_weights(1)
            dve.wait_ge(attn_in, ATTN_LOADS)
            dve.wait_ge(mask_in, 16 * LAYERS)
            dve.wait_ge(pool_consts, POOL_CONSTS)
            for l in range(2):
                link(dve.scalar_tensor_tensor(out=k_factor[:, 1 + l, :], in0=qk_scales[:, l, 0, :],
                                              scalar=Q_SCALE, in1=qk_scales[:, l, 1, :],
                                              op0=ALU.mult, op1=ALU.mult))
            link(dve.tensor_tensor(k_sq[:], null_k[:], null_k[:], ALU.mult))
            link(dve.tensor_reduce(sumsq[:, 0:1], k_sq[:], AX_X, ALU.add))
            dve.tensor_scalar(sumsq[:, 0:1], sumsq[:, 0:1], NORM_FLOOR, None, ALU.max
                              ).then_inc(null_sq_made, 1)
            for i in range(2):
                cols = slice(i, (STEPS - 1) * (HEADS + 2) + i + 1, HEADS + 2)
                ins = dve.tensor_copy(null_v_cols[i * DH:(i + 1) * DH, cols],
                                      null_v[i * DH:(i + 1) * DH, :].to_broadcast([DH, STEPS]))
            ins.then_inc(null_cols_made, 1)
            times_weights(2)
            times_weights(3)
            dve.wait_ge(coef_t_sb, 2)
            dve.tensor_scalar(k_split[:, 1, 1], ident[:, 0:DH], 0.0, None, ALU.mult)
            dve.wait_ge(null_r_made, LAYERS)
            for l in range(LAYERS):
                ins = dve.scalar_tensor_tensor(out=null_kl[:, l, :], in0=null_k[:], scalar=null_r[:, l:l + 1],
                                               in1=k_factor[:, l, :], op0=ALU.mult, op1=ALU.mult)
            ins.then_inc(null_kl_made, 1)
            def input_stats(m):
                dve.wait_ge(x_ready, m.count(1, 1))
                if m.layer is not None or m.c >= 1:
                    dve.wait_ge(xn_ready, m.count(1, 0))
                link(dve.bn_stats(stats[:], x_res[:, m.c % STEPS, :]), apart=True)
                link(dve.bn_aggr(mv[:], stats[:]))
                dve.tensor_scalar(var_eps[:], mv[:, 1:2], EPS, None, ALU.add).then_inc(var_ready, 1)

            def input_norm(m):
                dve.wait_ge(rstd_ready, m.count(1, 1))
                if m.layer is not None or m.c >= 1:
                    dve.wait_ge(xn_t_ps, m.count(1, 0))
                dve.tensor_scalar(xn[:], x_res[:, m.c % STEPS, :], mv[:, 0:1], rstd[:], ALU.subtract, ALU.mult
                                  ).then_inc(xn_ready, 1)

            def keys_values(m):
                dve.wait_ge(kvn_ps, m.count(1, 1))
                dve.tensor_copy(kvn[:], misc[1][:, 0:PROJ]).then_inc(kvn_sb, 1)
                dve.wait_ge(kvn_sb, m.count(1, 1))
                link(dve.tensor_tensor(k_sq[:], kvn[:, 0:DH], kvn[:, 0:DH], ALU.mult))
                link(dve.tensor_reduce(sumsq[:, 0:1], k_sq[:], AX_X, ALU.add))

            def query_squares(m, half):
                a, b = (0, 1 + HALF) if half == 0 else (1 + HALF, 1 + HEADS)
                dve.wait_ge(q_sq_sb, m.count(2, half + 1))
                squares = q_n[:, half * HALF:(half + 1) * HALF, :]
                link(dve.tensor_reduce(sumsq[:, 1 + half * HALF:b], squares, AX_X, ALU.add))
                dve.tensor_scalar(sumsq[:, a:b], sumsq[:, a:b], NORM_FLOOR, None, ALU.max
                                  ).then_inc(sumsq_ready, 1)

            def split_keys(m):
                if m.c >= STEPS:
                    dve.wait_ge(av_ready, m.count(HEADS, -HEADS))
                dve.tensor_copy(values[:, m.c % BATCH, m.c % STEPS // BATCH, 0:DH], kvn[:, DH:KV])
                dve.wait_ge(norm_ready, m.count(2, 1))
                link(dve.scalar_tensor_tensor(out=k_n[:], in0=kvn[:, 0:DH], scalar=r_norm[:, 0:1],
                                              in1=pick(k_factor, m.of_layer()), op0=ALU.mult, op1=ALU.mult))
                twice = k_n[:].unsqueeze(1).to_broadcast([P, 2, DH])
                if m.layer is not None:
                    dve.wait_ge(k_t_ps, m.count(1, 0))
                link(dve.tensor_copy(k_split[:, 0], twice))
                dve.tensor_tensor(k_split[:, 1, 0], k_n[:], k_split[:, 0, 0].bitcast(F32), ALU.subtract
                                  ).then_inc(k_split_ready, 1)

            def null_scores(m):
                dve.wait_ge(norm_ready, m.count(2, 2))
                link(dve.tensor_tensor(null_t[:], kvn[:, KV:PROJ], r_norm[:, 1:1 + HEADS], ALU.mult))
                dve.scalar_tensor_tensor(out=neg_null[:, m.c % BATCH, :], in0=null_t[:], scalar=-1.0,
                                         in1=pick(null_bias, m.of_layer()), op0=ALU.mult, op1=ALU.subtract
                                         ).then_inc(null_ready, 1)

            def keys_t(m):
                t = m.c % STEPS // BATCH
                dve.wait_ge(k_t_ps, m.count(1, 1))
                if m.c >= STEPS:
                    dve.wait_ge(scores_ready, m.count(HEADS, -HEADS))
                b, cols = m.c % BATCH, slice(P * t, P * (t + 1))
                link(dve.tensor_copy(keys[:, b, :, cols],
                                     misc[1][:, 0:2 * P].rearrange("p (i c) -> p i c", i=2)))
                dve.tensor_scalar(keys[DH:DH + 1, b, 1, cols],
                                  pick(masks, m.of_layer())[DH:DH + 1, SEQ * b + P * t:SEQ * b + P * (t + 1)],
                                  -1.0, BIG, ALU.add, ALU.mult).then_inc(keys_ready, 1)

            def logits(layer, i):
                first, n, w = lot(i)
                s = first // HEADS
                if first % HEADS == 0:
                    dve.wait_ge(bias_ready, layer * ROWS + s // BATCH + 1)
                    dve.wait_ge(null_ready, Step(layer, s).count(1, 1))
                wait_units(dve, scores_ready, layer, i)
                if i >= RING:
                    wait_units(dve, probs_ready, layer, i - RING)
                wait_apart(dve)
                for u in range(n):
                    h, cols = first % HEADS + u, slice(w * u, w * (u + 1))
                    dve.tensor_tensor_reduce(neg_logits[:, i % RING, cols], scores_ps[i % 2][:, cols],
                                             bias[:, s // BATCH % 2, h, 0:w], -1.0,
                                             neg_null[:, s % BATCH, h:h + 1], ALU.add, ALU.min,
                                             neg_max[:, s % BATCH, h:h + 1]).then_inc(logits_ready, 1)

            def copy_probs(layer, i):
                _, n, w = lot(i)
                wait_units(dve, probs_t_ready, layer, i)
                if i >= RING:
                    wait_units(dve, av_ready, layer, i - RING)
                dve.tensor_copy(probs_t[:, i % RING, 0:n * w], probs_t_bank[i % 2][:, 0:n * w]
                                ).then_inc(copied_vector, 1)

            def null_arguments(n, g):
                b, hs = n.c % BATCH, slice(GROUP * g, GROUP * (g + 1))
                dve.wait_ge(logits_ready, n.count(HEADS, GROUP * (g + 1)))
                dve.tensor_tensor(null_arg[:, b, hs], neg_null[:, b, hs], neg_max[:, b, hs], ALU.subtract
                                  ).then_inc(null_arg_ready, 1)

            def normalize_group(n, g):
                b, hs = n.c % BATCH, slice(GROUP * g, GROUP * (g + 1))
                av = av_bank[g % 2][:, 0:GROUP * VW].rearrange("p (h c) -> p h c", h=GROUP)
                dve.wait_ge(null_p_ready, n.count(GROUPS, g + 1))
                dve.wait_ge(av_ready, n.count(HEADS, GROUP * (g + 1)))
                link(dve.tensor_tensor(denom[:, hs], av[:, :, DH], null_p[:, b, hs], ALU.add))
                link(dve.reciprocal(r_denom[:, hs], denom[:, hs]))
                if n.c >= 1:
                    dve.wait_ge(o_t_ps, n.count(3, 0))
                dve.tensor_tensor(null_w[:, hs], null_p[:, b, hs], r_denom[:, hs], ALU.mult)
                dve.tensor_tensor(o_n[:, hs, :], av[:, :, 0:DH],
                                  r_denom[:, hs].unsqueeze(2).to_broadcast([P, GROUP, DH]), ALU.mult
                                  ).then_inc(group_ready, 1)

            def null_weights_t(n):
                dve.wait_ge(o_t_ps, n.count(3, 3))
                dve.tensor_copy(null_wt[:], misc[0][0:HEADS, 0:P]).then_inc(null_wt_sb, 1)

            def output_stats(n):
                dve.wait_ge(y_ps, n.count(1, 1))
                dve.tensor_copy(y_sb[:], misc[0][:, P:P + DIM]).then_inc(y_sb_ready, 1)
                dve.wait_ge(y_sb_ready, n.count(1, 1))
                link(dve.bn_stats(y_stats[:], y_sb[:]), apart=True)
                link(dve.bn_aggr(y_mv[:], y_stats[:]))
                dve.tensor_scalar(y_var[:], y_mv[:, 1:2], EPS, None, ALU.add).then_inc(y_var_ready, 1)

            def add_output(n):
                dve.wait_ge(y_rstd_ready, n.count(1, 1))
                link(dve.tensor_scalar(y_c[:], y_sb[:], y_mv[:, 0:1], y_rstd[:], ALU.subtract, ALU.mult))
                link(dve.tensor_tensor(y_c[:], y_c[:], pick(g_out, n.of_layer()), ALU.mult))
                tile = x_res[:, n.c % STEPS, :]
                dve.tensor_tensor(tile, tile, y_c[:], ALU.add).then_inc(x_ready, 1)

            dve.wait_ge(x_in, 32)
            add_experts(0)
            first = Step(None, 0)
            input_stats(first)
            add_experts(1)
            for l in range(2):
                dve.wait_ge(m_out_ps, l + 1)
                dve.tensor_scalar(m_bias[:, l * SEQ:(l + 1) * SEQ], bank[6 + l][0:HEADS, :], m_b2[:, l:l + 1],
                                  None, ALU.add).then_inc(m_out_sb, 1)
            add_experts(2)
            add_experts(3)

            input_norm(first)
            for l in range(LAYERS):
                dve.wait_ge(null_prod_made, l + 1)
                ins = dve.tensor_reduce(w_kvn[:, l, KV:PROJ], null_prod[l][:], AX_X, ALU.add)
            ins.then_inc(tables_made, 1)
            gate_times_up(CHUNKS)
            input_stats(Step(None, 1))
            gate_times_up(CHUNKS + 1)
            keys_values(first)
            query_squares(first, 0)
            gate_times_up(CHUNKS + 2)
            query_squares(first, 1)
            gate_times_up(CHUNKS + 3)
            split_keys(first)
            gate_times_up(CHUNKS + 4)
            times_weights(PAIRS)
            times_weights(PAIRS + 1)
            input_norm(Step(None, 1))
            keys_t(first)
            for j in range(PAIRS + 2, 2 * PAIRS):
                times_weights(j)
            null_scores(first)
            for s in range(STEPS // 2, STEPS):
                add_experts(s)

            def step(layer, s):
                places = VECTOR_AT_WIDE if lot(lots_of(s)[0])[1] == 1 else VECTOR_AT_NARROW
                m, after, before = Step(layer, s + 1), Step(layer, s + 2), Step(layer, s - 1)
                for i, k, h in heads_of(s):
                    if k == lot(i)[0]:
                        logits(layer, i)
                        for j in due(i, T_LAG):
                            if on_vector(j):
                                copy_probs(layer, j)
                    if h % GROUP == GROUP - 1:
                        null_arguments(Step(layer, s), h // GROUP)
                    if h % GROUP == 1 and k >= 2 * GROUP:
                        done = k - 2 * GROUP
                        normalize_group(Step(layer, done // HEADS), done % HEADS // GROUP)
                    if s == 0 and h == places["null_weights_t"]:
                        dve.wait_ge(null_out_ps, 1)
                        dve.tensor_copy(null_out[:].rearrange("h l n -> h (l n)"),
                                        misc[0][0:HEADS, 0:LAYERS * DIM]).then_inc(null_out_sb, 1)
                    if s >= 1:
                        if h == places["null_weights_t"]:
                            null_weights_t(before)
                        if h == places["output_stats"]:
                            output_stats(before)
                        if h == places["add_output"]:
                            add_output(before)
                    if m.exists():
                        if h == places["keys_values"]:
                            keys_values(m)
                        for half in at(h, places["query_squares"]):
                            query_squares(m, half)
                        if h == places["split_keys"]:
                            split_keys(m)
                        if h == places["keys_t"]:
                            keys_t(m)
                        if h == places["null_scores"]:
                            null_scores(m)
                    if after.exists():
                        if h == places["input_stats"]:
                            input_stats(after)
                        if h == places["input_norm"]:
                            input_norm(after)

            for s in range(BEFORE_LOOP):
                step(0, s)
            before_loop = links[0]
            with dve.Fori(0, LAYERS - 1) as layer:
                base[0], links[0] = layer * LINKS_LAYER + before_loop, 0
                for s in range(BEFORE_LOOP, BEFORE_LOOP + STEPS):
                    step(layer, s)
                assert links[0] == LINKS_LAYER, links
            base[0], links[0] = (LAYERS - 1) * LINKS_LAYER + before_loop, 0
            for s in range(BEFORE_LOOP, STEPS):
                step(LAYERS - 1, s)
            for i in left(T_LAG):
                if on_vector(i):
                    copy_probs(LAYERS - 1, i)
            last = Step(LAYERS - 1, STEPS - 1)
            normalize_group(last, GROUPS - 2)
            normalize_group(last, GROUPS - 1)
            null_weights_t(last)
            output_stats(last)
            add_output(last)

        @block.tensor
        def _(pe):
            def mm(to, stationary, moving, start=True, stop=True):
                return pe.matmul(to, stationary, moving, start=start, stop=stop, skip_group_check=True)

            pe.wait_ge(ident_in, 16)
            pe.wait_ge(x_in, 32)
            for s in range(STEPS):
                ins = pe.transpose(bank[s // 4][:, P * (s % 4):P * (s % 4 + 1)], x_res[:, s, :], ident[:])
                if s % 4 == 3:
                    ins.then_inc(x_t_ps, 1)
            pe.wait_ge(x_t_sb, 2)
            pe.wait_ge(route_in, 48)
            pe.wait_ge(g_rep_made, 1)
            for s in range(STEPS):
                to = bank[7][:, EXPERTS * s:EXPERTS * (s + 1)]
                mm(to, tokens_t[:, P * s:P * (s + 1)], w_t[:], stop=False)
                ins = mm(to, g_rep[:, s % BATCH, :], w_g[:], start=False)
            ins.then_inc(router_ps, 1)

            def gate_up(j):
                half, c = divmod(j, CHUNKS)
                if j >= 2:
                    pe.wait_ge(hidden_made, j - 1)
                moving = tokens_t[:, 512 * half:512 * (half + 1)]
                mm(bank[2 + j % 2][:], w_gate[:, c, :], moving)
                mm(bank[4 + j % 2][:], w_up[:, c, :], moving).then_inc(up_ps, 1)

            def coefficients_t():
                pe.wait_ge(coef_made, 1)
                pe.wait_ge(m_t_sb, 2)
                for s in range(STEPS):
                    ins = pe.transpose(bank[s // 4][0:2 * EXPERTS, P * (s % 4):P * (s % 4 + 1)],
                                       coef_split[:, s].rearrange("p i e -> p (i e)").bitcast(F32), ident[:])
                    if s % 4 == 3:
                        ins.then_inc(coef_t_ps, 1)

            def spread(j):
                half, c = divmod(j, PAIRS)
                if half == 0 and c >= 2:
                    pe.wait_ge(hidden_ready, j - 1)
                elif half == 0:
                    pe.wait_ge(consts_in, 48)
                    pe.wait_ge(coef_t_sb, 2)
                elif c < 2:
                    pe.wait_ge(x_ready, c + 3)
                else:
                    pe.wait_ge(hidden_ready, j - 1)
                mm(bank[j % 2][:], pair_sel_r[:, P * c:P * (c + 1)], coef_t[:, 512 * half:512 * (half + 1)]
                   ).then_inc(spread_ps, 1)

            def down(s):
                half, i = divmod(s, STEPS // 2)
                if i == 0:
                    pe.wait_ge(hidden_ready, (half + 1) * PAIRS)
                    pe.wait_ge(hidden_made, (half + 1) * CHUNKS)
                elif i >= 2:
                    pe.wait_ge(x_ready, s - 1)
                for c in range(CHUNKS):
                    ins = mm(bank[s % 2][:, 0:DIM], hidden[c][:, P * s:P * (s + 1)], w_down[:, c, :],
                             start=(c == 0), stop=(c == CHUNKS - 1))
                ins.then_inc(moe_ps, 1)

            def positions_t(stage):
                for l in range(2):
                    pe.wait_ge(m_norm_ready, STEPS * stage + ROWS * (l + 1))
                    for i in range(ROWS):
                        ins = pe.transpose(bank[6 * stage + l][:, P * i:P * (i + 1)], m_h[:, ROWS * l + i, :],
                                           ident[:])
                    ins.then_inc(m_t_ps, 1)

            pe.wait_ge(expert_in, 96)
            gate_up(0)
            gate_up(1)
            pe.wait_ge(mlp_in, MLP_LOADS)
            positions_t(0)
            for l in range(2):
                pe.wait_ge(m_t_sb, l + 1)
                if l == 1:
                    pe.wait_ge(router_arg, 1)
                for i in range(ROWS):
                    ins = mm(bank[6 + l][:, P * i:P * (i + 1)], m_act[:, ROWS * l + i, :], m_w1[:, l, :])
                ins.then_inc(m_h_ps, 1)
            coefficients_t()
            for j in range(2, CHUNKS):
                gate_up(j)
            for j in range(PAIRS):
                spread(j)
            pe.wait_ge(m_h_sb, 2)
            positions_t(1)
            down(0)
            down(1)
            for l in range(2):
                pe.wait_ge(m_t_sb, 2 + l + 1)
                mm(bank[6 + l][0:HEADS, :], m_w2[:, l, :],
                   m_act[:, ROWS * l:ROWS * (l + 1), :].rearrange("p s c -> p (s c)")).then_inc(m_out_ps, 1)
            down(2)
            down(3)

            def input_t(m):
                pe.wait_ge(xn_ready, m.count(1, 1))
                if m.layer is not None:
                    pe.wait_ge(q_ready, m.count(GROUPS, 0))
                pe.transpose(misc[0][:, 0:P], xn[:], ident[:]).then_inc(xn_t_ps, 1)

            def project_kvn(m):
                pe.wait_ge(xn_t_sb, m.count(1, 1))
                mm(misc[1][:, 0:PROJ], xn_t[:], pick(w_kvn, m.of_layer())).then_inc(kvn_ps, 1)

            def project_q(m, half):
                if half == 0:
                    pe.wait_ge(xn_t_sb, m.count(1, 1))
                else:
                    pe.wait_ge(kvn_sb, m.count(1, 1))
                mm(misc[half][:], xn_t[:], pick(w_q, m.of_layer())[:, 512 * half:512 * (half + 1)]
                   ).then_inc(q_ps, 1)

            def keys_t(m, before):
                pe.wait_ge(k_split_ready, m.count(1, 1))
                if before is None:
                    pe.wait_ge(q_sq_sb, m.count(2, 2))
                else:
                    pe.wait_ge(o_t_sb, before.count(2, 2))
                for i in range(2):
                    ins = mm(misc[1][:, P * i:P * (i + 1)], k_split[:, i].rearrange("p i d -> p (i d)"),
                             ident_r[:])
                ins.then_inc(k_t_ps, 1)

            def queries_t(m, g, before):
                pe.wait_ge(q_low, m.count(2, g // 2 + 1))
                if g >= 2:
                    pe.wait_ge(q_ready, m.count(GROUPS, g - 1))
                elif g == 1:
                    pe.wait_ge(keys_ready, m.count(1, 1))
                elif before is None:
                    pe.wait_ge(q_sq_sb, m.count(2, 1))
                    if m.c == 1:
                        pe.wait_ge(null_out_sb, 1)
                else:
                    pe.wait_ge(y_sb_ready, before.count(1, 1))
                for i in range(GROUP):
                    ins = mm(misc[g % 2][:, P * i:P * (i + 1)],
                             q_split[:, GROUP * g + i].rearrange("p i d -> p (i d)"), ident_r[:])
                ins.then_inc(q_t_ps, 1)

            def scores(layer, i):
                first, n, w = lot(i)
                s, h0 = divmod(first, HEADS)
                step, b = Step(layer, s), s % BATCH
                if h0 == 0:
                    pe.wait_ge(keys_ready, step.count(1, 1))
                if h0 % GROUP == 0:
                    pe.wait_ge(q_ready, step.count(GROUPS, h0 // GROUP + 1))
                if i >= 2:
                    wait_units(pe, logits_ready, layer, i - 2)
                for u in range(n):
                    h, to = h0 + u, scores_ps[i % 2][:, w * u:w * (u + 1)]
                    mm(to, q_stack[:, b, h, :], keys[:, b, 0, 0:w], stop=False)
                    ins = mm(to, q_ones[:, b, h, :], keys[:, b, 1, 0:w], start=False)
                ins.then_inc(scores_ready, n)

            def probs_transposed(layer, i):
                _, n, w = lot(i)
                wait_units(pe, probs_ready, layer, i)
                if i >= 2:
                    wait_copied(pe, layer, i - 2)
                for c in range(n * w // P):
                    ins = pe.transpose(probs_t_bank[i % 2][:, P * c:P * (c + 1)],
                                       probs[:, i % RING, P * c:P * (c + 1)], ident[:])
                ins.then_inc(probs_t_ready, n)

            def times_values(layer, i):
                first, n, w = lot(i)
                s, h0 = divmod(first, HEADS)
                wait_copied(pe, layer, i)
                if h0 % GROUP == 0 and first >= 2 * GROUP:
                    pe.wait_ge(group_ready, layer * (STEPS * GROUPS) + first // GROUP - 1)
                for u in range(n):
                    h = h0 + u
                    to = av_bank[h // GROUP % 2][:, VW * (h % GROUP):VW * (h % GROUP + 1)]
                    blocks = w // P
                    for c in range(blocks):
                        ins = mm(to, probs_t[:, i % RING, w * u + P * c:w * u + P * (c + 1)],
                                 values[:, s % BATCH, c, :], start=(c == 0), stop=(c == blocks - 1))
                ins.then_inc(av_ready, n)

            def outputs_t(n, i):
                pe.wait_ge(group_ready, n.count(GROUPS, 2 * i + 2))
                if Step(n.layer, n.c + 2).exists():
                    pe.wait_ge(q_sq_sb, Step(n.layer, n.c + 2).count(2, i + 1))
                elif Step(n.layer, n.c + 1).exists():
                    pe.wait_ge(q_ready, n.count(GROUPS, 2 * GROUPS))
                else:
                    pe.wait_ge(y_sb_ready, n.count(1, 0))
                for c in range(4):
                    two = o_n[:, 2 * (4 * i + c):2 * (4 * i + c) + 2, :].rearrange("p h d -> p (h d)")
                    ins = pe.transpose(misc[i][:, P * c:P * (c + 1)], two, ident[:])
                ins.then_inc(o_t_ps, 1)

            def null_weights_t(n):
                pe.wait_ge(o_t_sb, n.count(2, 1))
                pe.transpose(misc[0][0:HEADS, 0:P], null_w[:], ident[:]).then_inc(o_t_ps, 1)

            def project_output(n):
                pe.wait_ge(o_t_sb, n.count(2, 2))
                pe.wait_ge(null_wt_sb, n.count(1, 1))
                to, w = misc[0][:, P:P + DIM], pick(w_o, n.of_layer())
                for c in range(STEPS):
                    mm(to, o_t[:, c, :], w[:, DIM * c:DIM * (c + 1)], start=(c == 0), stop=False)
                mm(to, null_wt[:], pick(null_out, n.of_layer()), start=False).then_inc(y_ps, 1)

            first = Step(None, 0)
            gate_up(CHUNKS)
            pe.wait_ge(m_out_sb, 2)
            input_t(first)
            gate_up(CHUNKS + 1)
            pe.wait_ge(tables_made, 1)
            project_kvn(first)
            project_q(first, 0)
            gate_up(CHUNKS + 2)
            project_q(first, 1)
            gate_up(CHUNKS + 3)
            gate_up(CHUNKS + 4)
            spread(PAIRS)
            spread(PAIRS + 1)
            keys_t(first, None)
            spread(PAIRS + 2)
            spread(PAIRS + 3)
            for i in range(GROUPS):
                down(STEPS // 2 + i)
                queries_t(first, i, None)
            pe.wait_ge(x_ready, STEPS)
            pe.wait_ge(ones_made, 1)

            def null_outputs():
                pe.wait_ge(null_cols_made, 1)
                pe.wait_ge(q_sq_sb, 3)
                for l in range(LAYERS):
                    for c in range(STEPS):
                        ins = mm(misc[0][0:HEADS, DIM * l:DIM * (l + 1)],
                                 null_v_cols[:, HEADS * c:HEADS * (c + 1)],
                                 w_o[:, l, DIM * c:DIM * (c + 1)], start=(c == 0), stop=(c == STEPS - 1))
                ins.then_inc(null_out_ps, 1)

            def step(layer, s):
                places = TENSOR_AT_WIDE if lot(lots_of(s)[0])[1] == 1 else TENSOR_AT_NARROW
                m = Step(layer, s + 1)
                before = Step(layer, s - 1) if s >= 1 else None
                for i, k, h in heads_of(s):
                    if k == lot(i)[0]:
                        scores(layer, i)
                        for j in due(i, T_LAG):
                            probs_transposed(layer, j)
                        for j in due(i, AV_LAG):
                            times_values(layer, j)
                    if before is None:
                        if h == places["outputs_t"][0]:
                            null_outputs()
                    else:
                        for half in at(h, places["outputs_t"]):
                            outputs_t(before, half)
                        if h == places["null_weights_t"]:
                            null_weights_t(before)
                        if h == places["project_output"]:
                            project_output(before)
                    if not m.exists():
                        continue
                    if h == places["input_t"]:
                        input_t(m)
                    if h == places["project_kvn"]:
                        project_kvn(m)
                    for half in at(h, places["project_q"]):
                        project_q(m, half)
                    if h == places["keys_t"]:
                        keys_t(m, before)
                    for g in at(h, places["queries_t"]):
                        queries_t(m, g, before)

            for s in range(BEFORE_LOOP):
                step(0, s)
            with pe.Fori(0, LAYERS - 1) as layer:
                for s in range(BEFORE_LOOP, BEFORE_LOOP + STEPS):
                    step(layer, s)
            for s in range(BEFORE_LOOP, STEPS):
                step(LAYERS - 1, s)
            for i in left(T_LAG):
                probs_transposed(LAYERS - 1, i)
            for i in left(AV_LAG):
                times_values(LAYERS - 1, i)
            last = Step(LAYERS - 1, STEPS - 1)
            outputs_t(last, 0)
            outputs_t(last, 1)
            null_weights_t(last)
            project_output(last)


def kernel(**inputs):
    import numpy as np
    import concourse.bacc as bacc
    from concourse.bass_utils import run_bass_kernel_spmd

    a = {name: np.asarray(v) for name, v in inputs.items()}
    L0 = {n: a["L0_cond_" + n] for n in (
        "wt", "wg", "w_gate", "w_up", "w_down", "sw_gate", "sw_up", "sw_down")}

    def stacked(*names):
        return np.stack([a[n] for n in names])

    def later(name):
        return stacked(f"L2_cond_{name}", f"L3_cond_{name}")

    given = {
        "x": a["x"], "cond": a["cond_64"], "cond_t": a["cond_64"].T, "attn_bias": a["fside_16xSxS_0"],
        "masks": stacked("mask_BxS_bk0", "mask_BxS_bf1").reshape(2, BATCH * SEQ),
        "wt_t": L0["wt"].T, "wg_t": L0["wg"].T,
        "w_gate": L0["w_gate"], "w_up": L0["w_up"], "w_down": L0["w_down"],
        "sw_gate": L0["sw_gate"], "sw_up": L0["sw_up"], "sw_down": L0["sw_down"],
        "g_in_t": stacked("L1_cond_g_in", "L2_cond_g_norm", "L3_cond_g_norm").T,
        "g_out": stacked("L1_cond_g_out", "L2_cond_g_out", "L3_cond_g_out").reshape(-1),
        "null_bias": stacked("L1_cond_null_attn_bias", "L2_cond_null_attn_bias",
                             "L3_cond_null_attn_bias").reshape(-1),
        "w_q": stacked("L1_cond_Wq", "L2_cond_Wq", "L3_cond_Wq"),
        "w_kv": stacked("L1_cond_Wkv", "L2_cond_Wkv", "L3_cond_Wkv"),
        "w_o": stacked("L1_cond_Wo", "L2_cond_Wout", "L3_cond_Wout"),
        "q_scale": later("q_scale").reshape(-1), "k_scale": later("k_scale").reshape(-1),
        "w0": later("w0").reshape(-1), "b0": later("b0").reshape(-1), "b1": later("b1").reshape(-1),
        "m_cols": np.concatenate([later("g0"), later("g1")]).T, "w1": later("w1"), "w2": later("w2"),
        "b2_t": later("b2").T,
        "ident": np.eye(P, dtype=np.float32),
        "pos": (SEQ - 1 - np.arange(SEQ)).reshape(ROWS, P).T.astype(np.float32),
        "pair_sel": np.tile(np.repeat(np.eye(EXPERTS, dtype=np.float32), MID, axis=1), (2, 1)),
        "rank8": np.arange(EXPERTS, 0, -1).astype(np.float32),
    }
    nc = bacc.Bacc("TRN2", target_bir_lowering=False, num_devices=1)
    arrays, handles = {}, {}
    for name, array in given.items():
        arrays["in_" + name] = np.ascontiguousarray(array)
        handles[name] = nc.dram_tensor("in_" + name, array.shape, mybir.dt.from_np(array.dtype),
                                       kind="ExternalInput").ap()
    out = nc.dram_tensor("out_x", (BATCH, SEQ, DIM), F32, kind="ExternalOutput").ap()
    build(nc, handles, out)
    return run_bass_kernel_spmd(nc, [arrays], core_ids=[0]).results[0]["out_x"]
```
